# Optimizing a Trainium2 kernel written in Bass

```python
import numpy as np
import jax
import jax.numpy as jnp

def _softmax(x, axis=-1):
    return jax.nn.softmax(x, axis=axis)

def _gelu(x):
    return jax.nn.gelu(x, approximate=True)

def _silu(x):
    return jax.nn.silu(x)

def _sigmoid(x):
    return jax.nn.sigmoid(x)

def _layernorm(x, axis=-1, eps=1e-05):
    m = jnp.mean(x, axis=axis, keepdims=True)
    v = jnp.var(x, axis=axis, keepdims=True)
    return (x - m) / jnp.sqrt(v + eps)

def _scatter_add(tgt, idx, src, axis=0):
    return tgt.at[idx].add(src)

def _segment_sum(src, seg, n):
    return jax.ops.segment_sum(src, seg, n)
kernel_name = 'mk_hybrid_d1_jaxref_r8_ae0124'

def setup_inputs(seed: int=0):
    np.random.seed(seed)
    _w = jnp.asarray

    def _L0_attn_a_setup():
        import jax, jax.numpy as jnp
        import numpy as np
        D_MODEL = 128
        NHEAD = 16
        HEAD_DIM = D_MODEL // NHEAD
        ROTARY_DIM = HEAD_DIM
        D_INNER = 2 * D_MODEL
        HEADDIM = 64
        H_SSM = D_INNER // HEADDIM
        D_STATE = 128
        D_CONV = 4
        CHUNK = 32
        CONV_DIM = D_INNER + 2 * D_STATE
        D_IN_PROJ = 2 * D_INNER + 2 * D_STATE + H_SSM
        EPS = 1e-05

        def rmsnorm(x, w):
            var = jnp.mean(x * x, axis=-1, keepdims=True)
            return x * jax.lax.rsqrt(var + EPS) * w

        def apply_rope(q):
            T = q.shape[1]
            half = ROTARY_DIM // 2
            inv_freq = 1.0 / 10000.0 ** (jnp.arange(0, ROTARY_DIM, 2, dtype=jnp.float32) / ROTARY_DIM)
            freqs = jnp.arange(T, dtype=jnp.float32)[:, None] * inv_freq[None, :]
            cos = jnp.cos(freqs)[None, :, None, :]
            sin = jnp.sin(freqs)[None, :, None, :]
            q1 = q[..., :half]
            q2 = q[..., half:ROTARY_DIM]
            rest = q[..., ROTARY_DIM:]
            return jnp.concatenate([q1 * cos - q2 * sin, q2 * cos + q1 * sin, rest], axis=-1)

        def segsum(x):
            T = x.shape[-1]
            xc = jnp.cumsum(x, axis=-1)
            ss = xc[..., :, None] - xc[..., None, :]
            mask = jnp.tril(jnp.ones((T, T), dtype=bool))
            return jnp.where(mask, ss, -jnp.inf)

        def ssd(x, dt, A, Bm, Cm):
            b, l, h, p = x.shape
            n = Bm.shape[-1]
            c = l // CHUNK
            xdt = (x * dt[..., None]).reshape(b, c, CHUNK, h, p)
            Adt = (dt * A).reshape(b, c, CHUNK, h).transpose(0, 3, 1, 2)
            Br = Bm.reshape(b, c, CHUNK, n)
            Cr = Cm.reshape(b, c, CHUNK, n)
            Acs = jnp.cumsum(Adt, axis=-1)
            Lmat = jnp.exp(segsum(Adt))
            Y_diag = jnp.einsum('bcln,bcsn,bhcls,bcshp->bclhp', Cr, Br, Lmat, xdt)
            decay_states = jnp.exp(Acs[..., -1:] - Acs)
            states = jnp.einsum('bcln,bhcl,bclhp->bchpn', Br, decay_states, xdt)
            A_chunk = jnp.pad(Acs[..., -1], ((0, 0), (0, 0), (1, 0)))
            decay_chunk = jnp.exp(segsum(A_chunk))
            states = jnp.concatenate([jnp.zeros_like(states[:, :1]), states], axis=1)
            new_states = jnp.einsum('bhzc,bchpn->bzhpn', decay_chunk, states)
            states_prev = new_states[:, :-1]
            Y_off = jnp.einsum('bcln,bchpn,bhcl->bclhp', Cr, states_prev, jnp.exp(Acs))
            return (Y_diag + Y_off).reshape(b, l, h, p)
        key = jax.random.key(seed)
        ks = jax.random.split(key, 8)
        B, T = (2, 256)
        return {'x': jax.random.normal(ks[0], (B, T, D_MODEL), dtype=jnp.float32), 'W_in': jax.random.normal(ks[1], (3 * D_MODEL, D_MODEL), dtype=jnp.float32) * 0.02, 'W_zxbcdt': jax.random.normal(ks[2], (D_IN_PROJ, D_MODEL), dtype=jnp.float32) * 0.02, 'conv_w': jax.random.normal(ks[3], (CONV_DIM, D_CONV), dtype=jnp.float32) * 0.2, 'conv_b': jnp.zeros((CONV_DIM,), dtype=jnp.float32), 'dt_bias': jax.random.normal(ks[4], (H_SSM,), dtype=jnp.float32) * 0.5, 'A_log': jax.random.normal(ks[5], (H_SSM,), dtype=jnp.float32) * 0.5, 'D_param': jax.random.normal(ks[6], (H_SSM,), dtype=jnp.float32), 'norm_pre_w': jnp.ones((D_MODEL,), dtype=jnp.float32), 'norm_gated_w': jnp.ones((D_INNER,), dtype=jnp.float32), 'W_out': jax.random.normal(ks[7], (D_MODEL, D_INNER), dtype=jnp.float32) * 0.02}
    _L0_attn_a_in = _L0_attn_a_setup()

    def _L0_attn_b_setup():
        import jax, jax.numpy as jnp
        import numpy as np
        B, T, C = (4, 512, 128)
        NUM_LAYERS = 24
        LAYER_ID = 0
        EPS = 1e-05

        def _ln(x, w, b):
            m = x.mean(-1, keepdims=True)
            v = x.var(-1, keepdims=True)
            return (x - m) / jnp.sqrt(v + EPS) * w + b

        def _time_shift(x):
            return jnp.pad(x, ((0, 0), (1, 0), (0, 0)))[:, :-1]

        def _wkv(w, u, k, v):

            def step(carry, kv_t):
                aa, bb, pp = carry
                kt, vt = kv_t
                ww = u + kt
                p = jnp.maximum(pp, ww)
                e1 = jnp.exp(pp - p)
                e2 = jnp.exp(ww - p)
                y = (e1 * aa + e2 * vt) / (e1 * bb + e2)
                ww2 = pp + w
                p2 = jnp.maximum(ww2, kt)
                e1 = jnp.exp(ww2 - p2)
                e2 = jnp.exp(kt - p2)
                return ((e1 * aa + e2 * vt, e1 * bb + e2, p2), y)
            Bz, Tz, Cz = k.shape
            init = (jnp.zeros((Bz, Cz), k.dtype), jnp.zeros((Bz, Cz), k.dtype), jnp.full((Bz, Cz), -1e+38, k.dtype))
            kT = jnp.swapaxes(k, 0, 1)
            vT = jnp.swapaxes(v, 0, 1)
            _, y = jax.lax.scan(step, init, (kT, vT))
            return jnp.swapaxes(y, 0, 1)
        key = jax.random.key(seed)
        ks = jax.random.split(key, 9)
        s = 0.02
        ratio_0_to_1 = LAYER_ID / (NUM_LAYERS - 1)
        ratio_1_to_almost0 = 1.0 - LAYER_ID / NUM_LAYERS
        h = np.arange(C, dtype=np.float64)
        time_decay = (-5.0 + 8.0 * (h / (C - 1)) ** (0.7 + 1.3 * ratio_0_to_1)).astype(np.float32)
        zigzag = ((np.arange(C) + 1) % 3 - 1) * 0.5
        time_first = (np.ones(C) * np.log(0.3) + zigzag).astype(np.float32)
        xi = np.arange(C, dtype=np.float64) / C
        tmk = (xi ** ratio_1_to_almost0).astype(np.float32)
        tmv = (xi ** ratio_1_to_almost0 + 0.3 * ratio_0_to_1).astype(np.float32)
        tmr = (xi ** (0.5 * ratio_1_to_almost0)).astype(np.float32)
        cmk = (xi ** ratio_1_to_almost0).astype(np.float32)
        H = 4 * C
        return {'x': jax.random.normal(ks[0], (B, T, C), jnp.float32), 'ln0_w': jnp.ones(C), 'ln0_b': jnp.zeros(C), 'ln1_w': jnp.ones(C), 'ln1_b': jnp.zeros(C), 'ln2_w': jnp.ones(C), 'ln2_b': jnp.zeros(C), 'time_decay': jnp.asarray(time_decay), 'time_first': jnp.asarray(time_first), 'tmk': jnp.asarray(tmk), 'tmv': jnp.asarray(tmv), 'tmr': jnp.asarray(tmr), 'Wk': jax.random.normal(ks[1], (C, C), jnp.float32) * s, 'Wv': jax.random.normal(ks[2], (C, C), jnp.float32) * s, 'Wr': jax.random.normal(ks[3], (C, C), jnp.float32) * s, 'Wo': jax.random.normal(ks[4], (C, C), jnp.float32) * s, 'cmk': jnp.asarray(cmk), 'cmr': jnp.asarray(cmk), 'Wfk': jax.random.normal(ks[5], (H, C), jnp.float32) * s, 'Wfr': jax.random.normal(ks[6], (C, C), jnp.float32) * s, 'Wfv': jax.random.normal(ks[7], (C, H), jnp.float32) * s}
    _L0_attn_b_in = _L0_attn_b_setup()

    def _L0_ffn_setup():
        import jax, jax.numpy as jnp
        import numpy as np
        B, S, H = (4, 256, 128)
        D = 256
        E = 8
        K = 2
        key = jax.random.key(seed)
        ks = jax.random.split(key, 8)
        w = lambda k, shape: jax.random.normal(k, shape, jnp.float32) * 0.02
        return {'hidden_states': jax.random.normal(ks[0], (B, S, H), jnp.float32), 'gate_w': w(ks[1], (H, E)), 'w_gate': w(ks[2], (E, H, D)), 'w_up': w(ks[3], (E, H, D)), 'w_down': w(ks[4], (E, D, H)), 'ws_gate': w(ks[5], (H, D)), 'ws_up': w(ks[6], (H, D)), 'ws_down': w(ks[7], (D, H))}
    _L0_ffn_in = _L0_ffn_setup()
    _d = {'L0_attn_a_x': _L0_attn_a_in['x'], 'L0_attn_a_W_in': _L0_attn_a_in['W_in'], 'L0_attn_a_W_zxbcdt': _L0_attn_a_in['W_zxbcdt'], 'L0_attn_a_conv_w': _L0_attn_a_in['conv_w'], 'L0_attn_a_conv_b': _L0_attn_a_in['conv_b'], 'L0_attn_a_dt_bias': _L0_attn_a_in['dt_bias'], 'L0_attn_a_A_log': _L0_attn_a_in['A_log'], 'L0_attn_a_D_param': _L0_attn_a_in['D_param'], 'L0_attn_a_norm_pre_w': _L0_attn_a_in['norm_pre_w'], 'L0_attn_a_norm_gated_w': _L0_attn_a_in['norm_gated_w'], 'L0_attn_a_W_out': _L0_attn_a_in['W_out'], 'L0_attn_b_ln0_w': _L0_attn_b_in['ln0_w'], 'L0_attn_b_ln0_b': _L0_attn_b_in['ln0_b'], 'L0_attn_b_ln1_w': _L0_attn_b_in['ln1_w'], 'L0_attn_b_ln1_b': _L0_attn_b_in['ln1_b'], 'L0_attn_b_ln2_w': _L0_attn_b_in['ln2_w'], 'L0_attn_b_ln2_b': _L0_attn_b_in['ln2_b'], 'L0_attn_b_time_decay': _L0_attn_b_in['time_decay'], 'L0_attn_b_time_first': _L0_attn_b_in['time_first'], 'L0_attn_b_tmk': _L0_attn_b_in['tmk'], 'L0_attn_b_tmv': _L0_attn_b_in['tmv'], 'L0_attn_b_tmr': _L0_attn_b_in['tmr'], 'L0_attn_b_Wk': _L0_attn_b_in['Wk'], 'L0_attn_b_Wv': _L0_attn_b_in['Wv'], 'L0_attn_b_Wr': _L0_attn_b_in['Wr'], 'L0_attn_b_Wo': _L0_attn_b_in['Wo'], 'L0_attn_b_cmk': _L0_attn_b_in['cmk'], 'L0_attn_b_cmr': _L0_attn_b_in['cmr'], 'L0_attn_b_Wfk': _L0_attn_b_in['Wfk'], 'L0_attn_b_Wfr': _L0_attn_b_in['Wfr'], 'L0_attn_b_Wfv': _L0_attn_b_in['Wfv'], 'L0_ffn_gate_w': _L0_ffn_in['gate_w'], 'L0_ffn_w_gate': _L0_ffn_in['w_gate'], 'L0_ffn_w_up': _L0_ffn_in['w_up'], 'L0_ffn_w_down': _L0_ffn_in['w_down'], 'L0_ffn_ws_gate': _L0_ffn_in['ws_gate'], 'L0_ffn_ws_up': _L0_ffn_in['ws_up'], 'L0_ffn_ws_down': _L0_ffn_in['ws_down']}
    _x0 = _d['L0_attn_a_x']
    _d['L0_attn_a_x'] = jax.random.normal(jax.random.fold_in(jax.random.key(seed), 1), (4, 512, 128), dtype=_x0.dtype)
    del _x0
    return _d

def reference(L0_attn_a_x, L0_attn_a_W_in, L0_attn_a_W_zxbcdt, L0_attn_a_conv_w, L0_attn_a_conv_b, L0_attn_a_dt_bias, L0_attn_a_A_log, L0_attn_a_D_param, L0_attn_a_norm_pre_w, L0_attn_a_norm_gated_w, L0_attn_a_W_out, L0_attn_b_ln0_w, L0_attn_b_ln0_b, L0_attn_b_ln1_w, L0_attn_b_ln1_b, L0_attn_b_ln2_w, L0_attn_b_ln2_b, L0_attn_b_time_decay, L0_attn_b_time_first, L0_attn_b_tmk, L0_attn_b_tmv, L0_attn_b_tmr, L0_attn_b_Wk, L0_attn_b_Wv, L0_attn_b_Wr, L0_attn_b_Wo, L0_attn_b_cmk, L0_attn_b_cmr, L0_attn_b_Wfk, L0_attn_b_Wfr, L0_attn_b_Wfv, L0_ffn_gate_w, L0_ffn_w_gate, L0_ffn_w_up, L0_ffn_w_down, L0_ffn_ws_gate, L0_ffn_ws_up, L0_ffn_ws_down):

    def _L0_attn_a_ref(x, W_in, W_zxbcdt, conv_w, conv_b, dt_bias, A_log, D_param, norm_pre_w, norm_gated_w, W_out):
        import jax, jax.numpy as jnp
        import numpy as np
        D_MODEL = 128
        NHEAD = 16
        HEAD_DIM = D_MODEL // NHEAD
        ROTARY_DIM = HEAD_DIM
        D_INNER = 2 * D_MODEL
        HEADDIM = 64
        H_SSM = D_INNER // HEADDIM
        D_STATE = 128
        D_CONV = 4
        CHUNK = 32
        CONV_DIM = D_INNER + 2 * D_STATE
        D_IN_PROJ = 2 * D_INNER + 2 * D_STATE + H_SSM
        EPS = 1e-05

        def rmsnorm(x, w):
            var = jnp.mean(x * x, axis=-1, keepdims=True)
            return x * jax.lax.rsqrt(var + EPS) * w

        def apply_rope(q):
            T = q.shape[1]
            half = ROTARY_DIM // 2
            inv_freq = 1.0 / 10000.0 ** (jnp.arange(0, ROTARY_DIM, 2, dtype=jnp.float32) / ROTARY_DIM)
            freqs = jnp.arange(T, dtype=jnp.float32)[:, None] * inv_freq[None, :]
            cos = jnp.cos(freqs)[None, :, None, :]
            sin = jnp.sin(freqs)[None, :, None, :]
            q1 = q[..., :half]
            q2 = q[..., half:ROTARY_DIM]
            rest = q[..., ROTARY_DIM:]
            return jnp.concatenate([q1 * cos - q2 * sin, q2 * cos + q1 * sin, rest], axis=-1)

        def segsum(x):
            T = x.shape[-1]
            xc = jnp.cumsum(x, axis=-1)
            ss = xc[..., :, None] - xc[..., None, :]
            mask = jnp.tril(jnp.ones((T, T), dtype=bool))
            return jnp.where(mask, ss, -jnp.inf)

        def ssd(x, dt, A, Bm, Cm):
            b, l, h, p = x.shape
            n = Bm.shape[-1]
            c = l // CHUNK
            xdt = (x * dt[..., None]).reshape(b, c, CHUNK, h, p)
            Adt = (dt * A).reshape(b, c, CHUNK, h).transpose(0, 3, 1, 2)
            Br = Bm.reshape(b, c, CHUNK, n)
            Cr = Cm.reshape(b, c, CHUNK, n)
            Acs = jnp.cumsum(Adt, axis=-1)
            Lmat = jnp.exp(segsum(Adt))
            Y_diag = jnp.einsum('bcln,bcsn,bhcls,bcshp->bclhp', Cr, Br, Lmat, xdt)
            decay_states = jnp.exp(Acs[..., -1:] - Acs)
            states = jnp.einsum('bcln,bhcl,bclhp->bchpn', Br, decay_states, xdt)
            A_chunk = jnp.pad(Acs[..., -1], ((0, 0), (0, 0), (1, 0)))
            decay_chunk = jnp.exp(segsum(A_chunk))
            states = jnp.concatenate([jnp.zeros_like(states[:, :1]), states], axis=1)
            new_states = jnp.einsum('bhzc,bchpn->bzhpn', decay_chunk, states)
            states_prev = new_states[:, :-1]
            Y_off = jnp.einsum('bcln,bchpn,bhcl->bclhp', Cr, states_prev, jnp.exp(Acs))
            return (Y_diag + Y_off).reshape(b, l, h, p)
        N, T, _ = x.shape
        qkv = (x @ W_in.T).reshape(N, T, 3, NHEAD, HEAD_DIM)
        q = apply_rope(qkv[:, :, 0]).reshape(N, T, D_MODEL)
        residual = q
        h = rmsnorm(q, norm_pre_w)
        zxbcdt = h @ W_zxbcdt.T
        z = zxbcdt[..., :D_INNER]
        xBC = zxbcdt[..., D_INNER:D_INNER + CONV_DIM]
        dt = jax.nn.softplus(zxbcdt[..., -H_SSM:] + dt_bias)
        xp = jnp.pad(xBC, ((0, 0), (D_CONV - 1, 0), (0, 0)))
        conv_out = conv_b
        for k in range(D_CONV):
            conv_out = conv_out + xp[:, k:k + T, :] * conv_w[:, k]
        xBC = jax.nn.silu(conv_out)
        x_ssm = xBC[..., :D_INNER].reshape(N, T, H_SSM, HEADDIM)
        Bm = xBC[..., D_INNER:D_INNER + D_STATE]
        Cm = xBC[..., D_INNER + D_STATE:]
        A = -jnp.exp(A_log)
        y = ssd(x_ssm, dt, A, Bm, Cm) + D_param[None, None, :, None] * x_ssm
        y = y.reshape(N, T, D_INNER)
        y = rmsnorm(y * jax.nn.silu(z), norm_gated_w)
        out = y @ W_out.T
        return out + residual

    def _L0_attn_b_ref(x, ln0_w, ln0_b, ln1_w, ln1_b, ln2_w, ln2_b, time_decay, time_first, tmk, tmv, tmr, Wk, Wv, Wr, Wo, cmk, cmr, Wfk, Wfr, Wfv):
        import jax, jax.numpy as jnp
        import numpy as np
        B, T, C = (4, 512, 128)
        NUM_LAYERS = 24
        LAYER_ID = 0
        EPS = 1e-05

        def _ln(x, w, b):
            m = x.mean(-1, keepdims=True)
            v = x.var(-1, keepdims=True)
            return (x - m) / jnp.sqrt(v + EPS) * w + b

        def _time_shift(x):
            return jnp.pad(x, ((0, 0), (1, 0), (0, 0)))[:, :-1]

        def _wkv(w, u, k, v):

            def step(carry, kv_t):
                aa, bb, pp = carry
                kt, vt = kv_t
                ww = u + kt
                p = jnp.maximum(pp, ww)
                e1 = jnp.exp(pp - p)
                e2 = jnp.exp(ww - p)
                y = (e1 * aa + e2 * vt) / (e1 * bb + e2)
                ww2 = pp + w
                p2 = jnp.maximum(ww2, kt)
                e1 = jnp.exp(ww2 - p2)
                e2 = jnp.exp(kt - p2)
                return ((e1 * aa + e2 * vt, e1 * bb + e2, p2), y)
            Bz, Tz, Cz = k.shape
            init = (jnp.zeros((Bz, Cz), k.dtype), jnp.zeros((Bz, Cz), k.dtype), jnp.full((Bz, Cz), -1e+38, k.dtype))
            kT = jnp.swapaxes(k, 0, 1)
            vT = jnp.swapaxes(v, 0, 1)
            _, y = jax.lax.scan(step, init, (kT, vT))
            return jnp.swapaxes(y, 0, 1)
        x = _ln(x, ln0_w, ln0_b)
        h = _ln(x, ln1_w, ln1_b)
        xx = _time_shift(h)
        xk = h * tmk + xx * (1 - tmk)
        xv = h * tmv + xx * (1 - tmv)
        xr = h * tmr + xx * (1 - tmr)
        k = jnp.einsum('btc,oc->bto', xk, Wk)
        v = jnp.einsum('btc,oc->bto', xv, Wv)
        sr = jax.nn.sigmoid(jnp.einsum('btc,oc->bto', xr, Wr))
        w = -jnp.exp(time_decay)
        att = _wkv(w, time_first, k, v)
        rwkv = jnp.einsum('btc,oc->bto', sr * att, Wo)
        x = x + rwkv
        h2 = _ln(x, ln2_w, ln2_b)
        xx2 = _time_shift(h2)
        xk2 = h2 * cmk + xx2 * (1 - cmk)
        xr2 = h2 * cmr + xx2 * (1 - cmr)
        kf = jnp.einsum('btc,hc->bth', xk2, Wfk)
        kf = jnp.square(jax.nn.relu(kf))
        kv = jnp.einsum('bth,ch->btc', kf, Wfv)
        rkv = jax.nn.sigmoid(jnp.einsum('btc,oc->bto', xr2, Wfr)) * kv
        return x + rkv

    def _L0_ffn_ref(hidden_states, gate_w, w_gate, w_up, w_down, ws_gate, ws_up, ws_down):
        import jax, jax.numpy as jnp
        import numpy as np
        B, S, H = (4, 256, 128)
        D = 256
        E = 8
        K = 2
        b, s, h = hidden_states.shape
        x = hidden_states.reshape(-1, h)
        scores = jax.nn.softmax(x @ gate_w, axis=-1)
        topk_w, topk_idx = jax.lax.top_k(scores, K)
        topk_w = topk_w / (jnp.sum(topk_w, axis=-1, keepdims=True) + 1e-20)
        onehot = jax.nn.one_hot(topk_idx, E, dtype=x.dtype)
        w_per_expert = jnp.einsum('nke,nk->ne', onehot, topk_w)
        y = jnp.zeros_like(x)
        for e in range(E):
            hid = jax.nn.silu(x @ w_gate[e]) * (x @ w_up[e])
            y = y + w_per_expert[:, e:e + 1] * (hid @ w_down[e])
        shared = jax.nn.silu(x @ ws_gate) * (x @ ws_up) @ ws_down
        return (y + shared).reshape(b, s, h)
    x = L0_attn_a_x
    x = x + _L0_attn_a_ref(_layernorm(x, axis=-1), L0_attn_a_W_in, L0_attn_a_W_zxbcdt, L0_attn_a_conv_w, L0_attn_a_conv_b, L0_attn_a_dt_bias, L0_attn_a_A_log, L0_attn_a_D_param, L0_attn_a_norm_pre_w, L0_attn_a_norm_gated_w, L0_attn_a_W_out)
    x = x + _L0_ffn_ref(_layernorm(x, axis=-1), L0_ffn_gate_w, L0_ffn_w_gate, L0_ffn_w_up, L0_ffn_w_down, L0_ffn_ws_gate, L0_ffn_ws_up, L0_ffn_ws_down)
    x = x + _L0_attn_b_ref(_layernorm(x, axis=-1), L0_attn_b_ln0_w, L0_attn_b_ln0_b, L0_attn_b_ln1_w, L0_attn_b_ln1_b, L0_attn_b_ln2_w, L0_attn_b_ln2_b, L0_attn_b_time_decay, L0_attn_b_time_first, L0_attn_b_tmk, L0_attn_b_tmv, L0_attn_b_tmr, L0_attn_b_Wk, L0_attn_b_Wv, L0_attn_b_Wr, L0_attn_b_Wo, L0_attn_b_cmk, L0_attn_b_cmr, L0_attn_b_Wfk, L0_attn_b_Wfr, L0_attn_b_Wfv)
    x = x + _L0_ffn_ref(_layernorm(x, axis=-1), L0_ffn_gate_w, L0_ffn_w_gate, L0_ffn_w_up, L0_ffn_w_down, L0_ffn_ws_gate, L0_ffn_ws_up, L0_ffn_ws_down)
    return x

_drawn_inputs = setup_inputs


def setup_inputs(seed=0):
    import zlib

    import numpy as np

    out = dict(_drawn_inputs(seed))
    spreads = {'L0_attn_a_conv_b': (0.0, 0.1),
     'L0_attn_a_norm_pre_w': (1.0, 0.2),
     'L0_attn_a_norm_gated_w': (1.0, 0.2),
     'L0_attn_b_ln0_w': (1.0, 0.2),
     'L0_attn_b_ln0_b': (0.0, 0.1),
     'L0_attn_b_ln1_w': (1.0, 0.6),
     'L0_attn_b_ln1_b': (0.0, 0.8),
     'L0_attn_b_ln2_w': (1.0, 0.6),
     'L0_attn_b_ln2_b': (0.0, 0.8)}
    factors = {'L0_attn_a_dt_bias': 8.0,
     'L0_attn_a_A_log': 8.0,
     'L0_attn_b_time_decay': 8.0,
     'L0_attn_b_time_first': 8.0,
     'L0_attn_b_tmk': 8.0,
     'L0_attn_b_tmv': 8.0,
     'L0_attn_b_tmr': 8.0,
     'L0_attn_b_Wk': 8.0,
     'L0_attn_b_Wv': 8.0,
     'L0_attn_b_Wr': 8.0,
     'L0_attn_b_Wo': 8.0,
     'L0_attn_b_cmk': 8.0,
     'L0_attn_b_cmr': 8.0,
     'L0_attn_b_Wfk': 8.0,
     'L0_attn_b_Wfr': 8.0,
     'L0_attn_b_Wfv': 8.0,
     'L0_ffn_gate_w': 7.965,
     'L0_ffn_w_gate': 6.967,
     'L0_ffn_w_up': 6.94,
     'L0_ffn_w_down': 6.944,
     'L0_ffn_ws_gate': 4.924,
     'L0_ffn_ws_up': 4.851,
     'L0_ffn_ws_down': 4.873}
    for name, (base, spread) in spreads.items():
        noise = np.random.default_rng([zlib.crc32(name.encode()), seed]).standard_normal(out[name].shape)
        drawn = base * np.exp(spread * noise) if base else spread * noise
        out[name] = jnp.asarray(drawn.astype(out[name].dtype))
    for name, factor in factors.items():
        out[name] = (out[name] * factor).astype(out[name].dtype)
    return out
```

```python
from contextlib import ExitStack

import numpy as np

import concourse.bass as bass
from concourse import mybir

P = 128
SEQS, SEQ = 4, 512
TPS = SEQ // P
TILES = SEQS * TPS
TOKENS = SEQS * SEQ
INNER = 256
HEADS, HDIM = 4, 64
CONV_BLOCKS = 4
TAPS = 4
ZDT = INNER + HEADS
XTOK = INNER + P
EXPERTS = 8
BRANCHES = EXPERTS + 1
FFN = 256
FBLK = FFN // P
MOE_RING = 3
HIDDEN = 512
EPS = 1e-5

X_SCALE, W_SCALE, H_SCALE = 2.0 ** 11, 2.0 ** 8, 2.0 ** 4
GU_UNSCALE = 1.0 / (X_SCALE * W_SCALE)
DOWN_UNSCALE = 1.0 / (H_SCALE * W_SCALE)

ALU = mybir.AluOpType
ACT = mybir.ActivationFunctionType
F32 = mybir.dt.float32
F16 = mybir.dt.float16
AX_X = mybir.AxisListType.X

COLS = {}
for _name, _n in (("norm_pre_w", 1), ("gated_w", 2), ("conv_b", CONV_BLOCKS), ("conv_w", CONV_BLOCKS * TAPS),
                  ("ln1_w", 1), ("ln1_b", 1), ("ln2_w", 1), ("ln2_b", 1), ("decay", 1), ("first", 1),
                  ("tmk", 1), ("tmv", 1), ("tmr", 1), ("cmk", 1), ("cmr", 1),
                  ("dt_bias", HEADS), ("a_log", HEADS), ("d_skip", HEADS), ("ln0_w", P), ("ln0_b", P)):
    _at = max((b for _, b in COLS.values()), default=0)
    COLS[_name] = (_at, _at + _n)
NCOLS = max(b for _, b in COLS.values())


class Core:

    def __init__(self, nc):
        self.nc = nc
        self.live, self.retired = [], []

    def semaphore(self, name):
        ctx = ExitStack()
        sem = ctx.enter_context(self.nc.semaphore(name))
        self.live.append((sem, ctx))
        return sem

    def clear_retired(self, sp):
        for sem, _ in self.retired:
            sp.sem_clear(sem)

    def end_phase(self):
        for _, ctx in self.retired:
            ctx.close()
        self.retired, self.live = self.live, []


def constants(core, ctx):
    nc = core.nc

    def sb(name, shape, dt=F32):
        return ctx.enter_context(nc.sbuf_tensor(name, shape, dt))

    core.banks = [ctx.enter_context(nc.psum_tensor(f"bank{i}", [P, 512], F32)) for i in range(8)]
    core.x = sb("x", [P, TILES, P])
    core.cols = sb("cols", [P, NCOLS])
    core.ident = sb("ident", [P, P])
    core.causal = sb("causal", [P, P])
    core.after = sb("after", [P, P])
    core.ones = sb("ones", [P, P])
    core.mhalf = sb("mhalf", [P, TILES])
    core.router_w = sb("router_w", [P, EXPERTS])
    core.wsplit = sb("wsplit", [P, BRANCHES, 6, FFN], F16)
    core.moe_w_in = [ctx.enter_context(nc.semaphore(f"moe_w_in{e}")) for e in range(BRANCHES)]
    core.cols_in = ctx.enter_context(nc.semaphore("cols_in"))
    core.consts_ready = ctx.enter_context(nc.semaphore("consts_ready"))


def col(core, name, k=0, n=1):
    a = COLS[name][0] + k
    return core.cols[:, a:a + n]


def phase_mamba_in(core, io, shared):
    nc = core.nc
    with ExitStack() as ctx:
        def sb(name, shape, dt=F32):
            return ctx.enter_context(nc.sbuf_tensor(name, shape, dt))

        def sem(name):
            return core.semaphore("a1_" + name)

        wq = sb("wq", [P, 2 * P])
        wzx = sb("wzx", [P, ZDT + CONV_BLOCKS * P])
        rope = sb("rope", [P, 2, TPS, P])
        norm = sb("norm", [P, TILES, P])
        normT = sb("normT", [P, TOKENS])
        turned = sb("turned", [P, 2, 2, 2 * P])
        stats = sb("stats", [P, TILES, 6])
        mv = sb("mv", [P, TILES, 2])
        veps = sb("veps", [P, TILES])
        rstd = sb("rstd", [P, TILES])
        nbias = sb("nbias", [P, TILES])
        ssq = sb("ssq", [P, TILES])
        rms = sb("rms", [P, TILES])
        sq_junk = sb("sq_junk", [P, P])

        x, q, xbc, sz, dt_raw, xtok = core.x, shared.q, shared.xbc, shared.sz, shared.dt_raw, shared.xtok
        xnT_ps, q_ps, hT_ps, conv_ps, z_ps, tok_ps = (
            core.banks[0], core.banks[1:3], core.banks[3], core.banks[4:6], core.banks[6], core.banks[7])

        x_in = [sem(f"x_in{s}") for s in range(SEQS)]
        wq_in, wzx_in, rope_in = sem("wq_in"), sem("wzx_in"), sem("rope_in")
        veps_ready, xn_ready, xn_turned, xnT_ready = sem("veps"), sem("xn"), sem("xn_turned"), sem("xnT")
        q_made, q_roped, q_ready, ssq_ready = sem("q_made"), sem("q_roped"), sem("q_ready"), sem("ssq")
        h_ready, h_turned, hT_ready = sem("h"), sem("h_turned"), sem("hT")
        conv_in, tap0_done, conv_done, conv_act = sem("conv_in"), sem("tap0"), sem("conv_done"), sem("conv_act")
        z_made, z_done, tok_turned, tok_ready = sem("z_made"), sem("z_done"), sem("tok_turned"), sem("tok")
        dve_step, pool_step, act_step = sem("dve_step"), sem("pool_step"), sem("act_step")

        block = ctx.enter_context(nc.Block())

        @block.sync
        def _(sp):
            core.clear_retired(sp)
            xr = io["x"].rearrange("s (c p) d -> s p c d", p=P)
            for s in range(SEQS):
                sp.dma_start(x[:, TPS * s:TPS * (s + 1), :], xr[s]).then_inc(x_in[s], 16)
                if s == 0:
                    sp.dma_start(wq[:], io["wq"]).then_inc(wq_in, 16)
                    sp.dma_start(rope[:], io["rope"]).then_inc(rope_in, 16)
                    sp.dma_start(core.cols[:], io["cols"]).then_inc(core.cols_in, 16)
            sp.dma_start(wzx[:], io["wzx"]).then_inc(wzx_in, 16)
            sp.dma_start(shared.w_out[:], io["w_out"]).then_inc(shared.w_out_in, 16)
            sp.dma_start(core.router_w[:], io["router_w"]).then_inc(core.cols_in, 16)
            for e in range(MOE_RING):
                sp.dma_start(shared.moe_raw[:, e], io["moe"][e]).then_inc(core.moe_w_in[e], 16)

        @block.gpsimd
        def _(pool):
            steps = [0]

            def link(ins):
                steps[0] += 1
                ins.then_inc(pool_step, 1)
                pool.wait_ge(pool_step, steps[0])

            nc.gpsimd.memset(core.mhalf[:], -0.5).then_inc(core.consts_ready, 1)
            nc.gpsimd.memset(core.ones[:], 1.0).then_inc(core.consts_ready, 1)
            nc.gpsimd.memset(core.ident[:], 0.0).then_inc(core.consts_ready, 1)
            pool.wait_ge(core.consts_ready, 3)
            nc.gpsimd.affine_select(out=core.ident[:], in_=core.ident[:], compare_op=ALU.not_equal, fill=1.0,
                                    base=0, pattern=[[-1, P]], channel_multiplier=1).then_inc(core.consts_ready, 1)
            nc.gpsimd.affine_select(out=core.causal[:], in_=core.ones[:], compare_op=ALU.is_ge, fill=0.0,
                                    base=0, pattern=[[1, P]], channel_multiplier=-1).then_inc(core.consts_ready, 1)
            nc.gpsimd.affine_select(out=core.after[:], in_=core.ones[:], compare_op=ALU.is_gt, fill=0.0,
                                    base=0, pattern=[[-1, P]], channel_multiplier=1).then_inc(core.consts_ready, 1)

            def rms_norm(s):
                a, b = TPS * s, TPS * (s + 1)
                pool.wait_ge(ssq_ready, TPS * (s + 1))
                link(nc.gpsimd.tensor_scalar(ssq[:, a:b], ssq[:, a:b], 1.0 / P, EPS, ALU.mult, ALU.add))
                link(nc.gpsimd.tensor_tensor(rms[:, a:b], ssq[:, a:b], core.mhalf[:, a:b], ALU.pow))
                for i in range(a, b):
                    nc.gpsimd.tensor_scalar(norm[:, i, :], q[:, i, :], rms[:, i:i + 1], 0.0,
                                            ALU.mult, ALU.add).then_inc(h_ready, 1)

            for step in range(SEQS + 2):
                if step < SEQS:
                    s = step
                    a, b = TPS * s, TPS * (s + 1)
                    pool.wait_ge(veps_ready, s + 1)
                    link(nc.gpsimd.tensor_tensor(rstd[:, a:b], veps[:, a:b], core.mhalf[:, a:b], ALU.pow))
                    link(nc.gpsimd.tensor_tensor(nbias[:, a:b], mv[:, a:b, 0], rstd[:, a:b], ALU.mult))
                    link(nc.gpsimd.tensor_scalar(nbias[:, a:b], nbias[:, a:b], -1.0, 0.0, ALU.mult, ALU.add))
                    for i in range(a, b):
                        nc.gpsimd.tensor_scalar(norm[:, i, :], x[:, i, :], rstd[:, i:i + 1], nbias[:, i:i + 1],
                                                ALU.mult, ALU.add).then_inc(xn_ready, 1)
                if step >= 2:
                    rms_norm(step - 2)
                if 1 <= step <= SEQS:
                    s = step - 1
                    for pair in range(2):
                        n = 2 * s + pair
                        pool.wait_ge(q_roped, n + 1)
                        nc.gpsimd.tensor_tensor(
                            q[:, TPS * s + 2 * pair:TPS * s + 2 * pair + 2, :],
                            turned[:, pair, 0, :].rearrange("p (c d) -> p c d", c=2),
                            turned[:, pair, 1, :].rearrange("p (c d) -> p c d", c=2), ALU.add).then_inc(q_ready, 1)

        @block.vector
        def _(dve):
            steps = [0]

            def link(ins):
                steps[0] += 1
                ins.then_inc(dve_step, 1)
                dve.wait_ge(dve_step, steps[0])

            for s in range(SEQS):
                dve.wait_ge(x_in[s], 16)
                for i in range(TPS * s, TPS * (s + 1)):
                    last = nc.vector.bn_stats(stats[:, i, :], x[:, i, :])
                link(last)
                for i in range(TPS * s, TPS * (s + 1)):
                    last = nc.vector.bn_aggr(mv[:, i, :], stats[:, i, :])
                link(last)
                nc.vector.tensor_scalar(veps[:, TPS * s:TPS * (s + 1)], mv[:, TPS * s:TPS * (s + 1), 1], EPS, None,
                                        ALU.add).then_inc(veps_ready, 1)
            dve.wait_ge(rope_in, 16)

            def turn_q(s, pair):
                n = 2 * s + pair
                dve.wait_ge(q_made, n + 1)
                if s > 0:
                    dve.wait_ge(q_ready, n - 1)
                src = q_ps[pair][:, :].rearrange("p (c w d) -> p c w d", c=2, w=2)
                for w in range(2):
                    last = nc.vector.tensor_tensor(
                        turned[:, pair, w, :].rearrange("p (c d) -> p c d", c=2), src[:, :, w, :],
                        rope[:, w, 2 * pair:2 * pair + 2, :], ALU.mult)
                last.then_inc(q_roped, 1)

            def taps(s, b):
                t0, t1 = SEQ * s, SEQ * (s + 1)
                dve.wait_ge(tap0_done, CONV_BLOCKS * s + b + 1)
                for back in range(1, TAPS):
                    ins = nc.vector.scalar_tensor_tensor(
                        xbc[:, b, t0 + back:t1], conv_ps[b % 2][:, 0:SEQ - back],
                        col(core, "conv_w", TAPS * b + TAPS - 1 - back), xbc[:, b, t0 + back:t1],
                        ALU.mult, ALU.add)
                    if back < TAPS - 1:
                        link(ins)
                ins.then_inc(conv_done, 1)

            for step in range(1, SEQS + 3):
                for b in range(CONV_BLOCKS):
                    if step >= 3:
                        taps(step - 3, b)
                    if step <= SEQS and b < 2:
                        turn_q(step - 1, b)

        @block.scalar
        def _(act):
            act.wait_ge(core.cols_in, 32)

            def turn_out(i):
                act.wait_ge(tok_turned, i + 1)
                nc.scalar.copy(xtok[:, i, :], tok_ps[:, 0:XTOK]).then_inc(tok_ready, 1)

            for step in range(1, SEQS + 4):
                if 3 <= step < SEQS + 3:
                    s = step - 3
                    act.wait_ge(h_turned, s + 1)
                    nc.scalar.activation(normT[:, SEQ * s:SEQ * (s + 1)], hT_ps[:, :], ACT.Identity,
                                         scale=col(core, "norm_pre_w")).then_inc(hT_ready, 1)
                if step <= SEQS:
                    s = step - 1
                    act.wait_ge(xn_turned, s + 1)
                    nc.scalar.copy(normT[:, SEQ * s:SEQ * (s + 1)], xnT_ps[:, :]).then_inc(xnT_ready, 1)
                if 2 <= step < SEQS + 2:
                    s = step - 2
                    for i in range(TPS * s, TPS * (s + 1)):
                        act.wait_ge(q_ready, i // 2 + 1)
                        if i:
                            act.wait_ge(ssq_ready, i)
                        nc.scalar.activation(sq_junk[:], q[:, i, :], ACT.Square,
                                             accum_out=ssq[:, i:i + 1]).then_inc(ssq_ready, 1)
                for b in range(CONV_BLOCKS + 1):
                    s = step - 3
                    if 3 <= step < SEQS + 3:
                        t0, t1 = SEQ * s, SEQ * (s + 1)
                        if b < CONV_BLOCKS:
                            n = CONV_BLOCKS * s + b
                            act.wait_ge(conv_in, n + 1)
                            nc.scalar.activation(xbc[:, b, t0:t1], conv_ps[b % 2][:, :], ACT.Identity,
                                                 bias=col(core, "conv_b", b),
                                                 scale=col(core, "conv_w", TAPS * b + TAPS - 1)).then_inc(tap0_done, 1)
                            i = TPS * s + b
                            act.wait_ge(z_made, i + 1)
                            nc.scalar.activation(sz[:, i, :], z_ps[:, 0:INNER], ACT.Silu)
                            nc.scalar.copy(dt_raw[:, i, :], z_ps[:, INNER:ZDT]).then_inc(z_done, 1)
                        if b >= 1:
                            act.wait_ge(conv_done, CONV_BLOCKS * s + b)
                            nc.scalar.activation(xbc[:, b - 1, t0:t1], xbc[:, b - 1, t0:t1],
                                                 ACT.Silu).then_inc(conv_act, 1)
                    if step >= 4 and b < TPS:
                        turn_out(TPS * (step - 4) + b)

        @block.tensor
        def _(pe):
            pe.wait_ge(core.consts_ready, 6)

            def turn_tiles(bank, normed, free, turned, s):
                for c in range(TPS):
                    pe.wait_ge(normed, TPS * s + c + 1)
                    if c == 0 and s:
                        pe.wait_ge(free, s)
                    ins = nc.tensor.transpose(bank[:, P * c:P * (c + 1)], norm[:, TPS * s + c, :], core.ident[:])
                ins.then_inc(turned, 1)

            def project_q(s):
                pe.wait_ge(xnT_ready, s + 1)
                if s == 0:
                    pe.wait_ge(wq_in, 16)
                for c in range(TPS):
                    if c % 2 == 0 and s > 0:
                        pe.wait_ge(q_roped, 2 * s + c // 2 - 1)
                    ins = nc.tensor.matmul(q_ps[c // 2][:, 256 * (c % 2):256 * (c % 2) + 256],
                                           normT[:, SEQ * s + P * c:SEQ * s + P * (c + 1)], wq[:],
                                           start=True, stop=True)
                    if c % 2:
                        ins.then_inc(q_made, 1)

            def project_in(s, b):
                n = CONV_BLOCKS * s + b
                if n >= 2:
                    pe.wait_ge(conv_done, n - 1)
                nc.tensor.matmul(conv_ps[b % 2][:, :], wzx[:, ZDT + P * b:ZDT + P * (b + 1)],
                                 normT[:, SEQ * s:SEQ * (s + 1)], start=True, stop=True).then_inc(conv_in, 1)
                i = TPS * s + b
                if i:
                    pe.wait_ge(z_done, i)
                nc.tensor.matmul(z_ps[:, 0:ZDT], normT[:, P * i:P * (i + 1)], wzx[:, 0:ZDT],
                                 start=True, stop=True).then_inc(z_made, 1)

            def turn_tok(s, c):
                i = TPS * s + c
                if c == 0:
                    pe.wait_ge(conv_act, CONV_BLOCKS * s + 3)
                if i:
                    pe.wait_ge(tok_ready, i)
                for b in range(3):
                    ins = nc.tensor.transpose(tok_ps[:, P * b:P * (b + 1)], xbc[:, b, P * i:P * (i + 1)],
                                              core.ident[:])
                ins.then_inc(tok_turned, 1)

            for step in range(SEQS + 4):
                for b in range(CONV_BLOCKS):
                    if 3 <= step < SEQS + 3:
                        if b == 0:
                            pe.wait_ge(hT_ready, step - 2)
                            if step == 3:
                                pe.wait_ge(wzx_in, 16)
                        project_in(step - 3, b)
                    if step >= 4:
                        turn_tok(step - 4, b)
                    if b == 0 and 1 <= step <= SEQS:
                        project_q(step - 1)
                if step < SEQS:
                    turn_tiles(xnT_ps, xn_ready, xnT_ready, xn_turned, step)
                if 2 <= step < SEQS + 2:
                    turn_tiles(hT_ps, h_ready, hT_ready, h_turned, step - 2)


def phase_ssd(core, io, shared):
    nc = core.nc
    units = [(c, s) for c in range(TPS) for s in range(SEQS)]
    NU = len(units)
    with ExitStack() as ctx:
        def sb(name, shape, dt=F32):
            return ctx.enter_context(nc.sbuf_tensor(name, shape, dt))

        def sem(name):
            return core.semaphore("a2_" + name)

        x, q, xbc, sz, dt_raw, xtok = core.x, shared.q, shared.xbc, shared.sz, shared.dt_raw, shared.xtok
        v = sb("dt_in", [P, TILES, HEADS])
        e = sb("dt_exp", [P, TILES, HEADS])
        dt = sb("dt", [P, TILES, HEADS])
        ea = sb("ea", [P, HEADS])
        adt = sb("adt", [P, TILES, HEADS])
        decays = sb("decays", [P, 3, TILES, HEADS])
        wdec = sb("wdec", [P, TILES, HEADS])
        diag_d = sb("diag_d", [P, HEADS, P])
        seg_l = sb("seg_l", [P, 2, HEADS, P])
        xdt = sb("xdt", [P, 2, INNER])
        xw = sb("xw", [P, 2, INNER])
        expo = sb("expo", [P, 2, HEADS, P])
        gm = sb("gm", [P, 2, P])
        mix = sb("mix", [P, 2, HEADS, P])
        state = sb("state", [P, SEQS, INNER])
        y_off = sb("y_off", [P, 2, INNER])
        y = sb("y", [P, 2, INNER])
        g = sb("g", [P, 2, INNER])
        g_junk = sb("g_junk", [P, INNER])
        ssq = sb("ssq2", [P, TILES])
        ms = sb("ms2", [P, TILES])
        rms = sb("rms2", [P, TILES])
        gT = sb("gT", [P, 2, 2, P])

        g_ps, seg_ps, y_ps, st_ps, out_ps = (core.banks[0:2], core.banks[2:4], core.banks[4:6], core.banks[6],
                                             core.banks[7])

        dt_abs, dt_act, adt_ready, cum_made, decay_ready, w_ready = (
            sem("dt_abs"), sem("dt_act"), sem("adt"), sem("cum"), sem("decay"), sem("w"))
        segl_ready, xdt_ready, xw_ready = sem("segl"), sem("xdt"), sem("xw")
        cb_made, seg_made, expo_ready, gm_ready, mix_ready = sem("cb"), sem("seg"), sem("expo"), sem("gm"), sem("mix")
        y_made, st_made, st_ready, y_ready, g_ready, ssq_ready = (
            sem("y_made"), sem("st_made"), sem("st"), sem("y"), sem("g"), sem("ssq"))
        g_turned, gT_ready, out_made, rms_ready, xq_ready, x_ready = (
            sem("g_turned"), sem("gT"), sem("out"), sem("rms"), sem("xq"), sem("x"))
        dve_step, pool_step, act_step = sem("dve_step"), sem("pool_step"), sem("act_step")

        def heads(ap):
            return ap.rearrange("p (h d) -> p h d", h=HEADS)

        def per_head(ap):
            return ap.unsqueeze(2).broadcast_to([P, HEADS, HDIM])

        moe_hi, moe_lo = sem("moe_hi"), sem("moe_lo")

        def moe_pair(e, half):
            return core.wsplit[:, e].rearrange("p (m f) n -> p m f n", f=2)[:, :, half, :]

        block = ctx.enter_context(nc.Block())

        @block.sync
        def _(sp):
            core.clear_retired(sp)
            for e in range(MOE_RING, BRANCHES):
                sp.wait_ge(moe_lo, e - MOE_RING + 1)
                sp.dma_start(shared.moe_raw[:, e % MOE_RING], io["moe"][e]).then_inc(core.moe_w_in[e], 16)

        @block.vector
        def _(dve):
            steps = [0]

            def link(ins):
                steps[0] += 1
                ins.then_inc(dve_step, 1)
                dve.wait_ge(dve_step, steps[0])

            def split_low(e):
                dve.wait_ge(moe_hi, e + 1)
                raw = shared.moe_raw[:, e % MOE_RING].rearrange("p (m n) -> p m n", m=3)
                nc.vector.scalar_tensor_tensor(moe_pair(e, 1), raw, W_SCALE, moe_pair(e, 0), ALU.mult,
                                               ALU.subtract).then_inc(moe_lo, 1)

            link(nc.vector.tensor_tensor(v[:], dt_raw[:], col(core, "dt_bias", 0, HEADS).unsqueeze(1)
                                         .broadcast_to([P, TILES, HEADS]), ALU.add))
            nc.vector.scalar_tensor_tensor(e[:], v[:], -1.0, v[:], ALU.mult, ALU.min).then_inc(dt_abs, 1)
            for h in range(HEADS):
                nc.vector.tensor_scalar(diag_d[:, h, :], core.ident[:], col(core, "d_skip", h), None, ALU.mult)
            dve.wait_ge(dt_act, 3)
            link(nc.vector.scalar_tensor_tensor(dt[:], v[:], 0.0, e[:], ALU.max, ALU.add))
            nc.vector.scalar_tensor_tensor(adt[:], dt[:], -1.0, ea[:].unsqueeze(1).broadcast_to([P, TILES, HEADS]),
                                           ALU.mult, ALU.mult).then_inc(adt_ready, 1)
            dve.wait_ge(decay_ready, 1)
            nc.vector.tensor_tensor(wdec[:], dt[:], decays[:, 1], ALU.mult).then_inc(w_ready, 1)

            def mixing(n):
                c, s = units[n]
                i = TPS * s + c
                dve.wait_ge(cb_made, n + 1)
                nc.vector.tensor_tensor(gm[:, n % 2, :], g_ps[n % 2][:, 0:P], core.causal[:],
                                        ALU.mult).then_inc(gm_ready, 1)
                dve.wait_ge(gm_ready, n + 1)
                dve.wait_ge(expo_ready, n + 1)
                if n >= 2:
                    dve.wait_ge(y_made, n - 1)
                nc.vector.tensor_tensor(mix[:, n % 2], expo[:, n % 2],
                                        gm[:, n % 2, :].unsqueeze(1).broadcast_to([P, HEADS, P]),
                                        ALU.mult).then_inc(mix_ready, 1)

            def joining(n):
                c, s = units[n]
                i = TPS * s + c
                dve.wait_ge(y_made, n + 1)
                ps = y_ps[n % 2]
                if n >= 2:
                    dve.wait_ge(g_ready, n - 1)
                if c == 0:
                    nc.vector.tensor_copy(y[:, n % 2, :], ps[:, 0:INNER]).then_inc(y_ready, 1)
                else:
                    link(nc.vector.tensor_tensor(heads(y_off[:, n % 2, :]), heads(ps[:, INNER:2 * INNER]),
                                                 per_head(decays[:, 0, i, :]), ALU.mult))
                    nc.vector.tensor_tensor(y[:, n % 2, :], y_off[:, n % 2, :], ps[:, 0:INNER],
                                            ALU.add).then_inc(y_ready, 1)
                if c < TPS - 1:
                    dve.wait_ge(st_made, n + 1)
                    if c == 0:
                        nc.vector.tensor_copy(state[:, s, :], st_ps[:, 0:INNER]).then_inc(st_ready, 1)
                    else:
                        link(nc.vector.tensor_tensor(heads(state[:, s, :]), heads(state[:, s, :]),
                                                     per_head(decays[:, 2, i, :]), ALU.mult))
                        nc.vector.tensor_tensor(state[:, s, :], state[:, s, :], st_ps[:, 0:INNER],
                                                ALU.add).then_inc(st_ready, 1)

            def closing(n):
                c, s = units[n]
                i = TPS * s + c
                dve.wait_ge(out_made, n + 1)
                dve.wait_ge(rms_ready, n + 1)
                if n == 0:
                    dve.wait_ge(xq_ready, 1)
                nc.vector.scalar_tensor_tensor(x[:, i, :], out_ps[:, INNER:INNER + P], rms[:, i:i + 1], q[:, i, :],
                                               ALU.mult, ALU.add).then_inc(x_ready, 1)

            for step in range(NU + 3):
                if step < NU:
                    mixing(step)
                if 1 <= step < NU + 1:
                    joining(step - 1)
                if step >= 3:
                    closing(step - 3)
                if step < BRANCHES:
                    split_low(step)

        @block.scalar
        def _(act):
            act.wait_ge(dt_abs, 1)
            nc.scalar.activation(e[:], e[:], ACT.Exp).then_inc(dt_act, 1)
            nc.scalar.activation(ea[:], col(core, "a_log", 0, HEADS), ACT.Exp).then_inc(dt_act, 1)
            act.wait_ge(dt_act, 2)
            nc.scalar.activation(e[:], e[:], ACT.Ln, bias=1.0).then_inc(dt_act, 1)
            act.wait_ge(adt_ready, 1)

            def segments(n):
                c, s = units[n]
                i = TPS * s + c
                if n >= 2:
                    act.wait_ge(seg_made, n - 1)
                for h in range(HEADS):
                    ins = nc.scalar.mul(seg_l[:, n % 2, h, :], core.after[:], adt[:, i, h:h + 1])
                ins.then_inc(segl_ready, 1)

            segments(0)
            act.wait_ge(cum_made, 1)
            nc.scalar.activation(decays[:].rearrange("p a i h -> p (a i h)"), g_ps[1][:, 0:3 * TILES * HEADS],
                                 ACT.Exp).then_inc(decay_ready, 1)
            for step in range(NU + 3):
                if step + 1 < NU:
                    segments(step + 1)
                if step < BRANCHES:
                    act.wait_ge(core.moe_w_in[step], 16)
                    nc.scalar.mul(moe_pair(step, 0), shared.moe_raw[:, step % MOE_RING]
                                  .rearrange("p (m n) -> p m n", m=3), W_SCALE).then_inc(moe_hi, 1)
                if step < NU:
                    n = step
                    act.wait_ge(seg_made, n + 1)
                    if n >= 2:
                        act.wait_ge(mix_ready, n - 1)
                    nc.scalar.activation(expo[:, n % 2].rearrange("p h l -> p (h l)"), seg_ps[n % 2][:, :],
                                         ACT.Exp).then_inc(expo_ready, 1)
                if 2 <= step < NU + 2:
                    n = step - 2
                    c, s = units[n]
                    i = TPS * s + c
                    act.wait_ge(g_ready, n + 1)
                    if n:
                        act.wait_ge(ssq_ready, n)
                    nc.scalar.activation(g_junk[:], g[:, n % 2, :], ACT.Square,
                                         accum_out=ssq[:, i:i + 1]).then_inc(ssq_ready, 1)
                    act.wait_ge(g_turned, n + 1)
                    if n >= 2:
                        act.wait_ge(out_made, n - 1)
                    for k in range(2):
                        ins = nc.scalar.mul(gT[:, n % 2, k, :], out_ps[:, P * k:P * (k + 1)],
                                            col(core, "gated_w", k))
                    ins.then_inc(gT_ready, 1)

        @block.gpsimd
        def _(pool):
            steps = [0]

            def link(ins):
                steps[0] += 1
                ins.then_inc(pool_step, 1)
                pool.wait_ge(pool_step, steps[0])

            def weighing(n):
                c, s = units[n]
                i = TPS * s + c
                if n >= 2:
                    pool.wait_ge(y_made, n - 1)
                nc.gpsimd.tensor_tensor(heads(xdt[:, n % 2, :]), heads(xtok[:, i, 0:INNER]), per_head(dt[:, i, :]),
                                        ALU.mult).then_inc(xdt_ready, 1)
                if c < TPS - 1:
                    if n == 0:
                        pool.wait_ge(w_ready, 1)
                    if n >= 2:
                        pool.wait_ge(st_made, n - 1)
                    nc.gpsimd.tensor_tensor(heads(xw[:, n % 2, :]), heads(xtok[:, i, 0:INNER]),
                                            per_head(wdec[:, i, :]), ALU.mult).then_inc(xw_ready, 1)

            nc.gpsimd.tensor_tensor(q[:], q[:], x[:], ALU.add).then_inc(xq_ready, 1)
            pool.wait_ge(adt_ready, 1)
            for step in range(NU + 3):
                if step < NU:
                    weighing(step)
                if 2 <= step < NU + 2:
                    n = step - 2
                    c, s = units[n]
                    i = TPS * s + c
                    pool.wait_ge(y_ready, n + 1)
                    if n >= 2:
                        pool.wait_ge(ssq_ready, n - 1)
                        pool.wait_ge(g_turned, n - 1)
                    nc.gpsimd.tensor_tensor(g[:, n % 2, :], y[:, n % 2, :], sz[:, i, :], ALU.mult).then_inc(g_ready, 1)
                if step >= 3:
                    n = step - 3
                    c, s = units[n]
                    i = TPS * s + c
                    pool.wait_ge(ssq_ready, n + 1)
                    link(nc.gpsimd.tensor_scalar(ms[:, i:i + 1], ssq[:, i:i + 1], 1.0 / INNER, EPS, ALU.mult, ALU.add))
                    nc.gpsimd.tensor_tensor(rms[:, i:i + 1], ms[:, i:i + 1], core.mhalf[:, 0:1],
                                            ALU.pow).then_inc(rms_ready, 1)

        @block.tensor
        def _(pe):
            pe.wait_ge(adt_ready, 1)
            flat = adt[:].rearrange("p i h -> p (i h)")
            for k, m in enumerate((core.causal, core.after, core.ones)):
                ins = nc.tensor.matmul(g_ps[1][:, 64 * k:64 * (k + 1)], m[:], flat, start=True, stop=True)
            ins.then_inc(cum_made, 1)

            def chunk(n):
                c, s = units[n]
                i = TPS * s + c
                tok = slice(P * i, P * (i + 1))
                if n >= 2:
                    pe.wait_ge(gm_ready, n - 1)
                if n == 1:
                    pe.wait_ge(decay_ready, 1)
                nc.tensor.matmul(g_ps[n % 2][:, 0:P], xbc[:, 2, tok], xbc[:, 3, tok],
                                 start=True, stop=True).then_inc(cb_made, 1)
                pe.wait_ge(segl_ready, n + 1)
                if n >= 2:
                    pe.wait_ge(expo_ready, n - 1)
                for h in range(HEADS):
                    ins = nc.tensor.matmul(seg_ps[n % 2][:, P * h:P * (h + 1)], seg_l[:, n % 2, h, :],
                                           core.causal[:], start=True, stop=True)
                ins.then_inc(seg_made, 1)

            def output(n):
                c, s = units[n]
                i = TPS * s + c
                ps = y_ps[n % 2]
                if c < TPS - 1:
                    pe.wait_ge(xw_ready, n + 1)
                    if n:
                        pe.wait_ge(st_ready, n)
                    nc.tensor.matmul(st_ps[:, 0:INNER], xtok[:, i, INNER:XTOK], xw[:, n % 2, :],
                                     start=True, stop=True).then_inc(st_made, 1)
                if n >= 2:
                    pe.wait_ge(y_ready, n - 1)
                if c:
                    pe.wait_ge(st_ready, n - SEQS + 1)
                    nc.tensor.matmul(ps[:, INNER:2 * INNER], xbc[:, 3, P * i:P * (i + 1)], state[:, s, :],
                                     start=True, stop=True)
                pe.wait_ge(xdt_ready, n + 1)
                pe.wait_ge(mix_ready, n + 1)
                for h in range(HEADS):
                    dst = ps[:, HDIM * h:HDIM * (h + 1)]
                    nc.tensor.matmul(dst, diag_d[:, h, :], xtok[:, i, HDIM * h:HDIM * (h + 1)], start=True, stop=False)
                    ins = nc.tensor.matmul(dst, mix[:, n % 2, h, :], xdt[:, n % 2, HDIM * h:HDIM * (h + 1)],
                                           start=False, stop=True)
                ins.then_inc(y_made, 1)

            def turn(n):
                pe.wait_ge(g_ready, n + 1)
                if n:
                    pe.wait_ge(x_ready, n)
                for k in range(2):
                    ins = nc.tensor.transpose(out_ps[:, P * k:P * (k + 1)], g[:, n % 2, P * k:P * (k + 1)],
                                              core.ident[:])
                ins.then_inc(g_turned, 1)

            def project(n):
                pe.wait_ge(gT_ready, n + 1)
                if n == 0:
                    pe.wait_ge(shared.w_out_in, 16)
                for k in range(2):
                    ins = nc.tensor.matmul(out_ps[:, INNER:INNER + P], gT[:, n % 2, k, :], shared.w_out[:, k, :],
                                           start=k == 0, stop=k == 1)
                ins.then_inc(out_made, 1)

            for step in range(NU + 3):
                if step < NU:
                    chunk(step)
                if step >= 3:
                    project(step - 3)
                if 1 <= step < NU + 1:
                    output(step - 1)
                if 2 <= step < NU + 2:
                    turn(step - 2)


class LayerNorm:

    def __init__(self, sb, sem):
        self.stats = sb("ln_stats", [P, TILES, 6])
        self.mv = sb("ln_mv", [P, TILES, 2])
        self.veps = sb("ln_veps", [P, TILES])
        self.rstd = sb("ln_rstd", [P, TILES])
        self.nbias = sb("ln_nbias", [P, TILES])
        self.veps_ready = sem("veps")
        self.ready = sem("normed")


def ln_stats(nc, link, ln, x, s):
    a, b = TPS * s, TPS * (s + 1)
    for i in range(a, b):
        last = nc.vector.bn_stats(ln.stats[:, i, :], x[:, i, :])
    link(last)
    for i in range(a, b):
        last = nc.vector.bn_aggr(ln.mv[:, i, :], ln.stats[:, i, :])
    link(last)
    nc.vector.tensor_scalar(ln.veps[:, a:b], ln.mv[:, a:b, 1], EPS, None, ALU.add).then_inc(ln.veps_ready, 1)


def ln_apply(nc, pool, core, link, ln, x, out, s):
    a, b = TPS * s, TPS * (s + 1)
    pool.wait_ge(ln.veps_ready, s + 1)
    link(nc.gpsimd.tensor_tensor(ln.rstd[:, a:b], ln.veps[:, a:b], core.mhalf[:, a:b], ALU.pow))
    link(nc.gpsimd.tensor_tensor(ln.nbias[:, a:b], ln.mv[:, a:b, 0], ln.rstd[:, a:b], ALU.mult))
    link(nc.gpsimd.tensor_scalar(ln.nbias[:, a:b], ln.nbias[:, a:b], -1.0, 0.0, ALU.mult, ALU.add))
    for i in range(a, b):
        nc.gpsimd.tensor_scalar(out[:, i, :], x[:, i, :], ln.rstd[:, i:i + 1], ln.nbias[:, i:i + 1],
                                ALU.mult, ALU.add).then_inc(ln.ready, 1)


def phase_moe(core, io, tag, prefetch=(), landed=None, out=None):
    nc = core.nc
    UNITS = SEQS * FBLK
    with ExitStack() as ctx:
        def sb(name, shape, dt=F32):
            return ctx.enter_context(nc.sbuf_tensor(f"{tag}_{name}", shape, dt))

        def sem(name):
            return core.semaphore(f"{tag}_{name}")

        x, w = core.x, core.wsplit
        ln = LayerNorm(sb, sem)
        norm = sb("norm", [P, TILES, P])
        normT = sb("normT", [P, TOKENS])
        x_hi = sb("x_hi", [P, TOKENS], F16)
        x_lo = sb("x_lo", [P, TOKENS], F16)
        shift = sb("shift", [P, TILES, EXPERTS])
        prob = sb("prob", [P, TILES, EXPERTS])
        prob2 = sb("prob2", [P, TILES, EXPERTS])
        eq = sb("eq", [P, TILES, EXPERTS])
        pick = sb("pick", [P, TILES, EXPERTS])
        first = sb("first", [P, TILES, EXPERTS])
        second = sb("second", [P, TILES, EXPERTS])
        rank = sb("rank", [P, EXPERTS])
        top = sb("top", [P, 6, TILES])
        w_branch = sb("w_branch", [P, BRANCHES, TILES])
        silu = sb("silu", [P, 2, SEQ])
        hid = sb("hid", [P, 2, SEQ])
        hid_hi = sb("hid_hi", [P, 2 * FBLK, SEQ], F16)
        hid_lo = sb("hid_lo", [P, 2 * FBLK, SEQ], F16)

        gate_ps, up_ps, down_ps, turn_ps, logit_ps = (core.banks[0:2], core.banks[2:4], core.banks[4:6],
                                                      core.banks[6], core.banks[7])

        x_turned, hi_ready, lo_ready, logits_made = sem("x_turned"), sem("x_hi"), sem("x_lo"), sem("logits")
        shift_ready, exp_ready, route_ready, rank_ready = sem("shift"), sem("exp"), sem("route"), sem("rank")
        gate_made, up_made, down_made = sem("gate"), sem("up"), sem("down")
        silu_ready, hid_ready, hid_hi_ready = sem("silu"), sem("hid"), sem("hid_hi")
        hid_lo0_ready, hid_lo1_ready, added = sem("hid_lo0"), sem("hid_lo1"), sem("added")
        dve_step, pool_step, stored = sem("dve_step"), sem("pool_step"), sem("stored")

        block = ctx.enter_context(nc.Block())

        @block.gpsimd
        def _(pool):
            steps = [0]

            def link(ins):
                steps[0] += 1
                ins.then_inc(pool_step, 1)
                pool.wait_ge(pool_step, steps[0])

            for s in range(SEQS):
                ln_apply(nc, pool, core, link, ln, x, norm, s)
            for k in range(EXPERTS):
                nc.gpsimd.memset(rank[:, k:k + 1], float(EXPERTS - k)).then_inc(rank_ready, 1)
            nc.gpsimd.memset(w_branch[:, 0, :], DOWN_UNSCALE).then_inc(rank_ready, 1)

            def branch(e):
                for s in range(SEQS):
                    slot = FBLK * (s % 2)
                    pool.wait_ge(hid_hi_ready, e * UNITS + 2 * s + 1)
                    nc.gpsimd.tensor_tensor(hid_lo[:, slot, :], hid[:, 0, :], hid_hi[:, slot, :],
                                            ALU.subtract).then_inc(hid_lo0_ready, 1)
            branch(0)
            with pool.Fori(1, BRANCHES) as e:
                branch(e)

        @block.vector
        def _(dve):
            steps = [0]

            def link(ins):
                steps[0] += 1
                ins.then_inc(dve_step, 1)
                dve.wait_ge(dve_step, steps[0])

            for s in range(SEQS + 1):
                if s < SEQS:
                    ln_stats(nc, link, ln, x, s)
                if s:
                    dve.wait_ge(hi_ready, s)
                    nc.vector.scalar_tensor_tensor(x_lo[:, SEQ * (s - 1):SEQ * s], turn_ps[:, :], X_SCALE,
                                                   x_hi[:, SEQ * (s - 1):SEQ * s], ALU.mult,
                                                   ALU.subtract).then_inc(lo_ready, 1)

            def all_experts(ap):
                return ap.unsqueeze(2).broadcast_to([P, TILES, EXPERTS])

            def choose(scores, chosen, best):
                link(nc.vector.tensor_reduce(best, scores, AX_X, ALU.max))
                link(nc.vector.tensor_tensor(eq[:], scores, all_experts(best), ALU.is_equal))
                link(nc.vector.tensor_tensor(pick[:], eq[:], rank[:].unsqueeze(1)
                                             .broadcast_to([P, TILES, EXPERTS]), ALU.mult))
                link(nc.vector.tensor_reduce(top[:, 5, :], pick[:], AX_X, ALU.max))
                link(nc.vector.tensor_tensor(chosen, pick[:], all_experts(top[:, 5, :]), ALU.is_equal))

            def route_softmax():
                dve.wait_ge(logits_made, 1)
                logits = logit_ps[:, 0:TILES * EXPERTS].rearrange("p (i k) -> p i k", i=TILES)
                link(nc.vector.tensor_reduce(top[:, 0, :], logits, AX_X, ALU.max))
                nc.vector.tensor_tensor(shift[:], logits, all_experts(top[:, 0, :]),
                                        ALU.subtract).then_inc(shift_ready, 1)

            def route_choose():
                dve.wait_ge(exp_ready, 1)
                dve.wait_ge(rank_ready, EXPERTS + 1)
                link(nc.vector.tensor_reduce(top[:, 1, :], shift[:], AX_X, ALU.add))
                link(nc.vector.reciprocal(top[:, 2, :], top[:, 1, :]))
                link(nc.vector.tensor_tensor(prob[:], shift[:], all_experts(top[:, 2, :]), ALU.mult))
                choose(prob[:], first[:], top[:, 3, :])
                link(nc.vector.scalar_tensor_tensor(prob2[:], first[:], -4.0, prob[:], ALU.mult, ALU.add))
                choose(prob2[:], second[:], top[:, 4, :])
                link(nc.vector.scalar_tensor_tensor(top[:, 0, :], top[:, 3, :], 1e-20, top[:, 4, :], ALU.add, ALU.add))
                link(nc.vector.reciprocal(top[:, 1, :], top[:, 0, :]))
                link(nc.vector.tensor_tensor(first[:], first[:], second[:], ALU.add))
                link(nc.vector.scalar_tensor_tensor(first[:], first[:], DOWN_UNSCALE, prob[:], ALU.mult, ALU.mult))
                link(nc.vector.tensor_tensor(w_branch[:, 1:BRANCHES, :].rearrange("p k i -> p i k"), first[:],
                                             all_experts(top[:, 1, :]), ALU.mult))

            def hidden(e, u):
                dve.wait_ge(silu_ready, e * UNITS + u + 1)
                dve.wait_ge(up_made, e * UNITS + u + 1)
                peeled = isinstance(e, int) and e == 0
                if u % 2 == 0 and not (peeled and u == 0):
                    dve.wait_ge(hid_lo0_ready, e * SEQS + u // 2)
                if u % 2 and not (peeled and u == 1):
                    dve.wait_ge(hid_lo1_ready, e * SEQS + u // 2)
                nc.vector.scalar_tensor_tensor(hid[:, u % 2, :], up_ps[u % 2][:, :], GU_UNSCALE * H_SCALE,
                                               silu[:, u % 2, :], ALU.mult, ALU.mult).then_inc(hid_ready, 1)

            def low(s, made):
                slot = FBLK * (s % 2) + 1
                dve.wait_ge(hid_hi_ready, made)
                nc.vector.tensor_tensor(hid_lo[:, slot, :], hid[:, 1, :], hid_hi[:, slot, :],
                                        ALU.subtract).then_inc(hid_lo1_ready, 1)

            def add(e, s, count):
                dve.wait_ge(down_made, count)
                for c in range(TPS):
                    i = TPS * s + c
                    ins = nc.vector.scalar_tensor_tensor(x[:, i, :], down_ps[s % 2][:, P * c:P * (c + 1)],
                                                         w_branch[:, e, i:i + 1], x[:, i, :], ALU.mult, ALU.add)
                ins.then_inc(added, 1)

            def branch(e):
                for s in range(SEQS):
                    hidden(e, 2 * s)
                    hidden(e, 2 * s + 1)
                    low(s, e * UNITS + 2 * s + 2)
                    if s:
                        add(e, s - 1, e * SEQS + s)
                    elif not (isinstance(e, int) and e == 0):
                        add(e - 1, SEQS - 1, e * SEQS)
                    if isinstance(e, int) and e == 0:
                        if s == 0:
                            route_softmax()
                        if s == 1:
                            route_choose()
            branch(0)
            with dve.Fori(1, BRANCHES) as e:
                branch(e)
            add(BRANCHES - 1, SEQS - 1, BRANCHES * SEQS)

        @block.scalar
        def _(act):
            for s in range(SEQS):
                act.wait_ge(x_turned, s + 1)
                nc.scalar.copy(normT[:, SEQ * s:SEQ * (s + 1)], turn_ps[:, :])
                nc.scalar.mul(x_hi[:, SEQ * s:SEQ * (s + 1)], turn_ps[:, :], X_SCALE).then_inc(hi_ready, 1)

            def high(u, made, read):
                slot = FBLK * (u // 2 % 2) + u % 2
                if read is not None:
                    act.wait_ge(down_made, read)
                act.wait_ge(hid_ready, made)
                nc.scalar.copy(hid_hi[:, slot, :], hid[:, u % 2, :]).then_inc(hid_hi_ready, 1)

            def branch(e):
                peeled = isinstance(e, int) and e == 0
                for s in range(SEQS):
                    for u in (2 * s, 2 * s + 1):
                        act.wait_ge(gate_made, e * UNITS + u + 1)
                        if not (peeled and s == 0):
                            act.wait_ge(hid_ready, e * UNITS + u - 1)
                        nc.scalar.activation(silu[:, u % 2, :], gate_ps[u % 2][:, :], ACT.Silu,
                                             scale=GU_UNSCALE).then_inc(silu_ready, 1)
                    for u in (2 * s, 2 * s + 1):
                        high(u, e * UNITS + u + 1, None if peeled and s < 2 else e * SEQS + s - 1)
                    if peeled and s == 0:
                        act.wait_ge(shift_ready, 1)
                        nc.scalar.activation(shift[:], shift[:], ACT.Exp).then_inc(exp_ready, 1)
            branch(0)
            with act.Fori(1, BRANCHES) as e:
                branch(e)

        @block.tensor
        def _(pe):
            for s in range(SEQS):
                for c in range(TPS):
                    pe.wait_ge(ln.ready, TPS * s + c + 1)
                    if c == 0 and s:
                        pe.wait_ge(lo_ready, s)
                    ins = nc.tensor.transpose(turn_ps[:, P * c:P * (c + 1)], norm[:, TPS * s + c, :], core.ident[:])
                ins.then_inc(x_turned, 1)

            def logits():
                pe.wait_ge(hi_ready, SEQS)
                for i in range(TILES):
                    ins = nc.tensor.matmul(logit_ps[:, EXPERTS * i:EXPERTS * (i + 1)], normT[:, P * i:P * (i + 1)],
                                           core.router_w[:], start=True, stop=True)
                ins.then_inc(logits_made, 1)

            def gate_up(e, u):
                s, blk = u // 2, u % 2
                tok = slice(SEQ * s, SEQ * (s + 1))
                if not (isinstance(e, int) and e == 0 and u < 2):
                    pe.wait_ge(hid_ready, e * UNITS + u - 1)
                if isinstance(e, int) and e == 0 and blk == 0:
                    pe.wait_ge(lo_ready, s + 1)
                for part, bank, made in ((0, gate_ps, gate_made), (2, up_ps, up_made)):
                    hi = w[:, e, part, P * blk:P * (blk + 1)]
                    lo = w[:, e, part + 1, P * blk:P * (blk + 1)]
                    dst = bank[u % 2][:, :]
                    nc.tensor.matmul(dst, hi, x_hi[:, tok], start=True, stop=False)
                    nc.tensor.matmul(dst, hi, x_lo[:, tok], start=False, stop=False)
                    nc.tensor.matmul(dst, lo, x_hi[:, tok], start=False, stop=True).then_inc(made, 1)

            def down(e, s, count):
                pe.wait_ge(hid_lo0_ready, count)
                pe.wait_ge(hid_lo1_ready, count)
                if not (isinstance(count, int) and count <= 2):
                    pe.wait_ge(added, count - 2)
                for c in range(TPS):
                    dst = down_ps[s % 2][:, P * c:P * (c + 1)]
                    for blk in range(FBLK):
                        slot = FBLK * (s % 2) + blk
                        h_hi = hid_hi[:, slot, P * c:P * (c + 1)]
                        h_lo = hid_lo[:, slot, P * c:P * (c + 1)]
                        d_hi = w[:, e, 4, P * blk:P * (blk + 1)]
                        d_lo = w[:, e, 5, P * blk:P * (blk + 1)]
                        nc.tensor.matmul(dst, h_hi, d_hi, start=blk == 0, stop=False)
                        nc.tensor.matmul(dst, h_hi, d_lo, start=False, stop=False)
                        ins = nc.tensor.matmul(dst, h_lo, d_hi, start=False, stop=blk == FBLK - 1)
                ins.then_inc(down_made, 1)

            def branch(e):
                for s in range(SEQS):
                    gate_up(e, 2 * s)
                    gate_up(e, 2 * s + 1)
                    if isinstance(e, int) and e == 0 and s == 0:
                        logits()
                    if s:
                        down(e, s - 1, e * SEQS + s)
                    elif not (isinstance(e, int) and e == 0):
                        down(e - 1, SEQS - 1, e * SEQS)
            branch(0)
            with pe.Fori(1, BRANCHES) as e:
                branch(e)
            down(BRANCHES - 1, SEQS - 1, BRANCHES * SEQS)

        @block.sync
        def _(sp):
            core.clear_retired(sp)
            for dst, name in prefetch:
                sp.dma_start(dst[:], io[name]).then_inc(landed, 16)
            if out is not None:
                dst = out.rearrange("s (c p) d -> s p c d", p=P)
                for s in range(SEQS):
                    sp.wait_ge(added, (BRANCHES - 1) * SEQS + s + 1)
                    sp.dma_start(dst[s], x[:, TPS * s:TPS * (s + 1), :]).then_inc(stored, 16)
                sp.wait_ge(stored, 16 * SEQS)


def phase_time_mix(core, io, shared):
    nc = core.nc
    with ExitStack() as ctx:
        def sb(name, shape, dt=F32):
            return ctx.enter_context(nc.sbuf_tensor("tm_" + name, shape, dt))

        def sem(name):
            return core.semaphore("tm_" + name)

        x, x4, w_rkvo = core.x, shared.x4, shared.w_rkvo
        ln_a, ln_b = LayerNorm(sb, sem), LayerNorm(lambda n, s: sb("b_" + n, s), lambda n: sem("b_" + n))
        v_eps = sb("v_eps", [P, TILES])
        hn = sb("hn", [P, TILES, P])
        hT = sb("hT", [P, SEQS, SEQ + 1])
        dif = sb("dif", [P, 2, SEQ])
        mixed = sb("mixed", [P, 2, 3, SEQ])
        w_decay = sb("w_decay", [P, 1])
        pp = sb("pp", [P, SEQ + 1])
        aa = sb("aa", [P, 2, SEQ + 1])
        bb = sb("bb", [P, 2, SEQ + 1])
        lead = sb("lead", [P, 2, SEQ])
        expo = sb("expo", [P, 2, 4, SEQ])
        e_r = sb("e_r", [P, 2, SEQ])
        e2v = sb("e2v", [P, SEQ])
        y2v = sb("y2v", [P, 2, SEQ])
        num = sb("num", [P, 2, SEQ])
        den = sb("den", [P, 2, SEQ])
        den_r = sb("den_r", [P, SEQ])
        recip = sb("recip", [P, SEQ])
        att = sb("att", [P, 2, SEQ])

        turn_ps, kvr_ps, out_ps = core.banks[0], (core.banks[1:4], core.banks[4:7]), core.banks[7]

        decay_act, decay_ready, x0_ready, x0_mul = sem("decay_act"), sem("decay"), sem("x0"), sem("x0_mul")
        h_turned, hT_ready, dif_ready, mixed_ready = sem("h_turned"), sem("hT"), sem("dif"), sem("mixed")
        kvr_made, raw_ready, lead_ready, lead_act = sem("kvr"), sem("raw"), sem("lead"), sem("lead_act")
        expo_ready, aabb_ready, numden_ready, att_ready = sem("expo"), sem("aabb"), sem("numden"), sem("att")
        neg_r_ready, er_ready, y2v_ready, zeroed = sem("neg_r"), sem("er"), sem("y2v"), sem("zeroed")
        out_made, x4_ready, x_ready = sem("out"), sem("x4"), sem("x")
        dve_step, pool_step, act_step = sem("dve_step"), sem("pool_step"), sem("act_step")

        block = ctx.enter_context(nc.Block())

        @block.sync
        def _(sp):
            core.clear_retired(sp)

        @block.gpsimd
        def _(pool):
            steps = [0]

            def link(ins):
                steps[0] += 1
                ins.then_inc(pool_step, 1)
                pool.wait_ge(pool_step, steps[0])

            nc.gpsimd.memset(hT[:, :, 0:1], 0.0).then_inc(zeroed, 1)
            nc.gpsimd.memset(pp[:, 0:1], -1e38).then_inc(zeroed, 1)
            nc.gpsimd.memset(aa[:, :, 0:1], 0.0).then_inc(zeroed, 1)
            nc.gpsimd.memset(bb[:, :, 0:1], 0.0).then_inc(zeroed, 1)

            def rows(name):
                return col(core, name, 0, P).unsqueeze(1).broadcast_to([P, TPS, P])

            for step in range(SEQS + 3):
                if step < SEQS:
                    s = step
                    a, b = TPS * s, TPS * (s + 1)
                    ln_apply(nc, pool, core, link, ln_a, x, x4, s)
                    pool.wait_ge(ln_a.ready, TPS * (s + 1))
                    nc.gpsimd.tensor_tensor(x4[:, a:b, :], x4[:, a:b, :], rows("ln0_w"), ALU.mult).then_inc(x0_mul, 1)
                    pool.wait_ge(x0_mul, s + 1)
                    nc.gpsimd.tensor_tensor(x4[:, a:b, :], x4[:, a:b, :], rows("ln0_b"), ALU.add).then_inc(x0_ready, 1)
                if 1 <= step <= SEQS:
                    ln_apply(nc, pool, core, link, ln_b, x4, hn, step - 1)
                if 2 <= step < SEQS + 2:
                    s = step - 2
                    pool.wait_ge(hT_ready, s + 1)
                    if s == 0:
                        pool.wait_ge(zeroed, 4)
                    if s >= 2:
                        pool.wait_ge(mixed_ready, 3 * (s - 1))
                    nc.gpsimd.tensor_tensor(dif[:, s % 2, :], hT[:, s, 1:SEQ + 1], hT[:, s, 0:SEQ],
                                            ALU.subtract).then_inc(dif_ready, 1)
                if step >= 3:
                    s = step - 3
                    k = s % 2
                    pool.wait_ge(aabb_ready, 2 * (s + 1))
                    pool.wait_ge(expo_ready, 4 * (s + 1))
                    if s >= 2:
                        pool.wait_ge(att_ready, s - 1)
                    link(nc.gpsimd.tensor_tensor(num[:, k, :], expo[:, k, 2, :], aa[:, k, 0:SEQ], ALU.mult))
                    link(nc.gpsimd.tensor_tensor(den[:, k, :], expo[:, k, 2, :], bb[:, k, 0:SEQ], ALU.mult))
                    pool.wait_ge(y2v_ready, s + 1)
                    nc.gpsimd.tensor_tensor(num[:, k, :], num[:, k, :], y2v[:, k, :], ALU.add).then_inc(numden_ready, 1)
                    nc.gpsimd.tensor_tensor(den[:, k, :], den[:, k, :], expo[:, k, 3, :],
                                            ALU.add).then_inc(numden_ready, 1)
            for s in range(SEQS):
                pool.wait_ge(x4_ready, s + 1)
                a, b = TPS * s, TPS * (s + 1)
                nc.gpsimd.tensor_tensor(x[:, a:b, :], x[:, a:b, :], x4[:, a:b, :], ALU.add).then_inc(x_ready, 1)

        @block.vector
        def _(dve):
            steps = [0]

            def link(ins):
                steps[0] += 1
                ins.then_inc(dve_step, 1)
                dve.wait_ge(dve_step, steps[0])

            dve.wait_ge(decay_act, 1)
            nc.vector.tensor_scalar(w_decay[:], w_decay[:], -1.0, None, ALU.mult).then_inc(decay_ready, 1)
            w_rows = w_decay[:].broadcast_to([P, SEQ])

            def double_stats(s):
                a, b = TPS * s, TPS * (s + 1)
                for i in range(a, b):
                    last = nc.vector.bn_stats(ln_a.stats[:, i, :], x[:, i, :])
                link(last)
                for i in range(a, b):
                    last = nc.vector.bn_aggr(ln_a.mv[:, i, :], ln_a.stats[:, i, :])
                link(last)
                link(nc.vector.tensor_scalar(v_eps[:, a:b], ln_a.mv[:, a:b, 1], EPS, EPS, ALU.add, ALU.mult))
                nc.vector.tensor_tensor(ln_a.veps[:, a:b], v_eps[:, a:b], ln_a.mv[:, a:b, 1],
                                        ALU.add).then_inc(ln_a.veps_ready, 1)

            def mixing(s):
                dve.wait_ge(dif_ready, s + 1)
                if s >= 2:
                    dve.wait_ge(kvr_made, 3 * (s - 1))
                for j, name in enumerate(("tmk", "tmv", "tmr")):
                    nc.vector.scalar_tensor_tensor(mixed[:, s % 2, j, :], dif[:, s % 2, :], col(core, name),
                                                   hT[:, s, 0:SEQ], ALU.mult, ALU.add).then_inc(mixed_ready, 1)

            def scans(s):
                k = s % 2
                kk, vv = kvr_ps[k][0][:, :], kvr_ps[k][1][:, :]
                if s == 0:
                    dve.wait_ge(decay_ready, 1)
                    dve.wait_ge(zeroed, 4)
                dve.wait_ge(kvr_made, 3 * s + 1)
                link(nc.vector.tensor_tensor_scan(pp[:, 1:SEQ + 1], w_rows, kk, -1e38, ALU.add, ALU.max))
                if s >= 2:
                    dve.wait_ge(expo_ready, 4 * (s - 1))
                    dve.wait_ge(numden_ready, 2 * (s - 1))
                nc.vector.scalar_tensor_tensor(lead[:, k, :], pp[:, 0:SEQ], col(core, "first"), kk,
                                               ALU.subtract, ALU.subtract).then_inc(lead_ready, 1)
                nc.vector.scalar_tensor_tensor(expo[:, k, 0, :], pp[:, 0:SEQ], w_decay[:], pp[:, 1:SEQ + 1],
                                               ALU.add, ALU.subtract).then_inc(raw_ready, 1)
                nc.vector.tensor_tensor(expo[:, k, 1, :], kk, pp[:, 1:SEQ + 1], ALU.subtract).then_inc(raw_ready, 1)
                dve.wait_ge(expo_ready, 4 * s + 2)
                dve.wait_ge(kvr_made, 3 * s + 2)
                link(nc.vector.tensor_tensor(e2v[:], expo[:, k, 1, :], vv, ALU.mult))
                nc.vector.tensor_tensor_scan(aa[:, k, 1:SEQ + 1], expo[:, k, 0, :], e2v[:], 0.0,
                                             ALU.mult, ALU.add).then_inc(aabb_ready, 1)
                nc.vector.tensor_tensor_scan(bb[:, k, 1:SEQ + 1], expo[:, k, 0, :], expo[:, k, 1, :], 0.0,
                                             ALU.mult, ALU.add).then_inc(aabb_ready, 1)
                dve.wait_ge(kvr_made, 3 * (s + 1))
                nc.vector.tensor_scalar(e_r[:, k, :], kvr_ps[k][2][:, :], -1.0, 80.0, ALU.mult,
                                        ALU.min).then_inc(neg_r_ready, 1)
                dve.wait_ge(expo_ready, 4 * s + 4)
                nc.vector.tensor_tensor(y2v[:, k, :], expo[:, k, 3, :], vv, ALU.mult).then_inc(y2v_ready, 1)

            def divide(s):
                k = s % 2
                dve.wait_ge(numden_ready, 2 * (s + 1))
                dve.wait_ge(er_ready, s + 1)
                link(nc.vector.scalar_tensor_tensor(den_r[:], e_r[:, k, :], 1.0, den[:, k, :], ALU.add, ALU.mult))
                link(nc.vector.reciprocal(recip[:], den_r[:]))
                if s >= 2:
                    dve.wait_ge(out_made, s - 1)
                nc.vector.tensor_tensor(att[:, k, :], num[:, k, :], recip[:], ALU.mult).then_inc(att_ready, 1)

            def join(s):
                a, b = TPS * s, TPS * (s + 1)
                dve.wait_ge(out_made, s + 1)
                nc.vector.tensor_tensor(x4[:, a:b, :], x4[:, a:b, :],
                                        out_ps[:, :].rearrange("p (c d) -> p c d", c=TPS), ALU.add).then_inc(x4_ready, 1)

            for step in range(SEQS + 5):
                if step < SEQS:
                    double_stats(step)
                if 1 <= step <= SEQS:
                    dve.wait_ge(x0_ready, step)
                    ln_stats(nc, link, ln_b, x4, step - 1)
                if 2 <= step < SEQS + 2:
                    mixing(step - 2)
                if 3 <= step < SEQS + 3:
                    scans(step - 3)
                if 4 <= step < SEQS + 4:
                    divide(step - 4)
                if step >= 5:
                    join(step - 5)

        @block.scalar
        def _(act):
            nc.scalar.activation(w_decay[:], col(core, "decay"), ACT.Exp).then_inc(decay_act, 1)
            for step in range(SEQS + 3):
                if 1 <= step < SEQS + 1:
                    s = step - 1
                    act.wait_ge(h_turned, s + 1)
                    nc.scalar.activation(hT[:, s, 1:SEQ + 1], turn_ps[:, :], ACT.Identity,
                                         bias=col(core, "ln1_b"), scale=col(core, "ln1_w")).then_inc(hT_ready, 1)
                if step >= 3:
                    s = step - 3
                    k = s % 2
                    for j in range(2):
                        act.wait_ge(raw_ready, 2 * s + j + 1)
                        nc.scalar.activation(expo[:, k, j, :], expo[:, k, j, :], ACT.Exp).then_inc(expo_ready, 1)
                    act.wait_ge(lead_ready, s + 1)
                    for j, sign in ((2, -1.0), (3, 1.0)):
                        nc.scalar.activation(expo[:, k, j, :], lead[:, k, :], ACT.Relu, scale=sign).then_inc(lead_act, 1)
                        act.wait_ge(lead_act, 2 * s + j - 1)
                        nc.scalar.activation(expo[:, k, j, :], expo[:, k, j, :], ACT.Exp,
                                             scale=-1.0).then_inc(expo_ready, 1)
                    act.wait_ge(neg_r_ready, s + 1)
                    nc.scalar.activation(e_r[:, k, :], e_r[:, k, :], ACT.Exp).then_inc(er_ready, 1)

        @block.tensor
        def _(pe):
            pe.wait_ge(shared.w_b_in, 16 * 4)
            for step in range(SEQS + 4):
                if 1 <= step < SEQS + 1:
                    s = step - 1
                    for c in range(TPS):
                        pe.wait_ge(ln_b.ready, TPS * s + c + 1)
                        if c == 0 and s:
                            pe.wait_ge(hT_ready, s)
                        ins = nc.tensor.transpose(turn_ps[:, P * c:P * (c + 1)], hn[:, TPS * s + c, :], core.ident[:])
                    ins.then_inc(h_turned, 1)
                if 2 <= step < SEQS + 2:
                    s = step - 2
                    for j in range(3):
                        pe.wait_ge(mixed_ready, 3 * s + j + 1)
                        if s >= 2 and j == 0:
                            pe.wait_ge(y2v_ready, s - 1)
                            pe.wait_ge(neg_r_ready, s - 1)
                        nc.tensor.matmul(kvr_ps[s % 2][j][:, :], w_rkvo[:, j, :], mixed[:, s % 2, j, :],
                                         start=True, stop=True).then_inc(kvr_made, 1)
                if step >= 4:
                    s = step - 4
                    pe.wait_ge(att_ready, s + 1)
                    if s:
                        pe.wait_ge(x4_ready, s)
                    for c in range(TPS):
                        ins = nc.tensor.matmul(out_ps[:, P * c:P * (c + 1)], att[:, s % 2, P * c:P * (c + 1)],
                                               w_rkvo[:, 3, :], start=True, stop=True)
                    ins.then_inc(out_made, 1)


def phase_channel_mix(core, io, shared):
    nc = core.nc
    HB = HIDDEN // P
    with ExitStack() as ctx:
        def sb(name, shape, dt=F32):
            return ctx.enter_context(nc.sbuf_tensor("cm_" + name, shape, dt))

        def sem(name):
            return core.semaphore("cm_" + name)

        x, x4 = core.x, shared.x4
        ln = LayerNorm(sb, sem)
        hn = sb("hn", [P, TILES, P])
        hT = sb("hT", [P, SEQS, SEQ + 1])
        dif = sb("dif", [P, 2, SEQ])
        mixed = sb("mixed", [P, 2, 2, SEQ])
        relu = sb("relu", [P, 2, SEQ])
        sq = sb("sq", [P, 2, HB, SEQ])
        sig = sb("sig", [P, 2, SEQ])
        rkv = sb("rkv", [P, 2, SEQ])

        turn_ps, hid_ps, kv_ps, r_ps = core.banks[0], core.banks[1:3], core.banks[3:5], core.banks[5:7]
        h_turned, hT_ready, dif_ready, mixed_ready = sem("h_turned"), sem("hT"), sem("dif"), sem("mixed")
        hid_made, relu_ready, sq_ready, kv_made = sem("hid"), sem("relu"), sem("sq"), sem("kv")
        r_made, sig_ready, rkv_ready, x_ready, zeroed = sem("r"), sem("sig"), sem("rkv"), sem("x"), sem("zeroed")
        dve_step, pool_step = sem("dve_step"), sem("pool_step")

        block = ctx.enter_context(nc.Block())

        @block.sync
        def _(sp):
            core.clear_retired(sp)

        @block.gpsimd
        def _(pool):
            steps = [0]

            def link(ins):
                steps[0] += 1
                ins.then_inc(pool_step, 1)
                pool.wait_ge(pool_step, steps[0])

            nc.gpsimd.memset(hT[:, :, 0:1], 0.0).then_inc(zeroed, 1)
            for step in range(SEQS + 1):
                if step < SEQS:
                    ln_apply(nc, pool, core, link, ln, x4, hn, step)
                if step >= 1:
                    s = step - 1
                    pool.wait_ge(hT_ready, s + 1)
                    if s == 0:
                        pool.wait_ge(zeroed, 1)
                    if s >= 2:
                        pool.wait_ge(mixed_ready, 2 * (s - 1))
                    nc.gpsimd.tensor_tensor(dif[:, s % 2, :], hT[:, s, 1:SEQ + 1], hT[:, s, 0:SEQ],
                                            ALU.subtract).then_inc(dif_ready, 1)

        @block.vector
        def _(dve):
            steps = [0]

            def link(ins):
                steps[0] += 1
                ins.then_inc(dve_step, 1)
                dve.wait_ge(dve_step, steps[0])

            for step in range(SEQS + 3):
                if step < SEQS:
                    ln_stats(nc, link, ln, x4, step)
                if 1 <= step < SEQS + 1:
                    s = step - 1
                    dve.wait_ge(dif_ready, s + 1)
                    if s >= 2:
                        dve.wait_ge(hid_made, HB * (s - 1))
                        dve.wait_ge(r_made, s - 1)
                    for j, name in enumerate(("cmk", "cmr")):
                        nc.vector.scalar_tensor_tensor(mixed[:, s % 2, j, :], dif[:, s % 2, :], col(core, name),
                                                       hT[:, s, 0:SEQ], ALU.mult, ALU.add).then_inc(mixed_ready, 1)
                if 2 <= step < SEQS + 2:
                    s = step - 2
                    for b in range(HB):
                        n = HB * s + b
                        dve.wait_ge(relu_ready, n + 1)
                        if s >= 2 and b == 0:
                            dve.wait_ge(kv_made, s - 1)
                        nc.vector.scalar_tensor_tensor(sq[:, s % 2, b, :], hid_ps[n % 2][:, :], 0.0,
                                                       relu[:, n % 2, :], ALU.max, ALU.mult).then_inc(sq_ready, 1)
                if step >= 3:
                    s = step - 3
                    a, b = TPS * s, TPS * (s + 1)
                    dve.wait_ge(kv_made, s + 1)
                    dve.wait_ge(sig_ready, s + 1)
                    nc.vector.tensor_tensor(rkv[:, s % 2, :], sig[:, s % 2, :], kv_ps[s % 2][:, :],
                                            ALU.mult).then_inc(rkv_ready, 1)
                    dve.wait_ge(rkv_ready, s + 1)
                    nc.vector.tensor_tensor(x[:, a:b, :], x[:, a:b, :],
                                            rkv[:, s % 2, :].rearrange("p (c d) -> p c d", c=TPS),
                                            ALU.add).then_inc(x_ready, 1)

        @block.scalar
        def _(act):
            for step in range(SEQS + 2):
                if step < SEQS:
                    act.wait_ge(h_turned, step + 1)
                    nc.scalar.activation(hT[:, step, 1:SEQ + 1], turn_ps[:, :], ACT.Identity,
                                         bias=col(core, "ln2_b"), scale=col(core, "ln2_w")).then_inc(hT_ready, 1)
                if step >= 2:
                    s = step - 2
                    for b in range(HB):
                        n = HB * s + b
                        act.wait_ge(hid_made, n + 1)
                        if n >= 2:
                            act.wait_ge(sq_ready, n - 1)
                        nc.scalar.activation(relu[:, n % 2, :], hid_ps[n % 2][:, :], ACT.Relu).then_inc(relu_ready, 1)
                    act.wait_ge(r_made, s + 1)
                    if s >= 2:
                        act.wait_ge(rkv_ready, s - 1)
                    nc.scalar.activation(sig[:, s % 2, :], r_ps[s % 2][:, :], ACT.Sigmoid).then_inc(sig_ready, 1)

        @block.tensor
        def _(pe):
            for step in range(SEQS + 3):
                if step < SEQS:
                    s = step
                    for c in range(TPS):
                        pe.wait_ge(ln.ready, TPS * s + c + 1)
                        if c == 0 and s:
                            pe.wait_ge(hT_ready, s)
                        ins = nc.tensor.transpose(turn_ps[:, P * c:P * (c + 1)], hn[:, TPS * s + c, :], core.ident[:])
                    ins.then_inc(h_turned, 1)
                if 2 <= step < SEQS + 2:
                    s = step - 2
                    pe.wait_ge(mixed_ready, 2 * (s + 1))
                    if s >= 2:
                        pe.wait_ge(sig_ready, s - 1)
                    for b in range(HB):
                        n = HB * s + b
                        if n >= 2:
                            pe.wait_ge(sq_ready, n - 1)
                        nc.tensor.matmul(hid_ps[n % 2][:, :], shared.w_fk[:, P * b:P * (b + 1)], mixed[:, s % 2, 0, :],
                                         start=True, stop=True).then_inc(hid_made, 1)
                    for c in range(TPS):
                        ins = nc.tensor.matmul(r_ps[s % 2][:, P * c:P * (c + 1)], mixed[:, s % 2, 1, P * c:P * (c + 1)],
                                               shared.w_fr[:], start=True, stop=True)
                    ins.then_inc(r_made, 1)
                if step >= 3:
                    s = step - 3
                    pe.wait_ge(sq_ready, HB * (s + 1))
                    if s >= 2:
                        pe.wait_ge(rkv_ready, s - 1)
                    for c in range(TPS):
                        for b in range(HB):
                            ins = nc.tensor.matmul(kv_ps[s % 2][:, P * c:P * (c + 1)],
                                                   sq[:, s % 2, b, P * c:P * (c + 1)], shared.w_fv[:, b, :],
                                                   start=b == 0, stop=b == HB - 1)
                    ins.then_inc(kv_made, 1)


class Shared:
    pass


def program(nc, io, stop_after=9):
    core = Core(nc)
    with ExitStack() as top:
        constants(core, top)
        with ExitStack() as mamba:
            sh = Shared()

            def sb(name, shape, dt=F32):
                return mamba.enter_context(nc.sbuf_tensor(name, shape, dt))
            sh.q = sb("q", [P, TILES, P])
            sh.xbc = sb("xbc", [P, CONV_BLOCKS, TOKENS])
            sh.sz = sb("sz", [P, TILES, INNER])
            sh.dt_raw = sb("dt_raw", [P, TILES, HEADS])
            sh.xtok = sb("xtok", [P, TILES, XTOK])
            sh.moe_raw = sb("moe_raw", [P, MOE_RING, 3 * FFN])
            sh.w_out = sb("w_out", [P, 2, P])
            sh.w_out_in = mamba.enter_context(nc.semaphore("w_out_in"))
            phase_mamba_in(core, io, sh)
            core.end_phase()
            phase_ssd(core, io, sh)
            core.end_phase()
        with ExitStack() as rwkv:
            sh = Shared()

            def sb(name, shape, dt=F32):
                return rwkv.enter_context(nc.sbuf_tensor(name, shape, dt))
            sh.w_rkvo = sb("w_rkvo", [P, 4, P])
            sh.w_fk = sb("w_fk", [P, HIDDEN])
            sh.w_fr = sb("w_fr", [P, P])
            sh.w_fv = sb("w_fv", [P, HIDDEN // P, P])
            sh.w_b_in = rwkv.enter_context(nc.semaphore("w_b_in"))
            phase_moe(core, io, "moe1", prefetch=[(sh.w_rkvo, "w_rkvo"), (sh.w_fk, "w_fk"), (sh.w_fr, "w_fr"),
                                                  (sh.w_fv, "w_fv")], landed=sh.w_b_in)
            core.end_phase()
            sh.x4 = sb("x4", [P, TILES, P])
            phase_time_mix(core, io, sh)
            core.end_phase()
            phase_channel_mix(core, io, sh)
            core.end_phase()
        phase_moe(core, io, "moe2", out=io["out"])
        core.end_phase()
        core.end_phase()


def rope_tables():
    head, half = 8, 4
    inv_freq = 1.0 / 10000.0 ** (np.arange(0, head, 2, dtype=np.float32) / np.float32(head))
    angle = np.arange(SEQ, dtype=np.float32)[:, None] * inv_freq[None, :].astype(np.float32)
    cos, sin = np.cos(angle), np.sin(angle)
    cos = np.tile(np.concatenate([cos, cos], 1), (1, P // head))
    sin = np.tile(np.concatenate([-sin, sin], 1), (1, P // head))
    t = np.stack([cos, sin]).astype(np.float32)
    return np.ascontiguousarray(t.reshape(2, TPS, P, P).transpose(2, 0, 1, 3))


def kernel(**inputs):
    import concourse.bacc as bacc
    from concourse.bass_utils import run_bass_kernel_spmd

    a = {k: np.asarray(v) for k, v in inputs.items()}
    A, B, M = "L0_attn_a_", "L0_attn_b_", "L0_ffn_"

    def column(v):
        return v.reshape(-1, P).T

    def rows(v):
        return np.broadcast_to(v[None, :], (P, v.size))

    w_in = a[A + "W_in"]
    partner = np.arange(P) ^ 4
    wz = a[A + "W_zxbcdt"].T
    cw = a[A + "conv_w"].reshape(CONV_BLOCKS, P, TAPS).transpose(1, 0, 2).reshape(P, -1)
    cols = np.concatenate([
        column(a[A + "norm_pre_w"]), column(a[A + "norm_gated_w"]), column(a[A + "conv_b"]), cw,
        *[column(a[B + n]) for n in ("ln1_w", "ln1_b", "ln2_w", "ln2_b", "time_decay", "time_first",
                                     "tmk", "tmv", "tmr", "cmk", "cmr")],
        *[rows(a[A + n]) for n in ("dt_bias", "A_log", "D_param")],
        rows(a[B + "ln0_w"]), rows(a[B + "ln0_b"])], axis=1)
    def branch(gate, up, down):
        return np.concatenate([gate, up, down.reshape(FBLK, P, P).transpose(1, 0, 2).reshape(P, FFN)], 1)

    moe = [branch(a[M + "ws_gate"], a[M + "ws_up"], a[M + "ws_down"])]
    moe += [branch(a[M + "w_gate"][e], a[M + "w_up"][e], a[M + "w_down"][e]) for e in range(EXPERTS)]
    arrays = {
        "x": a[A + "x"],
        "wq": np.concatenate([w_in[:P].T, w_in[partner].T], 1),
        "wzx": np.concatenate([wz[:, :INNER], wz[:, -HEADS:], wz[:, INNER:INNER + CONV_BLOCKS * P]], 1),
        "rope": rope_tables(),
        "cols": cols,
        "w_out": a[A + "W_out"].T.reshape(2, P, P).transpose(1, 0, 2),
        "router_w": a[M + "gate_w"],
        "moe": np.stack(moe),
        "w_rkvo": np.stack([a[B + n].T for n in ("Wk", "Wv", "Wr", "Wo")], 1),
        "w_fk": a[B + "Wfk"].T,
        "w_fr": a[B + "Wfr"].T,
        "w_fv": a[B + "Wfv"].T.reshape(HIDDEN // P, P, P).transpose(1, 0, 2),
    }
    arrays = {k: np.ascontiguousarray(v) for k, v in arrays.items()}
    nc = bacc.Bacc("TRN2", target_bir_lowering=False, num_devices=1)
    io = {k: nc.dram_tensor("in_" + k, v.shape, F32, kind="ExternalInput").ap() for k, v in arrays.items()}
    io["out"] = nc.dram_tensor("out", (SEQS, SEQ, P), F32, kind="ExternalOutput").ap()
    program(nc, io)
    r = run_bass_kernel_spmd(nc, [{"in_" + k: v for k, v in arrays.items()}], core_ids=[0])
    return r.results[0]["out"]
```

```python
from contextlib import ExitStack

import numpy as np

import concourse.bass as bass
from concourse import mybir

P = 128
SEQS, SEQ = 4, 512
TPS = SEQ // P
TILES = SEQS * TPS
TOKENS = SEQS * SEQ
INNER = 256
HEADS, HDIM = 4, 64
CONV_BLOCKS = 4
TAPS = 4
ZDT = INNER + HEADS
XTOK = INNER + P
EXPERTS = 8
BRANCHES = EXPERTS + 1
FFN = 256
FBLK = FFN // P
MOE_RING = 3
HIDDEN = 512
EPS = 1e-5

X_SCALE, W_SCALE, H_SCALE = 2.0 ** 11, 2.0 ** 8, 2.0 ** 4
GU_UNSCALE = 1.0 / (X_SCALE * W_SCALE)
DOWN_UNSCALE = 1.0 / (H_SCALE * W_SCALE)

ALU = mybir.AluOpType
ACT = mybir.ActivationFunctionType
F32 = mybir.dt.float32
F16 = mybir.dt.float16
AX_X = mybir.AxisListType.X

COLS = {}
for _name, _n in (("norm_pre_w", 1), ("gated_w", 2), ("conv_b", CONV_BLOCKS), ("conv_w", CONV_BLOCKS * TAPS),
                  ("ln1_w", 1), ("ln1_b", 1), ("ln2_w", 1), ("ln2_b", 1), ("decay", 1), ("first", 1),
                  ("tmk", 1), ("tmv", 1), ("tmr", 1), ("cmk", 1), ("cmr", 1),
                  ("dt_bias", HEADS), ("a_log", HEADS), ("d_skip", HEADS), ("ln0_w", P), ("ln0_b", P)):
    _at = max((b for _, b in COLS.values()), default=0)
    COLS[_name] = (_at, _at + _n)
NCOLS = max(b for _, b in COLS.values())


class Core:

    def __init__(self, nc):
        self.nc = nc
        self.live, self.retired = [], []

    def semaphore(self, name):
        ctx = ExitStack()
        sem = ctx.enter_context(self.nc.semaphore(name))
        self.live.append((sem, ctx))
        return sem

    def clear_retired(self, sp):
        for sem, _ in self.retired:
            sp.sem_clear(sem)

    def end_phase(self):
        for _, ctx in self.retired:
            ctx.close()
        self.retired, self.live = self.live, []


def constants(core, ctx):
    nc = core.nc

    def sb(name, shape, dt=F32):
        return ctx.enter_context(nc.sbuf_tensor(name, shape, dt))

    core.banks = [ctx.enter_context(nc.psum_tensor(f"bank{i}", [P, 512], F32)) for i in range(8)]
    core.x = sb("x", [P, TILES, P])
    core.cols = sb("cols", [P, NCOLS])
    core.ident = sb("ident", [P, P])
    core.causal = sb("causal", [P, P])
    core.after = sb("after", [P, P])
    core.ones = sb("ones", [P, P])
    core.mhalf = sb("mhalf", [P, TILES])
    core.router_w = sb("router_w", [P, EXPERTS])
    core.wsplit = sb("wsplit", [P, BRANCHES, 6, FFN], F16)
    core.moe_w_in = [ctx.enter_context(nc.semaphore(f"moe_w_in{e}")) for e in range(BRANCHES)]
    core.cols_in = ctx.enter_context(nc.semaphore("cols_in"))
    core.consts_ready = ctx.enter_context(nc.semaphore("consts_ready"))


def col(core, name, k=0, n=1):
    a = COLS[name][0] + k
    return core.cols[:, a:a + n]


def phase_mamba_in(core, io, shared):
    nc = core.nc
    with ExitStack() as ctx:
        def sb(name, shape, dt=F32):
            return ctx.enter_context(nc.sbuf_tensor(name, shape, dt))

        def sem(name):
            return core.semaphore("a1_" + name)

        wq = sb("wq", [P, 2 * P])
        wzx = sb("wzx", [P, ZDT + CONV_BLOCKS * P])
        rope = sb("rope", [P, 2, TPS, P])
        norm = sb("norm", [P, TILES, P])
        normT = sb("normT", [P, TOKENS])
        turned = sb("turned", [P, 2, 2, 2 * P])
        stats = sb("stats", [P, TILES, 6])
        mv = sb("mv", [P, TILES, 2])
        veps = sb("veps", [P, TILES])
        rstd = sb("rstd", [P, TILES])
        nbias = sb("nbias", [P, TILES])
        ssq = sb("ssq", [P, TILES])
        rms = sb("rms", [P, TILES])
        sq_junk = sb("sq_junk", [P, P])

        x, q, xbc, sz, dt_raw, xtok = core.x, shared.q, shared.xbc, shared.sz, shared.dt_raw, shared.xtok
        xnT_ps, q_ps, hT_ps, conv_ps, z_ps, tok_ps = (
            core.banks[0], core.banks[1:3], core.banks[3], core.banks[4:6], core.banks[6], core.banks[7])

        x_in = [sem(f"x_in{s}") for s in range(SEQS)]
        wq_in, wzx_in, rope_in = sem("wq_in"), sem("wzx_in"), sem("rope_in")
        veps_ready, xn_ready, xn_turned, xnT_ready = sem("veps"), sem("xn"), sem("xn_turned"), sem("xnT")
        q_made, q_roped, q_ready, ssq_ready = sem("q_made"), sem("q_roped"), sem("q_ready"), sem("ssq")
        h_ready, h_turned, hT_ready = sem("h"), sem("h_turned"), sem("hT")
        conv_in, tap0_done, conv_done, conv_act = sem("conv_in"), sem("tap0"), sem("conv_done"), sem("conv_act")
        z_made, z_done, tok_turned, tok_ready = sem("z_made"), sem("z_done"), sem("tok_turned"), sem("tok")
        dve_step, pool_step, act_step = sem("dve_step"), sem("pool_step"), sem("act_step")

        block = ctx.enter_context(nc.Block())

        @block.sync
        def _(sp):
            core.clear_retired(sp)
            xr = io["x"].rearrange("s (c p) d -> s p c d", p=P)
            for s in range(SEQS):
                sp.dma_start(x[:, TPS * s:TPS * (s + 1), :], xr[s]).then_inc(x_in[s], 16)
                if s == 0:
                    sp.dma_start(wq[:], io["wq"]).then_inc(wq_in, 16)
                    sp.dma_start(rope[:], io["rope"]).then_inc(rope_in, 16)
                    sp.dma_start(core.cols[:], io["cols"]).then_inc(core.cols_in, 16)
            sp.dma_start(wzx[:], io["wzx"]).then_inc(wzx_in, 16)
            sp.dma_start(shared.w_out[:], io["w_out"]).then_inc(shared.w_out_in, 16)
            sp.dma_start(core.router_w[:], io["router_w"]).then_inc(core.cols_in, 16)
            for e in range(MOE_RING):
                sp.dma_start(shared.moe_raw[:, e], io["moe"][e]).then_inc(core.moe_w_in[e], 16)

        @block.gpsimd
        def _(pool):
            steps = [0]

            def link(ins):
                steps[0] += 1
                ins.then_inc(pool_step, 1)
                pool.wait_ge(pool_step, steps[0])

            nc.gpsimd.memset(core.mhalf[:], -0.5).then_inc(core.consts_ready, 1)
            nc.gpsimd.memset(core.ones[:], 1.0).then_inc(core.consts_ready, 1)
            nc.gpsimd.memset(core.ident[:], 0.0).then_inc(core.consts_ready, 1)
            pool.wait_ge(core.consts_ready, 3)
            nc.gpsimd.affine_select(out=core.ident[:], in_=core.ident[:], compare_op=ALU.not_equal, fill=1.0,
                                    base=0, pattern=[[-1, P]], channel_multiplier=1).then_inc(core.consts_ready, 1)
            nc.gpsimd.affine_select(out=core.causal[:], in_=core.ones[:], compare_op=ALU.is_ge, fill=0.0,
                                    base=0, pattern=[[1, P]], channel_multiplier=-1).then_inc(core.consts_ready, 1)
            nc.gpsimd.affine_select(out=core.after[:], in_=core.ones[:], compare_op=ALU.is_gt, fill=0.0,
                                    base=0, pattern=[[-1, P]], channel_multiplier=1).then_inc(core.consts_ready, 1)

            def rms_norm(s):
                a, b = TPS * s, TPS * (s + 1)
                pool.wait_ge(ssq_ready, TPS * (s + 1))
                link(nc.gpsimd.tensor_scalar(ssq[:, a:b], ssq[:, a:b], 1.0 / P, EPS, ALU.mult, ALU.add))
                link(nc.gpsimd.tensor_tensor(rms[:, a:b], ssq[:, a:b], core.mhalf[:, a:b], ALU.pow))
                for i in range(a, b):
                    nc.gpsimd.tensor_scalar(norm[:, i, :], q[:, i, :], rms[:, i:i + 1], 0.0,
                                            ALU.mult, ALU.add).then_inc(h_ready, 1)

            for step in range(SEQS + 2):
                if step < SEQS:
                    s = step
                    a, b = TPS * s, TPS * (s + 1)
                    pool.wait_ge(veps_ready, s + 1)
                    link(nc.gpsimd.tensor_tensor(rstd[:, a:b], veps[:, a:b], core.mhalf[:, a:b], ALU.pow))
                    link(nc.gpsimd.tensor_tensor(nbias[:, a:b], mv[:, a:b, 0], rstd[:, a:b], ALU.mult))
                    link(nc.gpsimd.tensor_scalar(nbias[:, a:b], nbias[:, a:b], -1.0, 0.0, ALU.mult, ALU.add))
                    for i in range(a, b):
                        nc.gpsimd.tensor_scalar(norm[:, i, :], x[:, i, :], rstd[:, i:i + 1], nbias[:, i:i + 1],
                                                ALU.mult, ALU.add).then_inc(xn_ready, 1)
                if step >= 2:
                    rms_norm(step - 2)
                if 1 <= step <= SEQS:
                    s = step - 1
                    for pair in range(2):
                        n = 2 * s + pair
                        pool.wait_ge(q_roped, n + 1)
                        nc.gpsimd.tensor_tensor(
                            q[:, TPS * s + 2 * pair:TPS * s + 2 * pair + 2, :],
                            turned[:, pair, 0, :].rearrange("p (c d) -> p c d", c=2),
                            turned[:, pair, 1, :].rearrange("p (c d) -> p c d", c=2), ALU.add).then_inc(q_ready, 1)

        @block.vector
        def _(dve):
            steps = [0]

            def link(ins):
                steps[0] += 1
                ins.then_inc(dve_step, 1)
                dve.wait_ge(dve_step, steps[0])

            for s in range(SEQS):
                dve.wait_ge(x_in[s], 16)
                for i in range(TPS * s, TPS * (s + 1)):
                    last = nc.vector.bn_stats(stats[:, i, :], x[:, i, :])
                link(last)
                for i in range(TPS * s, TPS * (s + 1)):
                    last = nc.vector.bn_aggr(mv[:, i, :], stats[:, i, :])
                link(last)
                nc.vector.tensor_scalar(veps[:, TPS * s:TPS * (s + 1)], mv[:, TPS * s:TPS * (s + 1), 1], EPS, None,
                                        ALU.add).then_inc(veps_ready, 1)
            dve.wait_ge(rope_in, 16)

            def turn_q(s, pair):
                n = 2 * s + pair
                dve.wait_ge(q_made, n + 1)
                if s > 0:
                    dve.wait_ge(q_ready, n - 1)
                src = q_ps[pair][:, :].rearrange("p (c w d) -> p c w d", c=2, w=2)
                for w in range(2):
                    last = nc.vector.tensor_tensor(
                        turned[:, pair, w, :].rearrange("p (c d) -> p c d", c=2), src[:, :, w, :],
                        rope[:, w, 2 * pair:2 * pair + 2, :], ALU.mult)
                last.then_inc(q_roped, 1)

            def taps(s, b):
                t0, t1 = SEQ * s, SEQ * (s + 1)
                dve.wait_ge(tap0_done, CONV_BLOCKS * s + b + 1)
                for back in range(1, TAPS):
                    ins = nc.vector.scalar_tensor_tensor(
                        xbc[:, b, t0 + back:t1], conv_ps[b % 2][:, 0:SEQ - back],
                        col(core, "conv_w", TAPS * b + TAPS - 1 - back), xbc[:, b, t0 + back:t1],
                        ALU.mult, ALU.add)
                    if back < TAPS - 1:
                        link(ins)
                ins.then_inc(conv_done, 1)

            for step in range(1, SEQS + 3):
                for b in range(CONV_BLOCKS):
                    if step >= 3:
                        taps(step - 3, b)
                    if step <= SEQS and b < 2:
                        turn_q(step - 1, b)

        @block.scalar
        def _(act):
            act.wait_ge(core.cols_in, 32)

            def turn_out(i):
                act.wait_ge(tok_turned, i + 1)
                nc.scalar.copy(xtok[:, i, :], tok_ps[:, 0:XTOK]).then_inc(tok_ready, 1)

            for step in range(1, SEQS + 4):
                if 3 <= step < SEQS + 3:
                    s = step - 3
                    act.wait_ge(h_turned, s + 1)
                    nc.scalar.activation(normT[:, SEQ * s:SEQ * (s + 1)], hT_ps[:, :], ACT.Identity,
                                         scale=col(core, "norm_pre_w")).then_inc(hT_ready, 1)
                if step <= SEQS:
                    s = step - 1
                    act.wait_ge(xn_turned, s + 1)
                    nc.scalar.copy(normT[:, SEQ * s:SEQ * (s + 1)], xnT_ps[:, :]).then_inc(xnT_ready, 1)
                if 2 <= step < SEQS + 2:
                    s = step - 2
                    for i in range(TPS * s, TPS * (s + 1)):
                        act.wait_ge(q_ready, i // 2 + 1)
                        if i:
                            act.wait_ge(ssq_ready, i)
                        nc.scalar.activation(sq_junk[:], q[:, i, :], ACT.Square,
                                             accum_out=ssq[:, i:i + 1]).then_inc(ssq_ready, 1)
                for b in range(CONV_BLOCKS + 1):
                    s = step - 3
                    if 3 <= step < SEQS + 3:
                        t0, t1 = SEQ * s, SEQ * (s + 1)
                        if b < CONV_BLOCKS:
                            n = CONV_BLOCKS * s + b
                            act.wait_ge(conv_in, n + 1)
                            nc.scalar.activation(xbc[:, b, t0:t1], conv_ps[b % 2][:, :], ACT.Identity,
                                                 bias=col(core, "conv_b", b),
                                                 scale=col(core, "conv_w", TAPS * b + TAPS - 1)).then_inc(tap0_done, 1)
                            i = TPS * s + b
                            act.wait_ge(z_made, i + 1)
                            nc.scalar.activation(sz[:, i, :], z_ps[:, 0:INNER], ACT.Silu)
                            nc.scalar.copy(dt_raw[:, i, :], z_ps[:, INNER:ZDT]).then_inc(z_done, 1)
                        if b >= 1:
                            act.wait_ge(conv_done, CONV_BLOCKS * s + b)
                            nc.scalar.activation(xbc[:, b - 1, t0:t1], xbc[:, b - 1, t0:t1],
                                                 ACT.Silu).then_inc(conv_act, 1)
                    if step >= 4 and b < TPS:
                        turn_out(TPS * (step - 4) + b)

        @block.tensor
        def _(pe):
            pe.wait_ge(core.consts_ready, 6)

            def turn_tiles(bank, normed, free, turned, s):
                for c in range(TPS):
                    pe.wait_ge(normed, TPS * s + c + 1)
                    if c == 0 and s:
                        pe.wait_ge(free, s)
                    ins = nc.tensor.transpose(bank[:, P * c:P * (c + 1)], norm[:, TPS * s + c, :], core.ident[:])
                ins.then_inc(turned, 1)

            def project_q(s):
                pe.wait_ge(xnT_ready, s + 1)
                if s == 0:
                    pe.wait_ge(wq_in, 16)
                for c in range(TPS):
                    if c % 2 == 0 and s > 0:
                        pe.wait_ge(q_roped, 2 * s + c // 2 - 1)
                    ins = nc.tensor.matmul(q_ps[c // 2][:, 256 * (c % 2):256 * (c % 2) + 256],
                                           normT[:, SEQ * s + P * c:SEQ * s + P * (c + 1)], wq[:],
                                           start=True, stop=True)
                    if c % 2:
                        ins.then_inc(q_made, 1)

            def project_in(s, b):
                n = CONV_BLOCKS * s + b
                if n >= 2:
                    pe.wait_ge(conv_done, n - 1)
                nc.tensor.matmul(conv_ps[b % 2][:, :], wzx[:, ZDT + P * b:ZDT + P * (b + 1)],
                                 normT[:, SEQ * s:SEQ * (s + 1)], start=True, stop=True).then_inc(conv_in, 1)
                i = TPS * s + b
                if i:
                    pe.wait_ge(z_done, i)
                nc.tensor.matmul(z_ps[:, 0:ZDT], normT[:, P * i:P * (i + 1)], wzx[:, 0:ZDT],
                                 start=True, stop=True).then_inc(z_made, 1)

            def turn_tok(s, c):
                i = TPS * s + c
                if c == 0:
                    pe.wait_ge(conv_act, CONV_BLOCKS * s + 3)
                if i:
                    pe.wait_ge(tok_ready, i)
                for b in range(3):
                    ins = nc.tensor.transpose(tok_ps[:, P * b:P * (b + 1)], xbc[:, b, P * i:P * (i + 1)],
                                              core.ident[:])
                ins.then_inc(tok_turned, 1)

            for step in range(SEQS + 4):
                for b in range(CONV_BLOCKS):
                    if 3 <= step < SEQS + 3:
                        if b == 0:
                            pe.wait_ge(hT_ready, step - 2)
                            if step == 3:
                                pe.wait_ge(wzx_in, 16)
                        project_in(step - 3, b)
                    if step >= 4:
                        turn_tok(step - 4, b)
                    if b == 0 and 1 <= step <= SEQS:
                        project_q(step - 1)
                if step < SEQS:
                    turn_tiles(xnT_ps, xn_ready, xnT_ready, xn_turned, step)
                if 2 <= step < SEQS + 2:
                    turn_tiles(hT_ps, h_ready, hT_ready, h_turned, step - 2)


def phase_ssd(core, io, shared):
    nc = core.nc
    units = [(c, s) for c in range(TPS) for s in range(SEQS)]
    NU = len(units)
    WRING = 4
    with ExitStack() as ctx:
        def sb(name, shape, dt=F32):
            return ctx.enter_context(nc.sbuf_tensor(name, shape, dt))

        def sem(name):
            return core.semaphore("a2_" + name)

        x, q, xbc, sz, dt_raw, xtok = core.x, shared.q, shared.xbc, shared.sz, shared.dt_raw, shared.xtok
        v = sb("dt_in", [P, TILES, HEADS])
        e = sb("dt_exp", [P, TILES, HEADS])
        dt = sb("dt", [P, TILES, HEADS])
        ea = sb("ea", [P, HEADS])
        adt = sb("adt", [P, TILES, HEADS])
        decays = sb("decays", [P, 3, TILES, HEADS])
        wdec = sb("wdec", [P, TILES, HEADS])
        dx = sb("dx", [P, WRING, INNER])
        seg_l = sb("seg_l", [P, 2, HEADS, P])
        xdt = sb("xdt", [P, WRING, INNER])
        xw = sb("xw", [P, WRING, INNER])
        expo = sb("expo", [P, 2, HEADS, P])
        gm = sb("gm", [P, 2, P])
        mix = sb("mix", [P, 2, HEADS, P])
        state = sb("state", [P, SEQS, INNER])
        y_off = sb("y_off", [P, 2, INNER])
        y = sb("y", [P, 2, INNER])
        g = sb("g", [P, 2, INNER])
        g_junk = sb("g_junk", [P, INNER])
        ssq = sb("ssq2", [P, TILES])
        ms = sb("ms2", [P, TILES])
        rms = sb("rms2", [P, TILES])
        gT = sb("gT", [P, 2, 2, P])

        g_ps, seg_ps, y_ps, st_ps, out_ps = (core.banks[0:2], core.banks[2:4], core.banks[4:6], core.banks[6],
                                             core.banks[7])

        dt_abs, dt_act, adt_ready, cum_made, decay_ready, w_ready = (
            sem("dt_abs"), sem("dt_act"), sem("adt"), sem("cum"), sem("decay"), sem("w"))
        segl_ready, xdt_ready, xw_ready = sem("segl"), sem("xdt"), sem("xw")
        cb_made, seg_made, expo_ready, gm_ready, mix_ready = sem("cb"), sem("seg"), sem("expo"), sem("gm"), sem("mix")
        y_made, st_made, st_ready, y_ready, g_ready, ssq_ready = (
            sem("y_made"), sem("st_made"), sem("st"), sem("y"), sem("g"), sem("ssq"))
        g_turned, gT_ready, out_made, rms_ready, xq_ready, x_ready = (
            sem("g_turned"), sem("gT"), sem("out"), sem("rms"), sem("xq"), sem("x"))
        dve_step, pool_step, act_step = sem("dve_step"), sem("pool_step"), sem("act_step")
        stats_ready, veps_ready = sem("stats"), sem("veps")

        def heads(ap):
            return ap.rearrange("p (h d) -> p h d", h=HEADS)

        def per_head(ap):
            return ap.unsqueeze(2).broadcast_to([P, HEADS, HDIM])

        moe_hi, moe_lo = sem("moe_hi"), sem("moe_lo")

        def moe_pair(e, half):
            return core.wsplit[:, e].rearrange("p (m f) n -> p m f n", f=2)[:, :, half, :]

        block = ctx.enter_context(nc.Block())

        @block.sync
        def _(sp):
            core.clear_retired(sp)
            for e in range(MOE_RING, BRANCHES):
                sp.wait_ge(moe_lo, e - MOE_RING + 1)
                sp.dma_start(shared.moe_raw[:, e % MOE_RING], io["moe"][e]).then_inc(core.moe_w_in[e], 16)

        @block.vector
        def _(dve):
            steps = [0]

            def link(ins):
                steps[0] += 1
                ins.then_inc(dve_step, 1)
                dve.wait_ge(dve_step, steps[0])

            def split_low(e):
                dve.wait_ge(moe_hi, e + 1)
                raw = shared.moe_raw[:, e % MOE_RING].rearrange("p (m n) -> p m n", m=3)
                nc.vector.scalar_tensor_tensor(moe_pair(e, 1), raw, W_SCALE, moe_pair(e, 0), ALU.mult,
                                               ALU.subtract).then_inc(moe_lo, 1)

            link(nc.vector.tensor_tensor(v[:], dt_raw[:], col(core, "dt_bias", 0, HEADS).unsqueeze(1)
                                         .broadcast_to([P, TILES, HEADS]), ALU.add))
            nc.vector.scalar_tensor_tensor(e[:], v[:], -1.0, v[:], ALU.mult, ALU.min).then_inc(dt_abs, 1)
            dve.wait_ge(dt_act, 3)
            link(nc.vector.scalar_tensor_tensor(dt[:], v[:], 0.0, e[:], ALU.max, ALU.add))
            nc.vector.scalar_tensor_tensor(adt[:], dt[:], -1.0, ea[:].unsqueeze(1).broadcast_to([P, TILES, HEADS]),
                                           ALU.mult, ALU.mult).then_inc(adt_ready, 1)
            dve.wait_ge(decay_ready, 1)
            nc.vector.tensor_tensor(wdec[:], dt[:], decays[:, 1], ALU.mult).then_inc(w_ready, 1)

            def masking(n):
                dve.wait_ge(cb_made, n + 1)
                nc.vector.tensor_tensor(gm[:, n % 2, :], g_ps[n % 2][:, 0:P], core.causal[:],
                                        ALU.mult).then_inc(gm_ready, 1)

            def mixing(n):
                dve.wait_ge(gm_ready, n + 1)
                dve.wait_ge(expo_ready, n + 1)
                if n >= 2:
                    dve.wait_ge(y_made, n - 1)
                nc.vector.tensor_tensor(mix[:, n % 2], expo[:, n % 2],
                                        gm[:, n % 2, :].unsqueeze(1).broadcast_to([P, HEADS, P]),
                                        ALU.mult).then_inc(mix_ready, 1)

            def joining(n):
                c, s = units[n]
                i = TPS * s + c
                dve.wait_ge(y_made, n + 1)
                ps = y_ps[n % 2]
                if c < TPS - 1:
                    dve.wait_ge(st_made, n + 1)
                    if c == 0:
                        nc.vector.tensor_copy(state[:, s, :], st_ps[:, 0:INNER]).then_inc(st_ready, 1)
                    else:
                        link(nc.vector.tensor_tensor(heads(state[:, s, :]), heads(state[:, s, :]),
                                                     per_head(decays[:, 2, i, :]), ALU.mult))
                        nc.vector.tensor_tensor(state[:, s, :], state[:, s, :], st_ps[:, 0:INNER],
                                                ALU.add).then_inc(st_ready, 1)
                if n >= 2:
                    dve.wait_ge(g_ready, n - 1)
                if c == 0:
                    nc.vector.tensor_copy(y[:, n % 2, :], ps[:, 0:INNER]).then_inc(y_ready, 1)
                else:
                    link(nc.vector.tensor_tensor(heads(y_off[:, n % 2, :]), heads(ps[:, INNER:2 * INNER]),
                                                 per_head(decays[:, 0, i, :]), ALU.mult))
                    nc.vector.tensor_tensor(y[:, n % 2, :], y_off[:, n % 2, :], ps[:, 0:INNER],
                                            ALU.add).then_inc(y_ready, 1)

            def closing(n):
                c, s = units[n]
                i = TPS * s + c
                dve.wait_ge(out_made, n + 1)
                dve.wait_ge(rms_ready, n + 1)
                dve.wait_ge(xq_ready, s + 1)
                nc.vector.scalar_tensor_tensor(x[:, i, :], out_ps[:, INNER:INNER + P], rms[:, i:i + 1], q[:, i, :],
                                               ALU.mult, ALU.add).then_inc(x_ready, 1)

            def tile_stats(n):
                c, s = units[n]
                i = TPS * s + c
                dve.wait_ge(x_ready, n + 1)
                nc.vector.bn_stats(shared.ln.stats[:, i, :], x[:, i, :]).then_inc(stats_ready, 1)

            def tile_mean(n):
                c, s = units[n]
                i = TPS * s + c
                dve.wait_ge(stats_ready, n + 1)
                ins = nc.vector.bn_aggr(shared.ln.mv[:, i, :], shared.ln.stats[:, i, :])
                if s == SEQS - 1:
                    link(ins)
                    nc.vector.tensor_scalar(shared.ln.veps[:, c::TPS], shared.ln.mv[:, c::TPS, 1], EPS, None,
                                            ALU.add).then_inc(veps_ready, 1)

            for step in range(NU + 5):
                if 1 <= step < NU + 1:
                    mixing(step - 1)
                if step >= 5 and step < NU + 5:
                    closing(step - 5)
                if 2 <= step < NU + 2:
                    joining(step - 2)
                if step < NU:
                    masking(step)
                if 2 <= step < BRANCHES + 2:
                    split_low(step - 2)
                if step >= 5:
                    tile_stats(step - 5)
                if step >= 6:
                    tile_mean(step - 6)
            tile_mean(NU - 1)

        @block.scalar
        def _(act):
            act.wait_ge(dt_abs, 1)
            nc.scalar.activation(e[:], e[:], ACT.Exp).then_inc(dt_act, 1)
            nc.scalar.activation(ea[:], col(core, "a_log", 0, HEADS), ACT.Exp).then_inc(dt_act, 1)
            act.wait_ge(dt_act, 2)
            nc.scalar.activation(e[:], e[:], ACT.Ln, bias=1.0).then_inc(dt_act, 1)
            act.wait_ge(adt_ready, 1)

            def segments(n):
                c, s = units[n]
                i = TPS * s + c
                if n >= 2:
                    act.wait_ge(seg_made, n - 1)
                for h in range(HEADS):
                    ins = nc.scalar.mul(seg_l[:, n % 2, h, :], core.after[:], adt[:, i, h:h + 1])
                ins.then_inc(segl_ready, 1)

            segments(0)
            act.wait_ge(cum_made, 1)
            nc.scalar.activation(decays[:].rearrange("p a i h -> p (a i h)"), g_ps[1][:, 0:3 * TILES * HEADS],
                                 ACT.Exp).then_inc(decay_ready, 1)
            for step in range(NU + 5):
                if step + 1 < NU:
                    segments(step + 1)
                if 4 <= step < NU + 4:
                    n = step - 4
                    c, s = units[n]
                    i = TPS * s + c
                    act.wait_ge(g_ready, n + 1)
                    if n:
                        act.wait_ge(ssq_ready, n)
                    nc.scalar.activation(g_junk[:], g[:, n % 2, :], ACT.Square,
                                         accum_out=ssq[:, i:i + 1]).then_inc(ssq_ready, 1)
                if step < NU:
                    n = step
                    act.wait_ge(seg_made, n + 1)
                    if n >= 2:
                        act.wait_ge(mix_ready, n - 1)
                    nc.scalar.activation(expo[:, n % 2].rearrange("p h l -> p (h l)"), seg_ps[n % 2][:, :],
                                         ACT.Exp).then_inc(expo_ready, 1)
                if 4 <= step < NU + 4:
                    n = step - 4
                    act.wait_ge(g_turned, n + 1)
                    if n >= 2:
                        act.wait_ge(out_made, n - 1)
                    for k in range(2):
                        ins = nc.scalar.mul(gT[:, n % 2, k, :], out_ps[:, P * k:P * (k + 1)],
                                            col(core, "gated_w", k))
                    ins.then_inc(gT_ready, 1)
                if 2 <= step < BRANCHES + 2:
                    act.wait_ge(core.moe_w_in[step - 2], 16)
                    nc.scalar.mul(moe_pair(step - 2, 0), shared.moe_raw[:, (step - 2) % MOE_RING]
                                  .rearrange("p (m n) -> p m n", m=3), W_SCALE).then_inc(moe_hi, 1)

        @block.gpsimd
        def _(pool):
            steps = [0]

            def link(ins):
                steps[0] += 1
                ins.then_inc(pool_step, 1)
                pool.wait_ge(pool_step, steps[0])

            def weighing(n):
                c, s = units[n]
                i = TPS * s + c
                if n >= WRING:
                    pool.wait_ge(y_made, n - WRING + 1)
                nc.gpsimd.tensor_tensor(heads(dx[:, n % WRING, :]), heads(xtok[:, i, 0:INNER]),
                                        per_head(col(core, "d_skip", 0, HEADS)), ALU.mult)
                nc.gpsimd.tensor_tensor(heads(xdt[:, n % WRING, :]), heads(xtok[:, i, 0:INNER]), per_head(dt[:, i, :]),
                                        ALU.mult).then_inc(xdt_ready, 1)
                if c < TPS - 1:
                    if n == 0:
                        pool.wait_ge(w_ready, 1)
                    if n >= WRING:
                        pool.wait_ge(st_made, n - WRING + 1)
                    nc.gpsimd.tensor_tensor(heads(xw[:, n % WRING, :]), heads(xtok[:, i, 0:INNER]),
                                            per_head(wdec[:, i, :]), ALU.mult).then_inc(xw_ready, 1)

            pool.wait_ge(adt_ready, 1)
            weighing(0)
            weighing(1)
            for step in range(NU + 5):
                if step < SEQS:
                    seq = slice(TPS * step, TPS * (step + 1))
                    nc.gpsimd.tensor_tensor(q[:, seq], q[:, seq], x[:, seq], ALU.add).then_inc(xq_ready, 1)
                if 3 <= step < NU + 3:
                    n = step - 3
                    c, s = units[n]
                    i = TPS * s + c
                    pool.wait_ge(y_ready, n + 1)
                    if n >= 2:
                        pool.wait_ge(ssq_ready, n - 1)
                        pool.wait_ge(g_turned, n - 1)
                    nc.gpsimd.tensor_tensor(g[:, n % 2, :], y[:, n % 2, :], sz[:, i, :], ALU.mult).then_inc(g_ready, 1)
                if step + 2 < NU:
                    weighing(step + 2)
                if 4 <= step < NU + 4:
                    n = step - 4
                    c, s = units[n]
                    i = TPS * s + c
                    pool.wait_ge(ssq_ready, n + 1)
                    link(nc.gpsimd.tensor_scalar(ms[:, i:i + 1], ssq[:, i:i + 1], 1.0 / INNER, EPS, ALU.mult, ALU.add))
                    nc.gpsimd.tensor_tensor(rms[:, i:i + 1], ms[:, i:i + 1], core.mhalf[:, 0:1],
                                            ALU.pow).then_inc(rms_ready, 1)
                if step >= 11 and (step - 11) % SEQS == 0:
                    c = (step - 11) // SEQS
                    pool.wait_ge(veps_ready, c + 1)
                    ln_rstd(nc, core, link, shared.ln, slice(c, None, TPS))
            pool.wait_ge(veps_ready, TPS)
            ln_rstd(nc, core, link, shared.ln, slice(TPS - 1, None, TPS))

        @block.tensor
        def _(pe):
            pe.wait_ge(adt_ready, 1)
            flat = adt[:].rearrange("p i h -> p (i h)")
            for k, m in enumerate((core.causal, core.after, core.ones)):
                ins = nc.tensor.matmul(g_ps[1][:, 64 * k:64 * (k + 1)], m[:], flat, start=True, stop=True)
            ins.then_inc(cum_made, 1)

            def chunk(n):
                c, s = units[n]
                i = TPS * s + c
                tok = slice(P * i, P * (i + 1))
                if n >= 2:
                    pe.wait_ge(gm_ready, n - 1)
                if n == 1:
                    pe.wait_ge(decay_ready, 1)
                nc.tensor.matmul(g_ps[n % 2][:, 0:P], xbc[:, 2, tok], xbc[:, 3, tok],
                                 start=True, stop=True).then_inc(cb_made, 1)
                pe.wait_ge(segl_ready, n + 1)
                if n >= 2:
                    pe.wait_ge(expo_ready, n - 1)
                for h in range(HEADS):
                    ins = nc.tensor.matmul(seg_ps[n % 2][:, P * h:P * (h + 1)], seg_l[:, n % 2, h, :],
                                           core.causal[:], start=True, stop=True)
                ins.then_inc(seg_made, 1)

            def output(n):
                c, s = units[n]
                i = TPS * s + c
                ps = y_ps[n % 2]
                if n >= 2:
                    pe.wait_ge(y_ready, n - 1)
                if c:
                    pe.wait_ge(st_ready, n - SEQS + 1)
                    nc.tensor.matmul(ps[:, INNER:2 * INNER], xbc[:, 3, P * i:P * (i + 1)], state[:, s, :],
                                     start=True, stop=True)
                pe.wait_ge(xdt_ready, n + 1)
                nc.tensor.matmul(ps[:, 0:INNER], core.ident[:], dx[:, n % WRING, :], start=True, stop=False)
                pe.wait_ge(mix_ready, n + 1)
                for h in range(HEADS):
                    dst = ps[:, HDIM * h:HDIM * (h + 1)]
                    ins = nc.tensor.matmul(dst, mix[:, n % 2, h, :], xdt[:, n % WRING, HDIM * h:HDIM * (h + 1)],
                                           start=False, stop=h == HEADS - 1)
                ins.then_inc(y_made, 1)
                if c < TPS - 1:
                    pe.wait_ge(xw_ready, n + 1)
                    if n:
                        pe.wait_ge(st_ready, n)
                    nc.tensor.matmul(st_ps[:, 0:INNER], xtok[:, i, INNER:XTOK], xw[:, n % WRING, :],
                                     start=True, stop=True).then_inc(st_made, 1)

            def turn(n):
                pe.wait_ge(g_ready, n + 1)
                if n:
                    pe.wait_ge(x_ready, n)
                for k in range(2):
                    ins = nc.tensor.transpose(out_ps[:, P * k:P * (k + 1)], g[:, n % 2, P * k:P * (k + 1)],
                                              core.ident[:])
                ins.then_inc(g_turned, 1)

            def project(n):
                pe.wait_ge(gT_ready, n + 1)
                if n == 0:
                    pe.wait_ge(shared.w_out_in, 16)
                for k in range(2):
                    ins = nc.tensor.matmul(out_ps[:, INNER:INNER + P], gT[:, n % 2, k, :], shared.w_out[:, k, :],
                                           start=k == 0, stop=k == 1)
                ins.then_inc(out_made, 1)

            for step in range(NU + 5):
                if 5 <= step < NU + 5:
                    project(step - 5)
                if step < NU:
                    chunk(step)
                if 4 <= step < NU + 4:
                    turn(step - 4)
                if 1 <= step < NU + 1:
                    output(step - 1)


class LayerNorm:

    def __init__(self, nc, ctx, name):
        def sb(part, shape):
            return ctx.enter_context(nc.sbuf_tensor(f"{name}_{part}", shape, F32))

        self.stats = sb("stats", [P, TILES, 6])
        self.mv = sb("mv", [P, TILES, 2])
        self.veps = sb("veps", [P, TILES])
        self.rstd = sb("rstd", [P, TILES])
        self.nbias = sb("nbias", [P, TILES])


def ln_stats(nc, link, ln, x, s, veps_ready):
    a, b = TPS * s, TPS * (s + 1)
    for i in range(a, b):
        last = nc.vector.bn_stats(ln.stats[:, i, :], x[:, i, :])
    link(last)
    for i in range(a, b):
        last = nc.vector.bn_aggr(ln.mv[:, i, :], ln.stats[:, i, :])
    link(last)
    nc.vector.tensor_scalar(ln.veps[:, a:b], ln.mv[:, a:b, 1], EPS, None, ALU.add).then_inc(veps_ready, 1)


def ln_rstd(nc, core, link, ln, tiles):
    link(nc.gpsimd.tensor_tensor(ln.rstd[:, tiles], ln.veps[:, tiles], core.mhalf[:, tiles], ALU.pow))
    link(nc.gpsimd.tensor_tensor(ln.nbias[:, tiles], ln.mv[:, tiles, 0], ln.rstd[:, tiles], ALU.mult))
    link(nc.gpsimd.tensor_scalar(ln.nbias[:, tiles], ln.nbias[:, tiles], -1.0, 0.0, ALU.mult, ALU.add))


def of_seq(s):
    return slice(TPS * s, TPS * (s + 1))


def ln_apply(nc, ln, x, out, s, normed):
    for i in range(TPS * s, TPS * (s + 1)):
        nc.gpsimd.tensor_scalar(out[:, i, :], x[:, i, :], ln.rstd[:, i:i + 1], ln.nbias[:, i:i + 1],
                                ALU.mult, ALU.add).then_inc(normed, 1)


def phase_moe(core, io, tag, ln, prefetch=(), landed=None, out=None):
    nc = core.nc
    UNITS = SEQS * FBLK
    with ExitStack() as ctx:
        def sb(name, shape, dt=F32):
            return ctx.enter_context(nc.sbuf_tensor(f"{tag}_{name}", shape, dt))

        def sem(name):
            return core.semaphore(f"{tag}_{name}")

        x, w = core.x, core.wsplit
        norm = sb("norm", [P, TILES, P])
        normT = sb("normT", [P, TOKENS])
        x_hi = sb("x_hi", [P, TOKENS], F16)
        x_lo = sb("x_lo", [P, TOKENS], F16)
        shift = sb("shift", [P, TILES, EXPERTS])
        prob = sb("prob", [P, TILES, EXPERTS])
        prob2 = sb("prob2", [P, TILES, EXPERTS])
        eq = sb("eq", [P, TILES, EXPERTS])
        pick = sb("pick", [P, TILES, EXPERTS])
        first = sb("first", [P, TILES, EXPERTS])
        second = sb("second", [P, TILES, EXPERTS])
        rank = sb("rank", [P, EXPERTS])
        top = sb("top", [P, 6, TILES])
        w_branch = sb("w_branch", [P, BRANCHES, TILES])
        silu = sb("silu", [P, 2, SEQ])
        hid = sb("hid", [P, 2, SEQ])
        hid_hi = sb("hid_hi", [P, 2 * FBLK, SEQ], F16)
        hid_lo = sb("hid_lo", [P, 2 * FBLK, SEQ], F16)

        gate_ps, up_ps, down_ps, turn_ps, logit_ps = (core.banks[0:2], core.banks[2:4], core.banks[4:6],
                                                      core.banks[6], core.banks[7])
        normed, normT_ready = sem("normed"), sem("normT")

        x_turned, hi_ready, lo_ready, logits_made = sem("x_turned"), sem("x_hi"), sem("x_lo"), sem("logits")
        shift_ready, exp_ready, route_ready, rank_ready = sem("shift"), sem("exp"), sem("route"), sem("rank")
        gate_made, up_made, down_made = sem("gate"), sem("up"), sem("down")
        silu_ready, hid_ready, hid_hi_ready = sem("silu"), sem("hid"), sem("hid_hi")
        hid_lo0_ready, hid_lo1_ready, added = sem("hid_lo0"), sem("hid_lo1"), sem("added")
        dve_step, pool_step, act_step, stored = sem("dve_step"), sem("pool_step"), sem("act_step"), sem("stored")

        block = ctx.enter_context(nc.Block())

        @block.gpsimd
        def _(pool):
            steps = [0]

            def link(ins):
                steps[0] += 1
                ins.then_inc(pool_step, 1)
                pool.wait_ge(pool_step, steps[0])

            for s in range(SEQS):
                ln_apply(nc, ln, x, norm, s, normed)
            for k in range(EXPERTS):
                nc.gpsimd.memset(rank[:, k:k + 1], float(EXPERTS - k)).then_inc(rank_ready, 1)
            nc.gpsimd.memset(w_branch[:, 0, :], DOWN_UNSCALE).then_inc(rank_ready, 1)

            def branch(e):
                for s in range(SEQS):
                    slot = FBLK * (s % 2)
                    pool.wait_ge(hid_hi_ready, e * UNITS + 2 * s + 1)
                    nc.gpsimd.tensor_tensor(hid_lo[:, slot, :], hid[:, 0, :], hid_hi[:, slot, :],
                                            ALU.subtract).then_inc(hid_lo0_ready, 1)
            branch(0)
            with pool.Fori(1, BRANCHES) as e:
                branch(e)

        @block.vector
        def _(dve):
            steps = [0]

            def link(ins):
                steps[0] += 1
                ins.then_inc(dve_step, 1)
                dve.wait_ge(dve_step, steps[0])

            def low_x(s):
                dve.wait_ge(hi_ready, s + 1)
                tok = slice(SEQ * s, SEQ * (s + 1))
                nc.vector.scalar_tensor_tensor(x_lo[:, tok], normT[:, tok], X_SCALE, x_hi[:, tok], ALU.mult,
                                               ALU.subtract).then_inc(lo_ready, 1)

            def all_experts(ap):
                return ap.unsqueeze(2).broadcast_to([P, TILES, EXPERTS])

            def choose(scores, chosen, best):
                link(nc.vector.tensor_reduce(best, scores, AX_X, ALU.max))
                link(nc.vector.tensor_tensor(eq[:], scores, all_experts(best), ALU.is_equal))
                link(nc.vector.tensor_tensor(pick[:], eq[:], rank[:].unsqueeze(1)
                                             .broadcast_to([P, TILES, EXPERTS]), ALU.mult))
                link(nc.vector.tensor_reduce(top[:, 5, :], pick[:], AX_X, ALU.max))
                link(nc.vector.tensor_tensor(chosen, pick[:], all_experts(top[:, 5, :]), ALU.is_equal))

            def route_softmax():
                dve.wait_ge(logits_made, 1)
                logits = logit_ps[:, 0:TILES * EXPERTS].rearrange("p (i k) -> p i k", i=TILES)
                link(nc.vector.tensor_reduce(top[:, 0, :], logits, AX_X, ALU.max))
                nc.vector.tensor_tensor(shift[:], logits, all_experts(top[:, 0, :]),
                                        ALU.subtract).then_inc(shift_ready, 1)

            def route_choose():
                dve.wait_ge(exp_ready, 1)
                dve.wait_ge(rank_ready, EXPERTS + 1)
                link(nc.vector.tensor_reduce(top[:, 1, :], shift[:], AX_X, ALU.add))
                link(nc.vector.reciprocal(top[:, 2, :], top[:, 1, :]))
                link(nc.vector.tensor_tensor(prob[:], shift[:], all_experts(top[:, 2, :]), ALU.mult))
                choose(prob[:], first[:], top[:, 3, :])
                link(nc.vector.scalar_tensor_tensor(prob2[:], first[:], -4.0, prob[:], ALU.mult, ALU.add))
                choose(prob2[:], second[:], top[:, 4, :])
                link(nc.vector.scalar_tensor_tensor(top[:, 0, :], top[:, 3, :], 1e-20, top[:, 4, :], ALU.add, ALU.add))
                link(nc.vector.reciprocal(top[:, 1, :], top[:, 0, :]))
                link(nc.vector.tensor_tensor(first[:], first[:], second[:], ALU.add))
                link(nc.vector.scalar_tensor_tensor(first[:], first[:], DOWN_UNSCALE, prob[:], ALU.mult, ALU.mult))
                link(nc.vector.tensor_tensor(w_branch[:, 1:BRANCHES, :].rearrange("p k i -> p i k"), first[:],
                                             all_experts(top[:, 1, :]), ALU.mult))

            def hidden(e, u):
                dve.wait_ge(silu_ready, e * UNITS + u + 1)
                dve.wait_ge(up_made, e * UNITS + u + 1)
                peeled = isinstance(e, int) and e == 0
                if u % 2 == 0 and not (peeled and u == 0):
                    dve.wait_ge(hid_lo0_ready, e * SEQS + u // 2)
                if u % 2 and not (peeled and u == 1):
                    dve.wait_ge(hid_lo1_ready, e * SEQS + u // 2)
                nc.vector.scalar_tensor_tensor(hid[:, u % 2, :], up_ps[u % 2][:, :], GU_UNSCALE * H_SCALE,
                                               silu[:, u % 2, :], ALU.mult, ALU.mult).then_inc(hid_ready, 1)

            def low(s, made):
                slot = FBLK * (s % 2) + 1
                dve.wait_ge(hid_hi_ready, made)
                nc.vector.tensor_tensor(hid_lo[:, slot, :], hid[:, 1, :], hid_hi[:, slot, :],
                                        ALU.subtract).then_inc(hid_lo1_ready, 1)

            def add(e, s, count):
                dve.wait_ge(down_made, count)
                for c in range(TPS):
                    i = TPS * s + c
                    ins = nc.vector.scalar_tensor_tensor(x[:, i, :], down_ps[s % 2][:, P * c:P * (c + 1)],
                                                         w_branch[:, e, i:i + 1], x[:, i, :], ALU.mult, ALU.add)
                ins.then_inc(added, 1)

            def branch(e):
                for s in range(SEQS):
                    hidden(e, 2 * s)
                    if isinstance(e, int) and s + 1 < SEQS:
                        low_x(s + 1)
                    hidden(e, 2 * s + 1)
                    low(s, e * UNITS + 2 * s + 2)
                    if s:
                        add(e, s - 1, e * SEQS + s)
                    elif not (isinstance(e, int) and e == 0):
                        add(e - 1, SEQS - 1, e * SEQS)
            low_x(0)
            branch(0)
            route_softmax()
            route_choose()
            with dve.Fori(1, BRANCHES) as e:
                branch(e)
            add(BRANCHES - 1, SEQS - 1, BRANCHES * SEQS)

        @block.scalar
        def _(act):
            def high_x(s):
                act.wait_ge(x_turned, s + 1)
                tok = slice(SEQ * s, SEQ * (s + 1))
                nc.scalar.copy(normT[:, tok], turn_ps[:, :]).then_inc(normT_ready, 1)
                act.wait_ge(normT_ready, s + 1)
                nc.scalar.mul(x_hi[:, tok], normT[:, tok], X_SCALE).then_inc(hi_ready, 1)

            def high(u, made, read):
                slot = FBLK * (u // 2 % 2) + u % 2
                if read is not None:
                    act.wait_ge(down_made, read)
                act.wait_ge(hid_ready, made)
                nc.scalar.copy(hid_hi[:, slot, :], hid[:, u % 2, :]).then_inc(hid_hi_ready, 1)

            def branch(e):
                peeled = isinstance(e, int) and e == 0
                for s in range(SEQS):
                    for u in (2 * s, 2 * s + 1):
                        act.wait_ge(gate_made, e * UNITS + u + 1)
                        if not (peeled and s == 0):
                            act.wait_ge(hid_ready, e * UNITS + u - 1)
                        nc.scalar.activation(silu[:, u % 2, :], gate_ps[u % 2][:, :], ACT.Silu,
                                             scale=GU_UNSCALE).then_inc(silu_ready, 1)
                        if isinstance(e, int) and u == 2 * s and s + 1 < SEQS:
                            high_x(s + 1)
                    for u in (2 * s, 2 * s + 1):
                        high(u, e * UNITS + u + 1, None if peeled and s < 2 else e * SEQS + s - 1)
            nc.scalar.activation(silu[:, 0, 0:1], core.ident[:, 0:1], ACT.Silu).then_inc(act_step, 1)
            act.wait_ge(act_step, 1)
            high_x(0)
            branch(0)
            act.wait_ge(shift_ready, 1)
            nc.scalar.activation(shift[:], shift[:], ACT.Exp).then_inc(exp_ready, 1)
            with act.Fori(1, BRANCHES) as e:
                branch(e)

        @block.tensor
        def _(pe):
            def turn(s):
                for c in range(TPS):
                    pe.wait_ge(normed, TPS * s + c + 1)
                    if c == 0 and s:
                        pe.wait_ge(normT_ready, s)
                    ins = nc.tensor.transpose(turn_ps[:, P * c:P * (c + 1)], norm[:, TPS * s + c, :], core.ident[:])
                ins.then_inc(x_turned, 1)

            def logits():
                pe.wait_ge(normT_ready, SEQS)
                for i in range(TILES):
                    ins = nc.tensor.matmul(logit_ps[:, EXPERTS * i:EXPERTS * (i + 1)], normT[:, P * i:P * (i + 1)],
                                           core.router_w[:], start=True, stop=True)
                ins.then_inc(logits_made, 1)

            def gate_up(e, u):
                s, blk = u // 2, u % 2
                tok = slice(SEQ * s, SEQ * (s + 1))
                if not (isinstance(e, int) and e == 0 and u < 2):
                    pe.wait_ge(hid_ready, e * UNITS + u - 1)
                if isinstance(e, int) and e == 0 and blk == 0:
                    pe.wait_ge(lo_ready, s + 1)
                for part, bank, made in ((0, gate_ps, gate_made), (2, up_ps, up_made)):
                    hi = w[:, e, part, P * blk:P * (blk + 1)]
                    lo = w[:, e, part + 1, P * blk:P * (blk + 1)]
                    dst = bank[u % 2][:, :]
                    nc.tensor.matmul(dst, hi, x_hi[:, tok], start=True, stop=False)
                    nc.tensor.matmul(dst, hi, x_lo[:, tok], start=False, stop=False)
                    nc.tensor.matmul(dst, lo, x_hi[:, tok], start=False, stop=True).then_inc(made, 1)

            def down(e, s, count):
                pe.wait_ge(hid_lo0_ready, count)
                pe.wait_ge(hid_lo1_ready, count)
                if not (isinstance(count, int) and count <= 2):
                    pe.wait_ge(added, count - 2)
                for c in range(TPS):
                    dst = down_ps[s % 2][:, P * c:P * (c + 1)]
                    for blk in range(FBLK):
                        slot = FBLK * (s % 2) + blk
                        h_hi = hid_hi[:, slot, P * c:P * (c + 1)]
                        h_lo = hid_lo[:, slot, P * c:P * (c + 1)]
                        d_hi = w[:, e, 4, P * blk:P * (blk + 1)]
                        d_lo = w[:, e, 5, P * blk:P * (blk + 1)]
                        nc.tensor.matmul(dst, h_hi, d_hi, start=blk == 0, stop=False)
                        nc.tensor.matmul(dst, h_hi, d_lo, start=False, stop=False)
                        ins = nc.tensor.matmul(dst, h_lo, d_hi, start=False, stop=blk == FBLK - 1)
                ins.then_inc(down_made, 1)

            def branch(e):
                for s in range(SEQS):
                    gate_up(e, 2 * s)
                    if isinstance(e, int) and s + 1 < SEQS:
                        turn(s + 1)
                    gate_up(e, 2 * s + 1)
                    if isinstance(e, int) and s == SEQS - 1:
                        logits()
                    if s:
                        down(e, s - 1, e * SEQS + s)
                    elif not (isinstance(e, int) and e == 0):
                        down(e - 1, SEQS - 1, e * SEQS)
            turn(0)
            branch(0)
            with pe.Fori(1, BRANCHES) as e:
                branch(e)
            down(BRANCHES - 1, SEQS - 1, BRANCHES * SEQS)

        @block.sync
        def _(sp):
            core.clear_retired(sp)
            for dst, name in prefetch:
                sp.dma_start(dst[:], io[name]).then_inc(landed, 16)
            if out is not None:
                dst = out.rearrange("s (c p) d -> s p c d", p=P)
                for s in range(SEQS):
                    sp.wait_ge(added, (BRANCHES - 1) * SEQS + s + 1)
                    sp.dma_start(dst[s], x[:, TPS * s:TPS * (s + 1), :]).then_inc(stored, 16)
                sp.wait_ge(stored, 16 * SEQS)


def phase_time_mix(core, io, shared):
    nc = core.nc
    with ExitStack() as ctx:
        def sb(name, shape, dt=F32):
            return ctx.enter_context(nc.sbuf_tensor("tm_" + name, shape, dt))

        def sem(name):
            return core.semaphore("tm_" + name)

        x, x4, w_rkvo = core.x, shared.x4, shared.w_rkvo
        ln_a, ln_b = LayerNorm(nc, ctx, "tm_ln0"), LayerNorm(nc, ctx, "tm_ln1")
        veps_a, veps_b, veps_cm, normed = sem("veps_a"), sem("veps_b"), sem("veps_cm"), sem("normed")
        v_eps = sb("v_eps", [P, TILES])
        hn = sb("hn", [P, TILES, P])
        hT = sb("hT", [P, SEQS, SEQ + 1])
        w_now = sb("w_now", [P, 3, P])
        w_prev = sb("w_prev", [P, 3, P])
        w_decay = sb("w_decay", [P, 1])
        pp = sb("pp", [P, SEQ + 1])
        aa = sb("aa", [P, 2, SEQ + 1])
        bb = sb("bb", [P, 2, SEQ + 1])
        lead = sb("lead", [P, 2, SEQ])
        expo = sb("expo", [P, 2, 4, SEQ])
        e_r = sb("e_r", [P, 2, SEQ])
        e2v = sb("e2v", [P, SEQ])
        y2v = sb("y2v", [P, 2, SEQ])
        num = sb("num", [P, 2, SEQ])
        den = sb("den", [P, 2, SEQ])
        den_r = sb("den_r", [P, SEQ])
        recip = sb("recip", [P, SEQ])
        att = sb("att", [P, 2, SEQ])

        turn_ps, kvr_ps, out_ps = core.banks[0], (core.banks[1:4], core.banks[4:7]), core.banks[7]

        decay_act, decay_ready, rstd_ready = sem("decay_act"), sem("decay"), sem("rstd")
        h_turned, hT_ready, w_now_ready, w_prev_ready = sem("h_turned"), sem("hT"), sem("w_now"), sem("w_prev")
        kvr_made, raw_ready, lead_ready, lead_act = sem("kvr"), sem("raw"), sem("lead"), sem("lead_act")
        expo_ready, aabb_ready, numden_ready, att_ready = sem("expo"), sem("aabb"), sem("numden"), sem("att")
        e2v_ready, neg_r_ready, er_ready, y2v_ready, zeroed = sem("e2v"), sem("neg_r"), sem("er"), sem("y2v"), sem("zeroed")
        out_made, x4_ready = sem("out"), sem("x4")
        dve_step, pool_step, act_step = sem("dve_step"), sem("pool_step"), sem("act_step")

        block = ctx.enter_context(nc.Block())

        @block.sync
        def _(sp):
            core.clear_retired(sp)

        @block.gpsimd
        def _(pool):
            steps = [0]

            def link(ins):
                steps[0] += 1
                ins.then_inc(pool_step, 1)
                pool.wait_ge(pool_step, steps[0])

            nc.gpsimd.memset(hT[:, :, 0:1], 0.0).then_inc(zeroed, 1)
            nc.gpsimd.memset(pp[:, 0:1], -1e38).then_inc(zeroed, 1)
            nc.gpsimd.memset(aa[:, :, 0:1], 0.0).then_inc(zeroed, 1)
            nc.gpsimd.memset(bb[:, :, 0:1], 0.0).then_inc(zeroed, 1)

            pool.wait_ge(shared.w_b_in, 16 * 4)
            for j, name in enumerate(("tmk", "tmv", "tmr")):
                nc.gpsimd.tensor_scalar(w_now[:, j, :], w_rkvo[:, j, :], col(core, name), None,
                                        ALU.mult).then_inc(w_now_ready, 1)
            for j in range(3):
                pool.wait_ge(w_now_ready, j + 1)
                nc.gpsimd.tensor_tensor(w_prev[:, j, :], w_rkvo[:, j, :], w_now[:, j, :],
                                        ALU.subtract).then_inc(w_prev_ready, 1)

            def rstd(s):
                a, b = TPS * s, TPS * (s + 1)
                pool.wait_ge(veps_a, s + 1)
                nc.gpsimd.tensor_tensor(ln_a.rstd[:, a:b], ln_a.veps[:, a:b], core.mhalf[:, a:b],
                                        ALU.pow).then_inc(rstd_ready, 1)

            def sums(s):
                k = s % 2
                pool.wait_ge(aabb_ready, 2 * s + 1)
                pool.wait_ge(expo_ready, 4 * (s + 1))
                if s >= 2:
                    pool.wait_ge(att_ready, s - 1)
                link(nc.gpsimd.tensor_tensor(den[:, k, :], expo[:, k, 2, :], bb[:, k, 0:SEQ], ALU.mult))
                nc.gpsimd.tensor_tensor(den[:, k, :], den[:, k, :], expo[:, k, 3, :],
                                        ALU.add).then_inc(numden_ready, 1)
                pool.wait_ge(aabb_ready, 2 * (s + 1))
                link(nc.gpsimd.tensor_tensor(num[:, k, :], expo[:, k, 2, :], aa[:, k, 0:SEQ], ALU.mult))
                pool.wait_ge(y2v_ready, s + 1)
                nc.gpsimd.tensor_tensor(num[:, k, :], num[:, k, :], y2v[:, k, :], ALU.add).then_inc(numden_ready, 1)

            rstd(0)
            rstd(1)
            for step in range(SEQS + 1):
                if step < SEQS:
                    pool.wait_ge(veps_b, step + 1)
                    ln_rstd(nc, core, link, ln_b, of_seq(step))
                    ln_apply(nc, ln_b, x4, hn, step, normed)
                if step + 2 < SEQS:
                    rstd(step + 2)
                if step >= 1:
                    sums(step - 1)
            pool.wait_ge(veps_cm, 1)
            ln_rstd(nc, core, link, shared.ln_cm, of_seq(0))

        @block.vector
        def _(dve):
            steps = [0]

            def link(ins):
                steps[0] += 1
                ins.then_inc(dve_step, 1)
                dve.wait_ge(dve_step, steps[0])

            dve.wait_ge(decay_act, 1)
            nc.vector.tensor_scalar(w_decay[:], w_decay[:], -1.0, None, ALU.mult).then_inc(decay_ready, 1)
            w_rows = w_decay[:].broadcast_to([P, SEQ])

            def double_stats(s):
                a, b = TPS * s, TPS * (s + 1)
                for i in range(a, b):
                    last = nc.vector.bn_stats(ln_a.stats[:, i, :], x[:, i, :])
                link(last)
                for i in range(a, b):
                    last = nc.vector.bn_aggr(ln_a.mv[:, i, :], ln_a.stats[:, i, :])
                link(last)
                link(nc.vector.tensor_scalar(v_eps[:, a:b], ln_a.mv[:, a:b, 1], EPS, EPS, ALU.add, ALU.mult))
                nc.vector.tensor_tensor(ln_a.veps[:, a:b], v_eps[:, a:b], ln_a.mv[:, a:b, 1],
                                        ALU.add).then_inc(veps_a, 1)

            def rows(name):
                return col(core, name, 0, P)

            def normalise(s):
                a, b = TPS * s, TPS * (s + 1)
                for i in range(a, b):
                    ins = nc.vector.scalar_tensor_tensor(x4[:, i, :], x[:, i, :], ln_a.mv[:, i, 0:1], rows("ln0_w"),
                                                         ALU.subtract, ALU.mult)
                link(ins)
                dve.wait_ge(rstd_ready, s + 1)
                for i in range(a, b):
                    ins = nc.vector.scalar_tensor_tensor(x4[:, i, :], x4[:, i, :], ln_a.rstd[:, i:i + 1],
                                                         rows("ln0_b"), ALU.mult, ALU.add)
                link(ins)

            def scans(s):
                k = s % 2
                kk, vv = kvr_ps[k][0][:, :], kvr_ps[k][1][:, :]
                if s == 0:
                    dve.wait_ge(decay_ready, 1)
                    dve.wait_ge(zeroed, 4)
                dve.wait_ge(kvr_made, 3 * s + 1)
                link(nc.vector.tensor_tensor_scan(pp[:, 1:SEQ + 1], w_rows, kk, -1e38, ALU.add, ALU.max))
                if s >= 2:
                    dve.wait_ge(expo_ready, 4 * (s - 1))
                    dve.wait_ge(numden_ready, 2 * (s - 1))
                nc.vector.scalar_tensor_tensor(lead[:, k, :], pp[:, 0:SEQ], col(core, "first"), kk,
                                               ALU.subtract, ALU.subtract).then_inc(lead_ready, 1)
                nc.vector.scalar_tensor_tensor(expo[:, k, 0, :], pp[:, 0:SEQ], w_decay[:], pp[:, 1:SEQ + 1],
                                               ALU.add, ALU.subtract).then_inc(raw_ready, 1)
                nc.vector.tensor_tensor(expo[:, k, 1, :], kk, pp[:, 1:SEQ + 1], ALU.subtract).then_inc(raw_ready, 1)
                dve.wait_ge(kvr_made, 3 * (s + 1))
                nc.vector.tensor_scalar(e_r[:, k, :], kvr_ps[k][2][:, :], -1.0, 80.0, ALU.mult,
                                        ALU.min).then_inc(neg_r_ready, 1)
                dve.wait_ge(expo_ready, 4 * s + 2)
                nc.vector.tensor_tensor(e2v[:], expo[:, k, 1, :], vv, ALU.mult).then_inc(e2v_ready, 1)
                nc.vector.tensor_tensor_scan(bb[:, k, 1:SEQ + 1], expo[:, k, 0, :], expo[:, k, 1, :], 0.0,
                                             ALU.mult, ALU.add).then_inc(aabb_ready, 1)
                dve.wait_ge(e2v_ready, s + 1)
                nc.vector.tensor_tensor_scan(aa[:, k, 1:SEQ + 1], expo[:, k, 0, :], e2v[:], 0.0,
                                             ALU.mult, ALU.add).then_inc(aabb_ready, 1)
                dve.wait_ge(expo_ready, 4 * s + 4)
                nc.vector.tensor_tensor(y2v[:, k, :], expo[:, k, 3, :], vv, ALU.mult).then_inc(y2v_ready, 1)

            def divide(s):
                k = s % 2
                dve.wait_ge(numden_ready, 2 * s + 1)
                dve.wait_ge(er_ready, s + 1)
                link(nc.vector.scalar_tensor_tensor(den_r[:], e_r[:, k, :], 1.0, den[:, k, :], ALU.add, ALU.mult))
                link(nc.vector.reciprocal(recip[:], den_r[:]))
                dve.wait_ge(numden_ready, 2 * (s + 1))
                if s >= 2:
                    dve.wait_ge(out_made, s - 1)
                nc.vector.tensor_tensor(att[:, k, :], num[:, k, :], recip[:], ALU.mult).then_inc(att_ready, 1)

            def join(s):
                a, b = TPS * s, TPS * (s + 1)
                dve.wait_ge(out_made, s + 1)
                nc.vector.tensor_tensor(x4[:, a:b, :], x4[:, a:b, :],
                                        out_ps[:, :].rearrange("p (c d) -> p c d", c=TPS), ALU.add).then_inc(x4_ready, 1)

            double_stats(0)
            double_stats(1)
            for step in range(SEQS + 4):
                if 3 <= step < SEQS + 3:
                    divide(step - 3)
                if 2 <= step < SEQS + 2:
                    scans(step - 2)
                if step < SEQS:
                    normalise(step)
                    ln_stats(nc, link, ln_b, x4, step, veps_b)
                if step + 2 < SEQS:
                    double_stats(step + 2)
                if step == SEQS + 3:
                    dve.wait_ge(x4_ready, 1)
                    ln_stats(nc, link, shared.ln_cm, x4, 0, veps_cm)
                if step >= 4:
                    join(step - 4)

        @block.scalar
        def _(act):
            nc.scalar.activation(w_decay[:], col(core, "decay"), ACT.Exp).then_inc(decay_act, 1)
            for step in range(SEQS + 2):
                if step >= 2:
                    s = step - 2
                    k = s % 2
                    for j in range(2):
                        act.wait_ge(raw_ready, 2 * s + j + 1)
                        nc.scalar.activation(expo[:, k, j, :], expo[:, k, j, :], ACT.Exp).then_inc(expo_ready, 1)
                    act.wait_ge(lead_ready, s + 1)
                    for j, sign in ((2, -1.0), (3, 1.0)):
                        nc.scalar.activation(expo[:, k, j, :], lead[:, k, :], ACT.Relu, scale=sign).then_inc(lead_act, 1)
                        act.wait_ge(lead_act, 2 * s + j - 1)
                        nc.scalar.activation(expo[:, k, j, :], expo[:, k, j, :], ACT.Exp,
                                             scale=-1.0).then_inc(expo_ready, 1)
                    act.wait_ge(neg_r_ready, s + 1)
                    nc.scalar.activation(e_r[:, k, :], e_r[:, k, :], ACT.Exp).then_inc(er_ready, 1)
                if step < SEQS:
                    s = step
                    act.wait_ge(h_turned, s + 1)
                    nc.scalar.activation(hT[:, s, 1:SEQ + 1], turn_ps[:, :], ACT.Identity,
                                         bias=col(core, "ln1_b"), scale=col(core, "ln1_w")).then_inc(hT_ready, 1)

        @block.tensor
        def _(pe):
            pe.wait_ge(shared.w_b_in, 16 * 4)
            for step in range(SEQS + 3):
                if 1 <= step < SEQS + 1:
                    s = step - 1
                    pe.wait_ge(hT_ready, s + 1)
                    if s == 0:
                        pe.wait_ge(zeroed, 4)
                        pe.wait_ge(w_prev_ready, 3)
                    for j in range(3):
                        if s >= 2 and j == 0:
                            pe.wait_ge(y2v_ready, s - 1)
                            pe.wait_ge(neg_r_ready, s - 1)
                        nc.tensor.matmul(kvr_ps[s % 2][j][:, :], w_now[:, j, :], hT[:, s, 1:SEQ + 1],
                                         start=True, stop=False)
                        nc.tensor.matmul(kvr_ps[s % 2][j][:, :], w_prev[:, j, :], hT[:, s, 0:SEQ],
                                         start=False, stop=True).then_inc(kvr_made, 1)
                if step < SEQS:
                    s = step
                    for c in range(TPS):
                        pe.wait_ge(normed, TPS * s + c + 1)
                        if c == 0 and s:
                            pe.wait_ge(hT_ready, s)
                        ins = nc.tensor.transpose(turn_ps[:, P * c:P * (c + 1)], hn[:, TPS * s + c, :], core.ident[:])
                    ins.then_inc(h_turned, 1)
                if step >= 3:
                    s = step - 3
                    pe.wait_ge(att_ready, s + 1)
                    if s:
                        pe.wait_ge(x4_ready, s)
                    for c in range(TPS):
                        ins = nc.tensor.matmul(out_ps[:, P * c:P * (c + 1)], att[:, s % 2, P * c:P * (c + 1)],
                                               w_rkvo[:, 3, :], start=True, stop=True)
                    ins.then_inc(out_made, 1)


def phase_channel_mix(core, io, shared):
    nc = core.nc
    HB = HIDDEN // P
    HRING = 3
    with ExitStack() as ctx:
        def sb(name, shape, dt=F32):
            return ctx.enter_context(nc.sbuf_tensor("cm_" + name, shape, dt))

        def sem(name):
            return core.semaphore("cm_" + name)

        x, x4 = core.x, shared.x4
        ln = shared.ln_cm
        veps_ready, normed, veps_next = sem("veps"), sem("normed"), sem("veps_next")
        hn = sb("hn", [P, TILES, P])
        hT = sb("hT", [P, SEQS, SEQ + 1])
        dif = sb("dif", [P, 2, SEQ])
        mixed = sb("mixed", [P, 2, 2, SEQ])
        relu = sb("relu", [P, HRING, SEQ])
        sq = sb("sq", [P, 2, HB, SEQ])
        sig = sb("sig", [P, 2, SEQ])
        rkv = sb("rkv", [P, 2, SEQ])

        turn_ps, hid_ps, kv_ps, r_ps = core.banks[0], core.banks[1:4], core.banks[4:6], core.banks[6:8]
        h_turned, hT_ready, dif_ready, mixed_ready = sem("h_turned"), sem("hT"), sem("dif"), sem("mixed")
        hid_made, relu_ready, sq_ready, kv_made = sem("hid"), sem("relu"), sem("sq"), sem("kv")
        r_made, sig_ready, rkv_ready, x_ready, zeroed = sem("r"), sem("sig"), sem("rkv"), sem("x"), sem("zeroed")
        x4_added = sem("x4_added")
        dve_step, pool_step = sem("dve_step"), sem("pool_step")

        block = ctx.enter_context(nc.Block())

        @block.sync
        def _(sp):
            core.clear_retired(sp)

        @block.gpsimd
        def _(pool):
            steps = [0]

            def link(ins):
                steps[0] += 1
                ins.then_inc(pool_step, 1)
                pool.wait_ge(pool_step, steps[0])

            nc.gpsimd.memset(hT[:, :, 0:1], 0.0).then_inc(zeroed, 1)
            def normalise(s):
                if s:
                    pool.wait_ge(veps_ready, s)
                    ln_rstd(nc, core, link, ln, of_seq(s))
                ln_apply(nc, ln, x4, hn, s, normed)

            def difference(s):
                pool.wait_ge(hT_ready, s + 1)
                if s == 0:
                    pool.wait_ge(zeroed, 1)
                if s >= 2:
                    pool.wait_ge(mixed_ready, 2 * (s - 1))
                nc.gpsimd.tensor_tensor(dif[:, s % 2, :], hT[:, s, 1:SEQ + 1], hT[:, s, 0:SEQ],
                                        ALU.subtract).then_inc(dif_ready, 1)

            normalise(0)
            normalise(1)
            for s in range(SEQS):
                difference(s)
                if s + 2 < SEQS:
                    normalise(s + 2)
                nc.gpsimd.tensor_tensor(x[:, of_seq(s), :], x[:, of_seq(s), :], x4[:, of_seq(s), :],
                                        ALU.add).then_inc(x4_added, 1)
            for s in range(SEQS):
                pool.wait_ge(veps_next, s + 1)
                ln_rstd(nc, core, link, shared.ln, of_seq(s))

        @block.vector
        def _(dve):
            steps = [0]

            def link(ins):
                steps[0] += 1
                ins.then_inc(dve_step, 1)
                dve.wait_ge(dve_step, steps[0])

            def mixing(s):
                dve.wait_ge(dif_ready, s + 1)
                if s >= 2:
                    dve.wait_ge(hid_made, HB * (s - 1))
                    dve.wait_ge(r_made, s - 1)
                for j, name in enumerate(("cmk", "cmr")):
                    nc.vector.scalar_tensor_tensor(mixed[:, s % 2, j, :], dif[:, s % 2, :], col(core, name),
                                                   hT[:, s, 0:SEQ], ALU.mult, ALU.add).then_inc(mixed_ready, 1)

            def squares(s):
                for b in range(HB):
                    n = HB * s + b
                    dve.wait_ge(relu_ready, n + 1)
                    if s >= 2 and b == 0:
                        dve.wait_ge(kv_made, TPS * (s - 1))
                    nc.vector.scalar_tensor_tensor(sq[:, s % 2, b, :], hid_ps[n % HRING][:, :], 0.0,
                                                   relu[:, n % HRING, :], ALU.max, ALU.mult).then_inc(sq_ready, 1)

            def gated(s):
                dve.wait_ge(kv_made, TPS * (s + 1))
                dve.wait_ge(sig_ready, s + 1)
                nc.vector.tensor_tensor(rkv[:, s % 2, :], sig[:, s % 2, :], kv_ps[s % 2][:, :],
                                        ALU.mult).then_inc(rkv_ready, 1)
                dve.wait_ge(rkv_ready, s + 1)
                dve.wait_ge(x4_added, s + 1)
                nc.vector.tensor_tensor(x[:, of_seq(s), :], x[:, of_seq(s), :],
                                        rkv[:, s % 2, :].rearrange("p (c d) -> p c d", c=TPS),
                                        ALU.add).then_inc(x_ready, 1)
                dve.wait_ge(x_ready, s + 1)
                ln_stats(nc, link, shared.ln, x, s, veps_next)

            for s in range(1, SEQS):
                ln_stats(nc, link, ln, x4, s, veps_ready)
            mixing(0)
            for step in range(SEQS + 2):
                if step < SEQS:
                    squares(step)
                if step + 1 < SEQS:
                    mixing(step + 1)
                if step >= 2:
                    gated(step - 2)

        @block.scalar
        def _(act):
            def shifted(s):
                act.wait_ge(h_turned, s + 1)
                nc.scalar.activation(hT[:, s, 1:SEQ + 1], turn_ps[:, :], ACT.Identity,
                                     bias=col(core, "ln2_b"), scale=col(core, "ln2_w")).then_inc(hT_ready, 1)

            shifted(0)
            shifted(1)
            for s in range(SEQS):
                for b in range(HB):
                    n = HB * s + b
                    act.wait_ge(hid_made, n + 1)
                    if n >= HRING:
                        act.wait_ge(sq_ready, n - HRING + 1)
                    nc.scalar.activation(relu[:, n % HRING, :], hid_ps[n % HRING][:, :],
                                         ACT.Relu).then_inc(relu_ready, 1)
                act.wait_ge(r_made, s + 1)
                if s >= 2:
                    act.wait_ge(rkv_ready, s - 1)
                nc.scalar.activation(sig[:, s % 2, :], r_ps[s % 2][:, :], ACT.Sigmoid).then_inc(sig_ready, 1)
                if s + 2 < SEQS:
                    shifted(s + 2)

        @block.tensor
        def _(pe):
            def turn(s):
                for c in range(TPS):
                    pe.wait_ge(normed, TPS * s + c + 1)
                    if c == 0 and s:
                        pe.wait_ge(hT_ready, s)
                    ins = nc.tensor.transpose(turn_ps[:, P * c:P * (c + 1)], hn[:, TPS * s + c, :], core.ident[:])
                ins.then_inc(h_turned, 1)

            def hidden(s):
                pe.wait_ge(mixed_ready, 2 * s + 1)
                for b in range(HB):
                    n = HB * s + b
                    if n >= HRING:
                        pe.wait_ge(sq_ready, n - HRING + 1)
                    nc.tensor.matmul(hid_ps[n % HRING][:, :], shared.w_fk[:, P * b:P * (b + 1)], mixed[:, s % 2, 0, :],
                                     start=True, stop=True).then_inc(hid_made, 1)

            def receptance(s):
                pe.wait_ge(mixed_ready, 2 * (s + 1))
                if s >= 2:
                    pe.wait_ge(sig_ready, s - 1)
                for c in range(TPS):
                    ins = nc.tensor.matmul(r_ps[s % 2][:, P * c:P * (c + 1)], mixed[:, s % 2, 1, P * c:P * (c + 1)],
                                           shared.w_fr[:], start=True, stop=True)
                ins.then_inc(r_made, 1)

            def values(s):
                pe.wait_ge(sq_ready, HB * (s + 1))
                if s >= 2:
                    pe.wait_ge(rkv_ready, s - 1)
                for c in range(TPS):
                    for b in range(HB):
                        ins = nc.tensor.matmul(kv_ps[s % 2][:, P * c:P * (c + 1)],
                                               sq[:, s % 2, b, P * c:P * (c + 1)], shared.w_fv[:, b, :],
                                               start=b == 0, stop=b == HB - 1)
                    ins.then_inc(kv_made, 1)

            turn(0)
            turn(1)
            for step in range(SEQS + 1):
                if step < SEQS:
                    hidden(step)
                    receptance(step)
                if step >= 1:
                    values(step - 1)
                if step + 2 < SEQS:
                    turn(step + 2)


class Shared:
    pass


def program(nc, io, stop_after=9):
    core = Core(nc)
    with ExitStack() as top:
        constants(core, top)
        ln_moe1, ln_moe2, ln_cm = (LayerNorm(nc, top, name) for name in ("ln_moe1", "ln_moe2", "ln_cm"))
        with ExitStack() as mamba:
            sh = Shared()

            def sb(name, shape, dt=F32):
                return mamba.enter_context(nc.sbuf_tensor(name, shape, dt))
            sh.ln = ln_moe1
            sh.q = sb("q", [P, TILES, P])
            sh.xbc = sb("xbc", [P, CONV_BLOCKS, TOKENS])
            sh.sz = sb("sz", [P, TILES, INNER])
            sh.dt_raw = sb("dt_raw", [P, TILES, HEADS])
            sh.xtok = sb("xtok", [P, TILES, XTOK])
            sh.moe_raw = sb("moe_raw", [P, MOE_RING, 3 * FFN])
            sh.w_out = sb("w_out", [P, 2, P])
            sh.w_out_in = mamba.enter_context(nc.semaphore("w_out_in"))
            phase_mamba_in(core, io, sh)
            core.end_phase()
            phase_ssd(core, io, sh)
            core.end_phase()
        with ExitStack() as rwkv:
            sh = Shared()

            def sb(name, shape, dt=F32):
                return rwkv.enter_context(nc.sbuf_tensor(name, shape, dt))
            sh.ln, sh.ln_cm = ln_moe2, ln_cm
            sh.w_rkvo = sb("w_rkvo", [P, 4, P])
            sh.w_fk = sb("w_fk", [P, HIDDEN])
            sh.w_fr = sb("w_fr", [P, P])
            sh.w_fv = sb("w_fv", [P, HIDDEN // P, P])
            sh.w_b_in = rwkv.enter_context(nc.semaphore("w_b_in"))
            phase_moe(core, io, "moe1", ln_moe1, landed=sh.w_b_in,
                      prefetch=[(sh.w_rkvo, "w_rkvo"), (sh.w_fk, "w_fk"), (sh.w_fr, "w_fr"), (sh.w_fv, "w_fv")])
            core.end_phase()
            sh.x4 = sb("x4", [P, TILES, P])
            phase_time_mix(core, io, sh)
            core.end_phase()
            phase_channel_mix(core, io, sh)
            core.end_phase()
        phase_moe(core, io, "moe2", ln_moe2, out=io["out"])
        core.end_phase()
        core.end_phase()


def rope_tables():
    head, half = 8, 4
    inv_freq = 1.0 / 10000.0 ** (np.arange(0, head, 2, dtype=np.float32) / np.float32(head))
    angle = np.arange(SEQ, dtype=np.float32)[:, None] * inv_freq[None, :].astype(np.float32)
    cos, sin = np.cos(angle), np.sin(angle)
    cos = np.tile(np.concatenate([cos, cos], 1), (1, P // head))
    sin = np.tile(np.concatenate([-sin, sin], 1), (1, P // head))
    t = np.stack([cos, sin]).astype(np.float32)
    return np.ascontiguousarray(t.reshape(2, TPS, P, P).transpose(2, 0, 1, 3))


def kernel(**inputs):
    import concourse.bacc as bacc
    from concourse.bass_utils import run_bass_kernel_spmd

    a = {k: np.asarray(v) for k, v in inputs.items()}
    A, B, M = "L0_attn_a_", "L0_attn_b_", "L0_ffn_"

    def column(v):
        return v.reshape(-1, P).T

    def rows(v):
        return np.broadcast_to(v[None, :], (P, v.size))

    w_in = a[A + "W_in"]
    partner = np.arange(P) ^ 4
    wz = a[A + "W_zxbcdt"].T
    cw = a[A + "conv_w"].reshape(CONV_BLOCKS, P, TAPS).transpose(1, 0, 2).reshape(P, -1)
    cols = np.concatenate([
        column(a[A + "norm_pre_w"]), column(a[A + "norm_gated_w"]), column(a[A + "conv_b"]), cw,
        *[column(a[B + n]) for n in ("ln1_w", "ln1_b", "ln2_w", "ln2_b", "time_decay", "time_first",
                                     "tmk", "tmv", "tmr", "cmk", "cmr")],
        *[rows(a[A + n]) for n in ("dt_bias", "A_log", "D_param")],
        rows(a[B + "ln0_w"]), rows(a[B + "ln0_b"])], axis=1)
    def branch(gate, up, down):
        return np.concatenate([gate, up, down.reshape(FBLK, P, P).transpose(1, 0, 2).reshape(P, FFN)], 1)

    moe = [branch(a[M + "ws_gate"], a[M + "ws_up"], a[M + "ws_down"])]
    moe += [branch(a[M + "w_gate"][e], a[M + "w_up"][e], a[M + "w_down"][e]) for e in range(EXPERTS)]
    arrays = {
        "x": a[A + "x"],
        "wq": np.concatenate([w_in[:P].T, w_in[partner].T], 1),
        "wzx": np.concatenate([wz[:, :INNER], wz[:, -HEADS:], wz[:, INNER:INNER + CONV_BLOCKS * P]], 1),
        "rope": rope_tables(),
        "cols": cols,
        "w_out": a[A + "W_out"].T.reshape(2, P, P).transpose(1, 0, 2),
        "router_w": a[M + "gate_w"],
        "moe": np.stack(moe),
        "w_rkvo": np.stack([a[B + n].T for n in ("Wk", "Wv", "Wr", "Wo")], 1),
        "w_fk": a[B + "Wfk"].T,
        "w_fr": a[B + "Wfr"].T,
        "w_fv": a[B + "Wfv"].T.reshape(HIDDEN // P, P, P).transpose(1, 0, 2),
    }
    arrays = {k: np.ascontiguousarray(v) for k, v in arrays.items()}
    nc = bacc.Bacc("TRN2", target_bir_lowering=False, num_devices=1)
    io = {k: nc.dram_tensor("in_" + k, v.shape, F32, kind="ExternalInput").ap() for k, v in arrays.items()}
    io["out"] = nc.dram_tensor("out", (SEQS, SEQ, P), F32, kind="ExternalOutput").ap()
    program(nc, io)
    r = run_bass_kernel_spmd(nc, [{"in_" + k: v for k, v in arrays.items()}], core_ids=[0])
    return r.results[0]["out"]
```

```python
from contextlib import ExitStack

import numpy as np

import concourse.bass as bass
from concourse import mybir

P = 128
SEQS, SEQ = 4, 512
TPS = SEQ // P
TILES = SEQS * TPS
TOKENS = SEQS * SEQ
INNER = 256
HEADS, HDIM = 4, 64
CONV_BLOCKS = 4
TAPS = 4
ZDT = INNER + HEADS
XTOK = INNER + P
EXPERTS = 8
BRANCHES = EXPERTS + 1
FFN = 256
FBLK = FFN // P
MOE_RING = 3
HIDDEN = 512
EPS = 1e-5

X_SCALE, W_SCALE, H_SCALE = 2.0 ** 11, 2.0 ** 8, 2.0 ** 4
GU_UNSCALE = 1.0 / (X_SCALE * W_SCALE)
DOWN_UNSCALE = 1.0 / (H_SCALE * W_SCALE)

ALU = mybir.AluOpType
ACT = mybir.ActivationFunctionType
F32 = mybir.dt.float32
F16 = mybir.dt.float16
AX_X = mybir.AxisListType.X

COLS = {}
for _name, _n in (("norm_pre_w", 1), ("gated_w", 2), ("conv_b", CONV_BLOCKS), ("conv_w", CONV_BLOCKS * TAPS),
                  ("ln1_w", 1), ("ln1_b", 1), ("ln2_w", 1), ("ln2_b", 1), ("decay", 1), ("first", 1),
                  ("tmk", 1), ("tmv", 1), ("tmr", 1), ("cmk", 1), ("cmr", 1),
                  ("dt_bias", HEADS), ("a_log", HEADS), ("d_skip", HEADS), ("ln0_w", P), ("ln0_b", P)):
    _at = max((b for _, b in COLS.values()), default=0)
    COLS[_name] = (_at, _at + _n)
NCOLS = max(b for _, b in COLS.values())


class Core:

    def __init__(self, nc):
        self.nc = nc
        self.live, self.retired = [], []

    def semaphore(self, name):
        ctx = ExitStack()
        sem = ctx.enter_context(self.nc.semaphore(name))
        self.live.append((sem, ctx))
        return sem

    def clear_retired(self, sp):
        for sem, _ in self.retired:
            sp.sem_clear(sem)

    def end_phase(self):
        for _, ctx in self.retired:
            ctx.close()
        self.retired, self.live = self.live, []


def constants(core, ctx):
    nc = core.nc

    def sb(name, shape, dt=F32):
        return ctx.enter_context(nc.sbuf_tensor(name, shape, dt))

    core.banks = [ctx.enter_context(nc.psum_tensor(f"bank{i}", [P, 512], F32)) for i in range(8)]
    core.x = sb("x", [P, TILES, P])
    core.cols = sb("cols", [P, NCOLS])
    core.ident = sb("ident", [P, P])
    core.causal = sb("causal", [P, P])
    core.after = sb("after", [P, P])
    core.ones = sb("ones", [P, P])
    core.mhalf = sb("mhalf", [P, TILES])
    core.router_w = sb("router_w", [P, EXPERTS])
    core.wsplit = sb("wsplit", [P, BRANCHES, 6, FFN], F16)
    core.moe_w_in = [ctx.enter_context(nc.semaphore(f"moe_w_in{e}")) for e in range(BRANCHES)]
    core.cols_in = ctx.enter_context(nc.semaphore("cols_in"))
    core.consts_ready = ctx.enter_context(nc.semaphore("consts_ready"))


def col(core, name, k=0, n=1):
    a = COLS[name][0] + k
    return core.cols[:, a:a + n]


def phase_mamba_in(core, io, shared):
    nc = core.nc
    with ExitStack() as ctx:
        def sb(name, shape, dt=F32):
            return ctx.enter_context(nc.sbuf_tensor(name, shape, dt))

        def sem(name):
            return core.semaphore("a1_" + name)

        wq = sb("wq", [P, 2 * P])
        wzx = sb("wzx", [P, ZDT + CONV_BLOCKS * P])
        rope = sb("rope", [P, 2, TPS, P])
        norm = shared.norm
        normT = sb("normT", [P, TOKENS])
        turned = sb("turned", [P, 2, 2, 2 * P])
        stats = sb("stats", [P, TILES, 6])
        mv = sb("mv", [P, TILES, 2])
        veps = sb("veps", [P, TILES])
        rstd = sb("rstd", [P, TILES])
        nbias = sb("nbias", [P, TILES])
        ssq = sb("ssq", [P, TILES])
        rms = sb("rms", [P, TILES])
        sq_junk = sb("sq_junk", [P, P])

        x, q, xbc, sz, dt_raw, xtok = core.x, shared.q, shared.xbc, shared.sz, shared.dt_raw, shared.xtok
        xnT_ps, q_ps, hT_ps, conv_ps, z_ps, tok_ps = (
            core.banks[0], core.banks[1:3], core.banks[3], core.banks[4:6], core.banks[6], core.banks[7])

        def tok_bank(i):
            return xnT_ps if i >= TILES - TPS and i % 2 else tok_ps

        x_in = [sem(f"x_in{s}") for s in range(SEQS)]
        wq_in, wzx_in, rope_in = sem("wq_in"), sem("wzx_in"), sem("rope_in")
        veps_ready, xn_ready, xn_turned, xnT_ready = sem("veps"), sem("xn"), sem("xn_turned"), sem("xnT")
        q_made, q_roped, q_ready, ssq_ready = sem("q_made"), sem("q_roped"), sem("q_ready"), sem("ssq")
        h0_ready, h_ready, h_turned, hT_ready = sem("h0"), sem("h"), sem("h_turned"), sem("hT")
        rstd_ready, rms_ready, xq_ready = sem("rstd"), sem("rms"), sem("xq")
        conv_in, tap0_done, conv_done, conv_act = sem("conv_in"), sem("tap0"), sem("conv_done"), sem("conv_act")
        z_made, z_done, tok_turned, tok_ready = sem("z_made"), sem("z_done"), sem("tok_turned"), sem("tok")
        dve_step, pool_step, act_step = sem("dve_step"), sem("pool_step"), sem("act_step")

        block = ctx.enter_context(nc.Block())

        @block.sync
        def _(sp):
            core.clear_retired(sp)
            xr = io["x"].rearrange("s (c p) d -> s p c d", p=P)
            for s in range(SEQS):
                sp.dma_start(x[:, TPS * s:TPS * (s + 1), :], xr[s]).then_inc(x_in[s], 16)
                if s == 0:
                    sp.dma_start(wq[:], io["wq"]).then_inc(wq_in, 16)
                    sp.dma_start(rope[:], io["rope"]).then_inc(rope_in, 16)
                    sp.dma_start(core.cols[:], io["cols"]).then_inc(core.cols_in, 16)
            sp.dma_start(wzx[:], io["wzx"]).then_inc(wzx_in, 16)
            sp.dma_start(shared.w_out[:], io["w_out"]).then_inc(shared.w_out_in, 16)
            sp.dma_start(core.router_w[:], io["router_w"]).then_inc(shared.w_out_in, 16)
            for e in range(MOE_RING):
                sp.dma_start(shared.moe_raw[:, e], io["moe"][e]).then_inc(core.moe_w_in[e], 16)

        @block.gpsimd
        def _(pool):
            steps = [0]

            def link(ins):
                steps[0] += 1
                ins.then_inc(pool_step, 1)
                pool.wait_ge(pool_step, steps[0])

            nc.gpsimd.memset(core.mhalf[:], -0.5).then_inc(core.consts_ready, 1)
            nc.gpsimd.memset(core.ones[:], 1.0).then_inc(core.consts_ready, 1)
            nc.gpsimd.memset(core.ident[:], 0.0).then_inc(core.consts_ready, 1)
            pool.wait_ge(core.consts_ready, 3)
            nc.gpsimd.affine_select(out=core.ident[:], in_=core.ident[:], compare_op=ALU.not_equal, fill=1.0,
                                    base=0, pattern=[[-1, P]], channel_multiplier=1).then_inc(core.consts_ready, 1)
            nc.gpsimd.affine_select(out=core.causal[:], in_=core.ones[:], compare_op=ALU.is_ge, fill=0.0,
                                    base=0, pattern=[[1, P]], channel_multiplier=-1).then_inc(core.consts_ready, 1)
            nc.gpsimd.affine_select(out=core.after[:], in_=core.ones[:], compare_op=ALU.is_gt, fill=0.0,
                                    base=0, pattern=[[-1, P]], channel_multiplier=1).then_inc(core.consts_ready, 1)

            def rsqrt_var(s):
                a, b = TPS * s, TPS * (s + 1)
                pool.wait_ge(veps_ready, s + 1)
                link(nc.gpsimd.tensor_tensor(rstd[:, a:b], veps[:, a:b], core.mhalf[:, a:b], ALU.pow))
                link(nc.gpsimd.tensor_tensor(nbias[:, a:b], mv[:, a:b, 0], rstd[:, a:b], ALU.mult))
                nc.gpsimd.tensor_scalar(nbias[:, a:b], nbias[:, a:b], -1.0, 0.0, ALU.mult,
                                        ALU.add).then_inc(rstd_ready, 1)

            def add_q(s):
                for pair in range(2):
                    n = 2 * s + pair
                    pool.wait_ge(q_roped, n + 1)
                    nc.gpsimd.tensor_tensor(
                        q[:, TPS * s + 2 * pair:TPS * s + 2 * pair + 2, :],
                        turned[:, pair, 0, :].rearrange("p (c d) -> p c d", c=2),
                        turned[:, pair, 1, :].rearrange("p (c d) -> p c d", c=2), ALU.add).then_inc(q_ready, 1)

            def rms_norm(s):
                a, b = TPS * s, TPS * (s + 1)
                pool.wait_ge(ssq_ready, TPS * (s + 1))
                link(nc.gpsimd.tensor_scalar(ssq[:, a:b], ssq[:, a:b], 1.0 / P, EPS, ALU.mult, ALU.add))
                power = nc.gpsimd.tensor_tensor(rms[:, a:b], ssq[:, a:b], core.mhalf[:, a:b], ALU.pow)
                if s == 0:
                    power.then_inc(rms_ready, 1)
                else:
                    link(power)
                    for i in range(a, b):
                        nc.gpsimd.tensor_scalar(norm[:, i, :], q[:, i, :], rms[:, i:i + 1], 0.0,
                                                ALU.mult, ALU.add).then_inc(h_ready, 1)

            def add_residuals(s):
                if s == 0:
                    pool.wait_ge(h0_ready, TPS)
                else:
                    pool.wait_ge(h_ready, TPS * s)
                nc.gpsimd.tensor_tensor(q[:, of_seq(s)], q[:, of_seq(s)], x[:, of_seq(s)], ALU.add).then_inc(xq_ready, 1)

            for s in range(3):
                rsqrt_var(s)
            add_q(0)
            rms_norm(0)
            rsqrt_var(3)
            for s in range(1, SEQS):
                add_q(s)
                rms_norm(s)
                if s == 1:
                    add_residuals(0)
                if s == SEQS - 1:
                    for done in range(1, SEQS):
                        add_residuals(done)

        @block.vector
        def _(dve):
            steps = [0]

            def link(ins):
                steps[0] += 1
                ins.then_inc(dve_step, 1)
                dve.wait_ge(dve_step, steps[0])

            def statistics(s):
                dve.wait_ge(x_in[s], 16)
                for i in range(TPS * s, TPS * (s + 1)):
                    last = nc.vector.bn_stats(stats[:, i, :], x[:, i, :])
                link(last)
                for i in range(TPS * s, TPS * (s + 1)):
                    last = nc.vector.bn_aggr(mv[:, i, :], stats[:, i, :])
                link(last)
                nc.vector.tensor_scalar(veps[:, TPS * s:TPS * (s + 1)], mv[:, TPS * s:TPS * (s + 1), 1], EPS, None,
                                        ALU.add).then_inc(veps_ready, 1)

            def normalise(s):
                dve.wait_ge(rstd_ready, s + 1)
                for i in range(TPS * s, TPS * (s + 1)):
                    nc.vector.tensor_scalar(norm[:, i, :], x[:, i, :], rstd[:, i:i + 1], nbias[:, i:i + 1],
                                            ALU.mult, ALU.add).then_inc(xn_ready, 1)

            def rms_norm_first():
                dve.wait_ge(rms_ready, 1)
                for i in range(TPS):
                    nc.vector.tensor_scalar(norm[:, i, :], q[:, i, :], rms[:, i:i + 1], None,
                                            ALU.mult).then_inc(h0_ready, 1)

            def turn_q(s, pair):
                n = 2 * s + pair
                dve.wait_ge(q_made, n + 1)
                if s > 0:
                    dve.wait_ge(q_ready, n - 1)
                src = q_ps[pair][:, :].rearrange("p (c w d) -> p c w d", c=2, w=2)
                for w in range(2):
                    last = nc.vector.tensor_tensor(
                        turned[:, pair, w, :].rearrange("p (c d) -> p c d", c=2), src[:, :, w, :],
                        rope[:, w, 2 * pair:2 * pair + 2, :], ALU.mult)
                last.then_inc(q_roped, 1)

            def taps(s, b):
                t0, t1 = SEQ * s, SEQ * (s + 1)
                dve.wait_ge(tap0_done, CONV_BLOCKS * s + b + 1)
                for back in range(1, TAPS):
                    ins = nc.vector.scalar_tensor_tensor(
                        xbc[:, b, t0 + back:t1], conv_ps[b % 2][:, 0:SEQ - back],
                        col(core, "conv_w", TAPS * b + TAPS - 1 - back), xbc[:, b, t0 + back:t1],
                        ALU.mult, ALU.add)
                    if back < TAPS - 1:
                        link(ins)
                ins.then_inc(conv_done, 1)

            statistics(0)
            statistics(1)
            normalise(0)
            statistics(2)
            normalise(1)
            statistics(3)
            normalise(2)
            dve.wait_ge(rope_in, 16)
            for pair in range(2):
                turn_q(0, pair)
            for pair in range(2):
                turn_q(1, pair)
            rms_norm_first()
            normalise(3)
            for s in range(SEQS):
                for b in range(CONV_BLOCKS):
                    taps(s, b)
                    if s == 0 and b >= 2:
                        turn_q(2, b - 2)
                    if s == 1 and 1 <= b <= 2:
                        turn_q(3, b - 1)

        @block.scalar
        def _(act):
            def turn_out(i):
                act.wait_ge(tok_turned, i + 1)
                nc.scalar.copy(xtok[:, i, :], tok_bank(i)[:, 0:XTOK]).then_inc(tok_ready, 1)

            def copy_xnT(s):
                act.wait_ge(xn_turned, s + 1)
                nc.scalar.copy(normT[:, SEQ * s:SEQ * (s + 1)], xnT_ps[:, :]).then_inc(xnT_ready, 1)

            def copy_hT(s):
                act.wait_ge(h_turned, s + 1)
                nc.scalar.activation(normT[:, SEQ * s:SEQ * (s + 1)], hT_ps[:, :], ACT.Identity,
                                     scale=col(core, "norm_pre_w")).then_inc(hT_ready, 1)

            def square_q(i):
                act.wait_ge(q_ready, i // 2 + 1)
                if i:
                    act.wait_ge(ssq_ready, i)
                nc.scalar.activation(sq_junk[:], q[:, i, :], ACT.Square, accum_out=ssq[:, i:i + 1]).then_inc(ssq_ready, 1)

            def tap0(s, b):
                act.wait_ge(conv_in, CONV_BLOCKS * s + b + 1)
                nc.scalar.activation(xbc[:, b, SEQ * s:SEQ * (s + 1)], conv_ps[b % 2][:, :], ACT.Identity,
                                     bias=col(core, "conv_b", b),
                                     scale=col(core, "conv_w", TAPS * b + TAPS - 1)).then_inc(tap0_done, 1)

            def z_dt(i):
                act.wait_ge(z_made, i + 1)
                nc.scalar.activation(sz[:, i, :], z_ps[:, 0:INNER], ACT.Silu)
                nc.scalar.copy(dt_raw[:, i, :], z_ps[:, INNER:ZDT]).then_inc(z_done, 1)

            def conv_silu(n):
                s, b = n // CONV_BLOCKS, n % CONV_BLOCKS
                tok = slice(SEQ * s, SEQ * (s + 1))
                act.wait_ge(conv_done, n + 1)
                nc.scalar.activation(xbc[:, b, tok], xbc[:, b, tok], ACT.Silu).then_inc(conv_act, 1)

            copy_xnT(0)
            copy_xnT(1)
            for i in range(TPS):
                square_q(i)
            act.wait_ge(core.cols_in, 16)
            copy_hT(0)
            for s in range(SEQS):
                for b in range(CONV_BLOCKS):
                    n = CONV_BLOCKS * s + b
                    tap0(s, b)
                    if n:
                        conv_silu(n - 1)
                    z_dt(TPS * s + b)
                    if s == 0 and b in (0, 2):
                        copy_xnT(2 + b // 2)
                    if s + 1 < SEQS and b < 2:
                        square_q(TPS * (s + 1) + 2 * b)
                        square_q(TPS * (s + 1) + 2 * b + 1)
                    if s + 1 < SEQS and b == 3:
                        copy_hT(s + 1)
                    if s:
                        turn_out(TPS * (s - 1) + b)
            for c in range(TPS):
                if c == 2:
                    conv_silu(CONV_BLOCKS * SEQS - 1)
                turn_out(TPS * (SEQS - 1) + c)

        @block.tensor
        def _(pe):
            pe.wait_ge(core.consts_ready, 6)

            def turn_tiles(bank, normed, done, free, turned, s):
                for c in range(TPS):
                    pe.wait_ge(normed, done + c + 1)
                    if c == 0 and s:
                        pe.wait_ge(free, s)
                    ins = nc.tensor.transpose(bank[:, P * c:P * (c + 1)], norm[:, TPS * s + c, :], core.ident[:])
                ins.then_inc(turned, 1)

            def project_q(s):
                pe.wait_ge(xnT_ready, s + 1)
                if s == 0:
                    pe.wait_ge(wq_in, 16)
                for c in range(TPS):
                    if c % 2 == 0 and s > 0:
                        pe.wait_ge(q_roped, 2 * s + c // 2 - 1)
                    ins = nc.tensor.matmul(q_ps[c // 2][:, 256 * (c % 2):256 * (c % 2) + 256],
                                           normT[:, SEQ * s + P * c:SEQ * s + P * (c + 1)], wq[:],
                                           start=True, stop=True)
                    if c % 2:
                        ins.then_inc(q_made, 1)

            def project_in(s, b):
                n = CONV_BLOCKS * s + b
                if n >= 2:
                    pe.wait_ge(conv_done, n - 1)
                nc.tensor.matmul(conv_ps[b % 2][:, :], wzx[:, ZDT + P * b:ZDT + P * (b + 1)],
                                 normT[:, SEQ * s:SEQ * (s + 1)], start=True, stop=True).then_inc(conv_in, 1)
                i = TPS * s + b
                if i:
                    pe.wait_ge(z_done, i)
                nc.tensor.matmul(z_ps[:, 0:ZDT], normT[:, P * i:P * (i + 1)], wzx[:, 0:ZDT],
                                 start=True, stop=True).then_inc(z_made, 1)

            def turn_tok(s, c):
                i = TPS * s + c
                if c == 0:
                    pe.wait_ge(conv_act, CONV_BLOCKS * s + 3)
                if i:
                    pe.wait_ge(tok_ready, i if i <= TILES - TPS else i - 1)
                for b in range(3):
                    ins = nc.tensor.transpose(tok_bank(i)[:, P * b:P * (b + 1)], xbc[:, b, P * i:P * (i + 1)],
                                              core.ident[:])
                ins.then_inc(tok_turned, 1)

            def turn_x(s):
                turn_tiles(xnT_ps, xn_ready, TPS * s, xnT_ready, xn_turned, s)

            def turn_h(s):
                if s == 0:
                    turn_tiles(hT_ps, h0_ready, 0, hT_ready, h_turned, s)
                else:
                    turn_tiles(hT_ps, h_ready, TPS * (s - 1), hT_ready, h_turned, s)

            turn_x(0)
            project_q(0)
            turn_x(1)
            project_q(1)
            turn_h(0)
            for s in range(SEQS):
                pe.wait_ge(hT_ready, s + 1)
                if s == 0:
                    pe.wait_ge(wzx_in, 16)
                for b in range(CONV_BLOCKS):
                    project_in(s, b)
                    if s:
                        turn_tok(s - 1, b)
                    if s == 0 and b in (0, 2):
                        turn_x(2 + b // 2)
                    if s == 0 and b == 1:
                        project_q(2)
                    if s == 1 and b == 0:
                        project_q(3)
                    if s + 1 < SEQS and b == 2:
                        turn_h(s + 1)
            for c in range(TPS):
                turn_tok(SEQS - 1, c)


def phase_ssd(core, io, shared):
    nc = core.nc
    units = [(c, s) for c in range(TPS) for s in range(SEQS)]
    NU = len(units)
    LAST_CHUNK = NU - SEQS
    CHUNK_STATS = (2 * SEQS + 3, 3 * SEQS + 3, LAST_CHUNK + 6)
    WRING = 4
    with ExitStack() as ctx:
        def sb(name, shape, dt=F32):
            return ctx.enter_context(nc.sbuf_tensor(name, shape, dt))

        def sem(name):
            return core.semaphore("a2_" + name)

        x, q, xbc, sz, dt_raw, xtok = core.x, shared.q, shared.xbc, shared.sz, shared.dt_raw, shared.xtok
        v = sb("dt_in", [P, TILES, HEADS])
        e = sb("dt_exp", [P, TILES, HEADS])
        dt = sb("dt", [P, TILES, HEADS])
        ea = sb("ea", [P, HEADS])
        adt = sb("adt", [P, TILES, HEADS])
        decays = sb("decays", [P, 3, TILES, HEADS])
        wdec = sb("wdec", [P, TILES, HEADS])
        dx = sb("dx", [P, WRING, INNER])
        seg_l = sb("seg_l", [P, 2, HEADS, P])
        xdt = sb("xdt", [P, WRING, INNER])
        xw = sb("xw", [P, WRING, INNER])
        expo = sb("expo", [P, 2, HEADS, P])
        gm = sb("gm", [P, 2, P])
        mix = sb("mix", [P, 2, HEADS, P])
        state = sb("state", [P, SEQS, INNER])
        y_off = sb("y_off", [P, 2, INNER])
        y = sb("y", [P, 2, INNER])
        g = sb("g", [P, 2, INNER])
        g_junk = sb("g_junk", [P, INNER])
        ssq = sb("ssq2", [P, TILES])
        ms = sb("ms2", [P, TILES])
        rms = sb("rms2", [P, TILES])
        gT = sb("gT", [P, 2, 2, P])

        g_ps, seg_ps, y_ps, st_ps, out_ps = (core.banks[0:2], core.banks[2:4], core.banks[4:6], core.banks[6],
                                             core.banks[7])

        dt_abs, dt_act, adt_ready, cum_made, decay_ready, w_ready = (
            sem("dt_abs"), sem("dt_act"), sem("adt"), sem("cum"), sem("decay"), sem("w"))
        segl_ready, xdt_ready, xw_ready = sem("segl"), sem("xdt"), sem("xw")
        cb_made, seg_made, expo_ready, gm_ready, mix_ready = sem("cb"), sem("seg"), sem("expo"), sem("gm"), sem("mix")
        y_made, st_made, st_ready, y_ready, g_ready, ssq_ready = (
            sem("y_made"), sem("st_made"), sem("st"), sem("y"), sem("g"), sem("ssq"))
        g_turned, gT_ready, out_made, rms_ready, x_ready = sem("g_turned"), sem("gT"), sem("out"), sem("rms"), sem("x")
        dve_step, pool_step, act_step = sem("dve_step"), sem("pool_step"), sem("act_step")
        stats_ready, veps_ready = sem("stats"), sem("veps")
        rstd_ready, normed, x_turned, normT_ready, hi_ready, lo_ready = (
            sem("rstd"), sem("normed"), sem("x_turned"), sem("normT"), sem("x_hi"), sem("x_lo"))

        def heads(ap):
            return ap.rearrange("p (h d) -> p h d", h=HEADS)

        def per_head(ap):
            return ap.unsqueeze(2).broadcast_to([P, HEADS, HDIM])

        moe_hi, moe_lo = sem("moe_hi"), sem("moe_lo")

        def moe_pair(e, half):
            return core.wsplit[:, e].rearrange("p (m f) n -> p m f n", f=2)[:, :, half, :]

        block = ctx.enter_context(nc.Block())

        @block.sync
        def _(sp):
            core.clear_retired(sp)
            for e in range(MOE_RING, BRANCHES):
                sp.wait_ge(moe_lo, e - MOE_RING + 1)
                sp.dma_start(shared.moe_raw[:, e % MOE_RING], io["moe"][e]).then_inc(core.moe_w_in[e], 16)

        @block.vector
        def _(dve):
            steps = [0]

            def link(ins):
                steps[0] += 1
                ins.then_inc(dve_step, 1)
                dve.wait_ge(dve_step, steps[0])

            def mark(ins):
                steps[0] += 1
                ins.then_inc(dve_step, 1)
                return steps[0]

            def split_low(e):
                dve.wait_ge(moe_hi, e + 1)
                raw = shared.moe_raw[:, e % MOE_RING].rearrange("p (m n) -> p m n", m=3)
                nc.vector.scalar_tensor_tensor(moe_pair(e, 1), raw, W_SCALE, moe_pair(e, 0), ALU.mult,
                                               ALU.subtract).then_inc(moe_lo, 1)

            link(nc.vector.tensor_tensor(v[:], dt_raw[:], col(core, "dt_bias", 0, HEADS).unsqueeze(1)
                                         .broadcast_to([P, TILES, HEADS]), ALU.add))
            nc.vector.scalar_tensor_tensor(e[:], v[:], -1.0, v[:], ALU.mult, ALU.min).then_inc(dt_abs, 1)
            dve.wait_ge(dt_act, 3)
            link(nc.vector.scalar_tensor_tensor(dt[:], v[:], 0.0, e[:], ALU.max, ALU.add))
            nc.vector.scalar_tensor_tensor(adt[:], dt[:], -1.0, ea[:].unsqueeze(1).broadcast_to([P, TILES, HEADS]),
                                           ALU.mult, ALU.mult).then_inc(adt_ready, 1)
            dve.wait_ge(decay_ready, 1)
            nc.vector.tensor_tensor(wdec[:], dt[:], decays[:, 1], ALU.mult).then_inc(w_ready, 1)

            def masking(n):
                dve.wait_ge(cb_made, n + 1)
                nc.vector.tensor_tensor(gm[:, n % 2, :], g_ps[n % 2][:, 0:P], core.causal[:],
                                        ALU.mult).then_inc(gm_ready, 1)

            def mixing(n):
                dve.wait_ge(gm_ready, n + 1)
                dve.wait_ge(expo_ready, n + 1)
                if n >= 2:
                    dve.wait_ge(y_made, n - 1)
                nc.vector.tensor_tensor(mix[:, n % 2], expo[:, n % 2],
                                        gm[:, n % 2, :].unsqueeze(1).broadcast_to([P, HEADS, P]),
                                        ALU.mult).then_inc(mix_ready, 1)

            def joining(n):
                c, s = units[n]
                i = TPS * s + c
                ps = y_ps[n % 2]
                if 0 < c < TPS - 1:
                    scaled_state = mark(nc.vector.tensor_tensor(heads(state[:, s, :]), heads(state[:, s, :]),
                                                                per_head(decays[:, 2, i, :]), ALU.mult))
                dve.wait_ge(y_made, n + 1)
                if c:
                    scaled_y = mark(nc.vector.tensor_tensor(heads(y_off[:, n % 2, :]), heads(ps[:, INNER:2 * INNER]),
                                                            per_head(decays[:, 0, i, :]), ALU.mult))
                if c < TPS - 1:
                    dve.wait_ge(st_made, n + 1)
                    if c == 0:
                        nc.vector.tensor_copy(state[:, s, :], st_ps[:, 0:INNER]).then_inc(st_ready, 1)
                    else:
                        dve.wait_ge(dve_step, scaled_state)
                        nc.vector.tensor_tensor(state[:, s, :], state[:, s, :], st_ps[:, 0:INNER],
                                                ALU.add).then_inc(st_ready, 1)
                if n >= 2:
                    dve.wait_ge(g_ready, n - 1)
                if c == 0:
                    nc.vector.tensor_copy(y[:, n % 2, :], ps[:, 0:INNER]).then_inc(y_ready, 1)
                else:
                    dve.wait_ge(dve_step, scaled_y)
                    nc.vector.tensor_tensor(y[:, n % 2, :], y_off[:, n % 2, :], ps[:, 0:INNER],
                                            ALU.add).then_inc(y_ready, 1)

            def closing(n):
                c, s = units[n]
                i = TPS * s + c
                dve.wait_ge(out_made, n + 1)
                dve.wait_ge(rms_ready, n + 1)
                nc.vector.scalar_tensor_tensor(x[:, i, :], out_ps[:, INNER:INNER + P], rms[:, i:i + 1], q[:, i, :],
                                               ALU.mult, ALU.add).then_inc(x_ready, 1)

            def tile_stats(n):
                c, s = units[n]
                i = TPS * s + c
                dve.wait_ge(x_ready, n + 1)
                nc.vector.bn_stats(shared.ln.stats[:, i, :], x[:, i, :]).then_inc(stats_ready, 1)

            def tile_mean(n):
                c, s = units[n]
                i = TPS * s + c
                dve.wait_ge(stats_ready, n + 1)
                ins = nc.vector.bn_aggr(shared.ln.mv[:, i, :], shared.ln.stats[:, i, :])
                if c == TPS - 1:
                    link(ins)
                    nc.vector.tensor_scalar(shared.ln.veps[:, i:i + 1], shared.ln.mv[:, i:i + 1, 1], EPS, None,
                                            ALU.add).then_inc(veps_ready, 1)
                elif s == SEQS - 1:
                    link(ins)
                    nc.vector.tensor_scalar(shared.ln.veps[:, c::TPS], shared.ln.mv[:, c::TPS, 1], EPS, None,
                                            ALU.add).then_inc(veps_ready, 1)

            for step in range(NU + 5):
                if step == NU + 4:
                    dve.wait_ge(hi_ready, 1)
                    nc.vector.tensor_tensor(shared.x_lo[:, 0:SEQ], shared.normT[:, 0:SEQ], shared.x_hi[:, 0:SEQ],
                                            ALU.subtract).then_inc(lo_ready, 1)
                if 1 <= step < NU + 1:
                    mixing(step - 1)
                if step >= 5 and step < NU + 5:
                    closing(step - 5)
                if 2 <= step < NU + 2:
                    joining(step - 2)
                if step < NU:
                    masking(step)
                if 3 <= step < BRANCHES + 3:
                    split_low(step - 3)
                if 5 <= step < NU + 4:
                    tile_stats(step - 5)
                if 6 <= step <= LAST_CHUNK + 4:
                    tile_mean(step - 6)
                if step >= LAST_CHUNK + 5 and step < NU + 4:
                    if step == LAST_CHUNK + 5:
                        tile_mean(step - 6)
                    tile_mean(step - 5)
                if step == NU + 3:
                    dve.wait_ge(rstd_ready, 1)
                    ln_apply(nc.vector, shared.ln, x, shared.norm, 0, normed)

        @block.scalar
        def _(act):
            act.wait_ge(dt_abs, 1)
            nc.scalar.activation(e[:], e[:], ACT.Exp).then_inc(dt_act, 1)
            nc.scalar.activation(ea[:], col(core, "a_log", 0, HEADS), ACT.Exp).then_inc(dt_act, 1)
            act.wait_ge(dt_act, 2)
            nc.scalar.activation(e[:], e[:], ACT.Ln, bias=1.0).then_inc(dt_act, 1)
            nc.scalar.activation(g_junk[:, 0:1], core.ident[:, 0:1], ACT.Exp).then_inc(act_step, 1)
            act.wait_ge(act_step, 1)
            act.wait_ge(adt_ready, 1)

            def segments(n):
                c, s = units[n]
                i = TPS * s + c
                if n >= 2:
                    act.wait_ge(seg_made, n - 1)
                for h in range(HEADS):
                    ins = nc.scalar.mul(seg_l[:, n % 2, h, :], core.after[:], adt[:, i, h:h + 1])
                ins.then_inc(segl_ready, 1)

            segments(0)
            act.wait_ge(cum_made, 1)
            nc.scalar.activation(decays[:].rearrange("p a i h -> p (a i h)"), g_ps[1][:, 0:3 * TILES * HEADS],
                                 ACT.Exp).then_inc(decay_ready, 1)
            for step in range(NU + 5):
                if step + 1 < NU:
                    segments(step + 1)
                if 4 <= step < NU + 4:
                    n = step - 4
                    c, s = units[n]
                    i = TPS * s + c
                    act.wait_ge(g_ready, n + 1)
                    if n:
                        act.wait_ge(ssq_ready, n)
                    nc.scalar.activation(g_junk[:], g[:, n % 2, :], ACT.Square,
                                         accum_out=ssq[:, i:i + 1]).then_inc(ssq_ready, 1)
                if step < NU:
                    n = step
                    act.wait_ge(seg_made, n + 1)
                    if n >= 2:
                        act.wait_ge(mix_ready, n - 1)
                    nc.scalar.activation(expo[:, n % 2].rearrange("p h l -> p (h l)"), seg_ps[n % 2][:, :],
                                         ACT.Exp).then_inc(expo_ready, 1)
                if 4 <= step < NU + 4:
                    n = step - 4
                    act.wait_ge(g_turned, n + 1)
                    if n >= 2:
                        act.wait_ge(out_made, n - 1)
                    for k in range(2):
                        ins = nc.scalar.mul(gT[:, n % 2, k, :], out_ps[:, P * k:P * (k + 1)],
                                            col(core, "gated_w", k))
                    ins.then_inc(gT_ready, 1)
                if step == NU + 3:
                    act.wait_ge(x_turned, 1)
                    nc.scalar.mul(shared.normT[:, 0:SEQ], g_ps[0][:, :], X_SCALE).then_inc(normT_ready, 1)
                    act.wait_ge(normT_ready, 1)
                    nc.scalar.copy(shared.x_hi[:, 0:SEQ], shared.normT[:, 0:SEQ]).then_inc(hi_ready, 1)
                if 2 <= step < BRANCHES + 2:
                    act.wait_ge(core.moe_w_in[step - 2], 16)
                    nc.scalar.mul(moe_pair(step - 2, 0), shared.moe_raw[:, (step - 2) % MOE_RING]
                                  .rearrange("p (m n) -> p m n", m=3), W_SCALE).then_inc(moe_hi, 1)

        @block.gpsimd
        def _(pool):
            steps = [0]

            def link(ins):
                steps[0] += 1
                ins.then_inc(pool_step, 1)
                pool.wait_ge(pool_step, steps[0])

            def weighing(n):
                c, s = units[n]
                i = TPS * s + c
                if n >= WRING:
                    pool.wait_ge(y_made, n - WRING + 1)
                nc.gpsimd.tensor_tensor(heads(dx[:, n % WRING, :]), heads(xtok[:, i, 0:INNER]),
                                        per_head(col(core, "d_skip", 0, HEADS)), ALU.mult)
                nc.gpsimd.tensor_tensor(heads(xdt[:, n % WRING, :]), heads(xtok[:, i, 0:INNER]), per_head(dt[:, i, :]),
                                        ALU.mult).then_inc(xdt_ready, 1)
                if c < TPS - 1:
                    if n == 0:
                        pool.wait_ge(w_ready, 1)
                    if n >= WRING:
                        pool.wait_ge(st_made, n - WRING + 1)
                    nc.gpsimd.tensor_tensor(heads(xw[:, n % WRING, :]), heads(xtok[:, i, 0:INNER]),
                                            per_head(wdec[:, i, :]), ALU.mult).then_inc(xw_ready, 1)

            pool.wait_ge(adt_ready, 1)
            weighing(0)
            weighing(1)
            for step in range(NU + 5):
                if 3 <= step < NU + 3:
                    n = step - 3
                    c, s = units[n]
                    i = TPS * s + c
                    pool.wait_ge(y_ready, n + 1)
                    if n >= 2:
                        pool.wait_ge(ssq_ready, n - 1)
                        pool.wait_ge(g_turned, n - 1)
                    nc.gpsimd.tensor_tensor(g[:, n % 2, :], y[:, n % 2, :], sz[:, i, :], ALU.mult).then_inc(g_ready, 1)
                if step + 2 < NU:
                    weighing(step + 2)
                if 4 <= step < NU + 4:
                    n = step - 4
                    c, s = units[n]
                    i = TPS * s + c
                    pool.wait_ge(ssq_ready, n + 1)
                    link(nc.gpsimd.tensor_scalar(ms[:, i:i + 1], ssq[:, i:i + 1], 1.0 / INNER, EPS, ALU.mult, ALU.add))
                    nc.gpsimd.tensor_tensor(rms[:, i:i + 1], ms[:, i:i + 1], core.mhalf[:, 0:1],
                                            ALU.pow).then_inc(rms_ready, 1)
                if step in CHUNK_STATS:
                    c = CHUNK_STATS.index(step)
                    pool.wait_ge(veps_ready, c + 1)
                    ln_rstd(nc, core, link, shared.ln, slice(c, None, TPS))
                if step >= LAST_CHUNK + 6:
                    s = step - LAST_CHUNK - 6
                    pool.wait_ge(veps_ready, TPS + s)
                    i = TPS * (s + 1) - 1
                    ln_rstd(nc, core, link, shared.ln, slice(i, i + 1), rstd_ready if s == 0 else None)

        @block.tensor
        def _(pe):
            pe.wait_ge(adt_ready, 1)
            flat = adt[:].rearrange("p i h -> p (i h)")
            for k, m in enumerate((core.causal, core.after, core.ones)):
                ins = nc.tensor.matmul(g_ps[1][:, 64 * k:64 * (k + 1)], m[:], flat, start=True, stop=True)
            ins.then_inc(cum_made, 1)

            def chunk(n):
                c, s = units[n]
                i = TPS * s + c
                tok = slice(P * i, P * (i + 1))
                if n >= 2:
                    pe.wait_ge(gm_ready, n - 1)
                if n == 1:
                    pe.wait_ge(decay_ready, 1)
                nc.tensor.matmul(g_ps[n % 2][:, 0:P], xbc[:, 2, tok], xbc[:, 3, tok],
                                 start=True, stop=True).then_inc(cb_made, 1)
                pe.wait_ge(segl_ready, n + 1)
                if n >= 2:
                    pe.wait_ge(expo_ready, n - 1)
                for h in range(HEADS):
                    ins = nc.tensor.matmul(seg_ps[n % 2][:, P * h:P * (h + 1)], seg_l[:, n % 2, h, :],
                                           core.causal[:], start=True, stop=True)
                ins.then_inc(seg_made, 1)

            def output(n):
                c, s = units[n]
                i = TPS * s + c
                ps = y_ps[n % 2]
                if n >= 2:
                    pe.wait_ge(y_ready, n - 1)
                if c:
                    pe.wait_ge(st_ready, n - SEQS + 1)
                    nc.tensor.matmul(ps[:, INNER:2 * INNER], xbc[:, 3, P * i:P * (i + 1)], state[:, s, :],
                                     start=True, stop=True)
                pe.wait_ge(xdt_ready, n + 1)
                nc.tensor.matmul(ps[:, 0:INNER], core.ident[:], dx[:, n % WRING, :], start=True, stop=False)
                pe.wait_ge(mix_ready, n + 1)
                for h in range(HEADS):
                    dst = ps[:, HDIM * h:HDIM * (h + 1)]
                    ins = nc.tensor.matmul(dst, mix[:, n % 2, h, :], xdt[:, n % WRING, HDIM * h:HDIM * (h + 1)],
                                           start=False, stop=h == HEADS - 1)
                ins.then_inc(y_made, 1)
                if c < TPS - 1:
                    pe.wait_ge(xw_ready, n + 1)
                    if n:
                        pe.wait_ge(st_ready, n)
                    nc.tensor.matmul(st_ps[:, 0:INNER], xtok[:, i, INNER:XTOK], xw[:, n % WRING, :],
                                     start=True, stop=True).then_inc(st_made, 1)

            def turn(n):
                pe.wait_ge(g_ready, n + 1)
                if n:
                    pe.wait_ge(x_ready, n)
                for k in range(2):
                    ins = nc.tensor.transpose(out_ps[:, P * k:P * (k + 1)], g[:, n % 2, P * k:P * (k + 1)],
                                              core.ident[:])
                ins.then_inc(g_turned, 1)

            def project(n):
                pe.wait_ge(gT_ready, n + 1)
                if n == 0:
                    pe.wait_ge(shared.w_out_in, 32)
                for k in range(2):
                    ins = nc.tensor.matmul(out_ps[:, INNER:INNER + P], gT[:, n % 2, k, :], shared.w_out[:, k, :],
                                           start=k == 0, stop=k == 1)
                ins.then_inc(out_made, 1)

            for step in range(NU + 5):
                if 5 <= step < NU + 5:
                    project(step - 5)
                if step < NU:
                    chunk(step)
                if 4 <= step < NU + 4:
                    turn(step - 4)
                if 1 <= step < NU + 1:
                    output(step - 1)
                if step == NU + 3:
                    for c in range(TPS):
                        pe.wait_ge(normed, c + 1)
                        ins = nc.tensor.transpose(g_ps[0][:, P * c:P * (c + 1)], shared.norm[:, c, :], core.ident[:])
                    ins.then_inc(x_turned, 1)


class LayerNorm:

    def __init__(self, nc, ctx, name):
        def sb(part, shape):
            return ctx.enter_context(nc.sbuf_tensor(f"{name}_{part}", shape, F32))

        self.stats = sb("stats", [P, TILES, 6])
        self.mv = sb("mv", [P, TILES, 2])
        self.veps = sb("veps", [P, TILES])
        self.rstd = sb("rstd", [P, TILES])
        self.nbias = sb("nbias", [P, TILES])


def ln_stats(nc, link, ln, x, s, veps_ready):
    a, b = TPS * s, TPS * (s + 1)
    for i in range(a, b):
        last = nc.vector.bn_stats(ln.stats[:, i, :], x[:, i, :])
    link(last)
    for i in range(a, b):
        last = nc.vector.bn_aggr(ln.mv[:, i, :], ln.stats[:, i, :])
    link(last)
    nc.vector.tensor_scalar(ln.veps[:, a:b], ln.mv[:, a:b, 1], EPS, None, ALU.add).then_inc(veps_ready, 1)


def ln_double_stats(nc, link, ln, v_eps, x, s, veps_ready):
    a, b = TPS * s, TPS * (s + 1)
    for i in range(a, b):
        last = nc.vector.bn_stats(ln.stats[:, i, :], x[:, i, :])
    link(last)
    for i in range(a, b):
        last = nc.vector.bn_aggr(ln.mv[:, i, :], ln.stats[:, i, :])
    link(last)
    link(nc.vector.tensor_scalar(v_eps[:, a:b], ln.mv[:, a:b, 1], EPS, EPS, ALU.add, ALU.mult))
    nc.vector.tensor_tensor(ln.veps[:, a:b], v_eps[:, a:b], ln.mv[:, a:b, 1], ALU.add).then_inc(veps_ready, 1)


def ln_rstd(nc, core, link, ln, tiles, ready=None):
    link(nc.gpsimd.tensor_tensor(ln.rstd[:, tiles], ln.veps[:, tiles], core.mhalf[:, tiles], ALU.pow))
    link(nc.gpsimd.tensor_tensor(ln.nbias[:, tiles], ln.mv[:, tiles, 0], ln.rstd[:, tiles], ALU.mult))
    last = nc.gpsimd.tensor_scalar(ln.nbias[:, tiles], ln.nbias[:, tiles], -1.0, 0.0, ALU.mult, ALU.add)
    if ready is None:
        link(last)
    else:
        last.then_inc(ready, 1)


def of_seq(s):
    return slice(TPS * s, TPS * (s + 1))


def ln_apply(engine, ln, x, out, s, normed):
    for i in range(TPS * s, TPS * (s + 1)):
        engine.tensor_scalar(out[:, i, :], x[:, i, :], ln.rstd[:, i:i + 1], ln.nbias[:, i:i + 1],
                             ALU.mult, ALU.add).then_inc(normed, 1)


def phase_moe(core, io, tag, ln, moe_x, prefetch=(), landed=None, out=None, double=None):
    nc = core.nc
    UNITS = SEQS * FBLK
    with ExitStack() as ctx:
        def sb(name, shape, dt=F32):
            return ctx.enter_context(nc.sbuf_tensor(f"{tag}_{name}", shape, dt))

        def sem(name):
            return core.semaphore(f"{tag}_{name}")

        x, w = core.x, core.wsplit
        norm = sb("norm", [P, TILES, P])
        normT, x_hi, x_lo = moe_x
        shift = sb("shift", [P, TILES, EXPERTS])
        prob = sb("prob", [P, TILES, EXPERTS])
        prob2 = sb("prob2", [P, TILES, EXPERTS])
        eq = sb("eq", [P, TILES, EXPERTS])
        pick = sb("pick", [P, TILES, EXPERTS])
        first = sb("first", [P, TILES, EXPERTS])
        second = sb("second", [P, TILES, EXPERTS])
        rank = sb("rank", [P, EXPERTS])
        top = sb("top", [P, 6, TILES])
        w_branch = sb("w_branch", [P, BRANCHES, TILES])
        silu = sb("silu", [P, 2, SEQ])
        hid = sb("hid", [P, 2, SEQ])
        hid_hi = sb("hid_hi", [P, 2 * FBLK, SEQ], F16)
        hid_lo = sb("hid_lo", [P, 2 * FBLK, SEQ], F16)

        gate_ps, up_ps, down_ps, turn_ps, logit_ps = (core.banks[0:2], core.banks[2:4], core.banks[4:6],
                                                      core.banks[6], core.banks[7])
        normed, normed_late, normT_ready = sem("normed"), sem("normed_late"), sem("normT")
        lo_late_ready, veps_next, veps_last = sem("x_lo_late"), sem("veps_next"), sem("veps_last")

        x_turned, hi_ready, lo_ready, logits_made = sem("x_turned"), sem("x_hi"), sem("x_lo"), sem("logits")
        shift_ready, exp_ready, route_ready, rank_ready = sem("shift"), sem("exp"), sem("route"), sem("rank")
        gate_made, up_made, down_made = sem("gate"), sem("up"), sem("down")
        silu_ready, hid_ready, hid_hi_ready = sem("silu"), sem("hid"), sem("hid_hi")
        hid_lo0_ready, hid_lo1_ready, added = sem("hid_lo0"), sem("hid_lo1"), sem("added")
        dve_step, pool_step, act_step, stored = sem("dve_step"), sem("pool_step"), sem("act_step"), sem("stored")

        block = ctx.enter_context(nc.Block())

        @block.gpsimd
        def _(pool):
            steps = [0]

            def link(ins):
                steps[0] += 1
                ins.then_inc(pool_step, 1)
                pool.wait_ge(pool_step, steps[0])

            for s in range(2, SEQS):
                if s == SEQS - 1:
                    pool.wait_ge(veps_last, 1)
                    ln_rstd(nc, core, link, ln, of_seq(s))
                ln_apply(nc.gpsimd, ln, x, norm, s, normed_late)
            for k in range(EXPERTS):
                nc.gpsimd.memset(rank[:, k:k + 1], float(EXPERTS - k)).then_inc(rank_ready, 1)
            nc.gpsimd.memset(w_branch[:, 0, :], DOWN_UNSCALE).then_inc(rank_ready, 1)

            def branch(e):
                for s in range(SEQS):
                    slot = FBLK * (s % 2)
                    pool.wait_ge(hid_hi_ready, e * UNITS + 2 * s + 1)
                    nc.gpsimd.tensor_tensor(hid_lo[:, slot, :], hid[:, 0, :], hid_hi[:, slot, :],
                                            ALU.subtract).then_inc(hid_lo0_ready, 1)
                    if isinstance(e, int) and s < 2:
                        pool.wait_ge(hi_ready, s + 2)
                        tok = slice(SEQ * (s + 2), SEQ * (s + 3))
                        nc.gpsimd.tensor_tensor(x_lo[:, tok], normT[:, tok], x_hi[:, tok],
                                                ALU.subtract).then_inc(lo_late_ready, 1)
            branch(0)
            with pool.Fori(1, BRANCHES) as e:
                branch(e)
            if double is not None:
                pool.wait_ge(veps_next, 1)
                ln_rstd(nc, core, link, double[0], of_seq(0))

        @block.vector
        def _(dve):
            steps = [0]

            def link(ins):
                steps[0] += 1
                ins.then_inc(dve_step, 1)
                dve.wait_ge(dve_step, steps[0])

            def low_x(s):
                dve.wait_ge(hi_ready, s)
                tok = slice(SEQ * s, SEQ * (s + 1))
                nc.vector.tensor_tensor(x_lo[:, tok], normT[:, tok], x_hi[:, tok], ALU.subtract).then_inc(lo_ready, 1)

            def all_experts(ap):
                return ap.unsqueeze(2).broadcast_to([P, TILES, EXPERTS])

            def choose(scores, chosen, best):
                link(nc.vector.tensor_reduce(best, scores, AX_X, ALU.max))
                link(nc.vector.tensor_tensor(eq[:], scores, all_experts(best), ALU.is_equal))
                link(nc.vector.tensor_tensor(pick[:], eq[:], rank[:].unsqueeze(1)
                                             .broadcast_to([P, TILES, EXPERTS]), ALU.mult))
                link(nc.vector.tensor_reduce(top[:, 5, :], pick[:], AX_X, ALU.max))
                link(nc.vector.tensor_tensor(chosen, pick[:], all_experts(top[:, 5, :]), ALU.is_equal))

            def route_softmax():
                dve.wait_ge(logits_made, 1)
                logits = logit_ps[:, 0:TILES * EXPERTS].rearrange("p (i k) -> p i k", i=TILES)
                link(nc.vector.tensor_reduce(top[:, 0, :], logits, AX_X, ALU.max))
                nc.vector.tensor_tensor(shift[:], logits, all_experts(top[:, 0, :]),
                                        ALU.subtract).then_inc(shift_ready, 1)

            def route_first():
                dve.wait_ge(exp_ready, 1)
                dve.wait_ge(rank_ready, EXPERTS + 1)
                link(nc.vector.tensor_reduce(top[:, 1, :], shift[:], AX_X, ALU.add))
                link(nc.vector.reciprocal(top[:, 2, :], top[:, 1, :]))
                link(nc.vector.tensor_tensor(prob[:], shift[:], all_experts(top[:, 2, :]), ALU.mult))
                choose(prob[:], first[:], top[:, 3, :])

            def route_second():
                link(nc.vector.scalar_tensor_tensor(prob2[:], first[:], -4.0, prob[:], ALU.mult, ALU.add))
                choose(prob2[:], second[:], top[:, 4, :])

            def route_weights():
                link(nc.vector.scalar_tensor_tensor(top[:, 0, :], top[:, 3, :], 1e-20, top[:, 4, :], ALU.add, ALU.add))
                link(nc.vector.reciprocal(top[:, 1, :], top[:, 0, :]))
                link(nc.vector.tensor_tensor(first[:], first[:], second[:], ALU.add))
                link(nc.vector.scalar_tensor_tensor(first[:], first[:], DOWN_UNSCALE, prob[:], ALU.mult, ALU.mult))
                link(nc.vector.tensor_tensor(w_branch[:, 1:BRANCHES, :].rearrange("p k i -> p i k"), first[:],
                                             all_experts(top[:, 1, :]), ALU.mult))

            def hidden(e, u):
                dve.wait_ge(silu_ready, e * UNITS + u + 1)
                dve.wait_ge(up_made, e * UNITS + u + 1)
                peeled = isinstance(e, int) and e == 0
                if u % 2 == 0 and not (peeled and u == 0):
                    dve.wait_ge(hid_lo0_ready, e * SEQS + u // 2)
                if u % 2 and not (peeled and u == 1):
                    dve.wait_ge(hid_lo1_ready, e * SEQS + u // 2)
                nc.vector.scalar_tensor_tensor(hid[:, u % 2, :], up_ps[u % 2][:, :], GU_UNSCALE * H_SCALE,
                                               silu[:, u % 2, :], ALU.mult, ALU.mult).then_inc(hid_ready, 1)

            def low(s, made):
                slot = FBLK * (s % 2) + 1
                dve.wait_ge(hid_hi_ready, made)
                nc.vector.tensor_tensor(hid_lo[:, slot, :], hid[:, 1, :], hid_hi[:, slot, :],
                                        ALU.subtract).then_inc(hid_lo1_ready, 1)

            def add(e, s, count):
                dve.wait_ge(down_made, count)
                if isinstance(e, int) and e == 0:
                    nc.vector.scalar_tensor_tensor(x[:, of_seq(s), :], down_ps[s % 2][:, :]
                                                   .rearrange("p (c d) -> p c d", c=TPS), DOWN_UNSCALE,
                                                   x[:, of_seq(s), :], ALU.mult, ALU.add).then_inc(added, 1)
                    return
                for c in range(TPS):
                    i = TPS * s + c
                    ins = nc.vector.scalar_tensor_tensor(x[:, i, :], down_ps[s % 2][:, P * c:P * (c + 1)],
                                                         w_branch[:, e, i:i + 1], x[:, i, :], ALU.mult, ALU.add)
                ins.then_inc(added, 1)

            def branch(e):
                for s in range(SEQS):
                    hidden(e, 2 * s)
                    if isinstance(e, int) and s == 0:
                        low_x(1)
                    hidden(e, 2 * s + 1)
                    low(s, e * UNITS + 2 * s + 2)
                    if isinstance(e, int) and s == 1:
                        route_softmax()
                        route_first()
                    if isinstance(e, int) and s == 2:
                        route_second()
                    if isinstance(e, int) and s == 3:
                        route_weights()
                    if s:
                        add(e, s - 1, e * SEQS + s)
                    elif not (isinstance(e, int) and e == 0):
                        add(e - 1, SEQS - 1, e * SEQS)
            ln_apply(nc.vector, ln, x, norm, 1, normed)
            ln_stats(nc, link, ln, x, SEQS - 1, veps_last)
            branch(0)
            with dve.Fori(1, BRANCHES) as e:
                branch(e)
            if double is not None:
                dve.wait_ge(added, (BRANCHES - 1) * SEQS + 1)
                ln_double_stats(nc, link, double[0], double[1], x, 0, veps_next)
            add(BRANCHES - 1, SEQS - 1, BRANCHES * SEQS)

        @block.scalar
        def _(act):
            def high_x(s):
                act.wait_ge(x_turned, s)
                tok = slice(SEQ * s, SEQ * (s + 1))
                nc.scalar.mul(normT[:, tok], turn_ps[:, :], X_SCALE).then_inc(normT_ready, 1)
                act.wait_ge(normT_ready, s)
                nc.scalar.copy(x_hi[:, tok], normT[:, tok]).then_inc(hi_ready, 1)

            def high(u, made, read):
                slot = FBLK * (u // 2 % 2) + u % 2
                if read is not None:
                    act.wait_ge(down_made, read)
                act.wait_ge(hid_ready, made)
                nc.scalar.copy(hid_hi[:, slot, :], hid[:, u % 2, :]).then_inc(hid_hi_ready, 1)

            def branch(e):
                peeled = isinstance(e, int) and e == 0
                for s in range(SEQS):
                    for u in (2 * s, 2 * s + 1):
                        act.wait_ge(gate_made, e * UNITS + u + 1)
                        if not (peeled and s == 0):
                            act.wait_ge(hid_ready, e * UNITS + u - 1)
                        nc.scalar.activation(silu[:, u % 2, :], gate_ps[u % 2][:, :], ACT.Silu,
                                             scale=GU_UNSCALE).then_inc(silu_ready, 1)
                        if isinstance(e, int) and u + 1 < SEQS:
                            high_x(u + 1)
                    for u in (2 * s, 2 * s + 1):
                        high(u, e * UNITS + u + 1, None if peeled and s < 2 else e * SEQS + s - 1)
                    if peeled and s == 1:
                        act.wait_ge(shift_ready, 1)
                        nc.scalar.activation(shift[:], shift[:], ACT.Exp, scale=1.0 / X_SCALE).then_inc(exp_ready, 1)
            nc.scalar.activation(silu[:, 0, 0:1], core.ident[:, 0:1], ACT.Silu).then_inc(act_step, 1)
            act.wait_ge(act_step, 1)
            branch(0)
            with act.Fori(1, BRANCHES) as e:
                branch(e)

        @block.tensor
        def _(pe):
            def turn(s):
                for c in range(TPS):
                    if s < 2:
                        pe.wait_ge(normed, c + 1)
                    else:
                        pe.wait_ge(normed_late, TPS * (s - 2) + c + 1)
                    if c == 0 and s > 1:
                        pe.wait_ge(normT_ready, s - 1)
                    ins = nc.tensor.transpose(turn_ps[:, P * c:P * (c + 1)], norm[:, TPS * s + c, :], core.ident[:])
                ins.then_inc(x_turned, 1)

            def logits():
                pe.wait_ge(normT_ready, SEQS - 1)
                for i in range(TILES):
                    ins = nc.tensor.matmul(logit_ps[:, EXPERTS * i:EXPERTS * (i + 1)], normT[:, P * i:P * (i + 1)],
                                           core.router_w[:], start=True, stop=True)
                ins.then_inc(logits_made, 1)

            def gate_up(e, u):
                s, blk = u // 2, u % 2
                tok = slice(SEQ * s, SEQ * (s + 1))
                if not (isinstance(e, int) and e == 0 and u < 2):
                    pe.wait_ge(hid_ready, e * UNITS + u - 1)
                first_use = isinstance(e, int) and blk == 0 and s > 0
                if first_use:
                    pe.wait_ge(hi_ready, s)
                for part, bank, made in ((0, gate_ps, gate_made), (2, up_ps, up_made)):
                    hi = w[:, e, part, P * blk:P * (blk + 1)]
                    lo = w[:, e, part + 1, P * blk:P * (blk + 1)]
                    dst = bank[u % 2][:, :]
                    nc.tensor.matmul(dst, hi, x_hi[:, tok], start=True, stop=False)
                    nc.tensor.matmul(dst, lo, x_hi[:, tok], start=False, stop=False)
                    if first_use and part == 0:
                        if s < 2:
                            pe.wait_ge(lo_ready, s)
                        else:
                            pe.wait_ge(lo_late_ready, s - 1)
                    nc.tensor.matmul(dst, hi, x_lo[:, tok], start=False, stop=True).then_inc(made, 1)

            def down(e, s, count):
                pe.wait_ge(hid_lo0_ready, count)
                pe.wait_ge(hid_lo1_ready, count)
                if not (isinstance(count, int) and count <= 2):
                    pe.wait_ge(added, count - 2)
                for c in range(TPS):
                    dst = down_ps[s % 2][:, P * c:P * (c + 1)]
                    for blk in range(FBLK):
                        slot = FBLK * (s % 2) + blk
                        h_hi = hid_hi[:, slot, P * c:P * (c + 1)]
                        h_lo = hid_lo[:, slot, P * c:P * (c + 1)]
                        d_hi = w[:, e, 4, P * blk:P * (blk + 1)]
                        d_lo = w[:, e, 5, P * blk:P * (blk + 1)]
                        nc.tensor.matmul(dst, h_hi, d_hi, start=blk == 0, stop=False)
                        nc.tensor.matmul(dst, h_hi, d_lo, start=False, stop=False)
                        ins = nc.tensor.matmul(dst, h_lo, d_hi, start=False, stop=blk == FBLK - 1)
                ins.then_inc(down_made, 1)

            def branch(e):
                for s in range(SEQS):
                    for u in (2 * s, 2 * s + 1):
                        gate_up(e, u)
                        if isinstance(e, int) and u + 1 < SEQS:
                            turn(u + 1)
                    if isinstance(e, int) and s == 1:
                        logits()
                    if s:
                        down(e, s - 1, e * SEQS + s)
                    elif not (isinstance(e, int) and e == 0):
                        down(e - 1, SEQS - 1, e * SEQS)
            branch(0)
            with pe.Fori(1, BRANCHES) as e:
                branch(e)
            down(BRANCHES - 1, SEQS - 1, BRANCHES * SEQS)

        @block.sync
        def _(sp):
            core.clear_retired(sp)
            for dst, name in prefetch:
                sp.dma_start(dst[:], io[name]).then_inc(landed, 16)
            if out is not None:
                dst = out.rearrange("s (c p) d -> s p c d", p=P)
                for s in range(SEQS):
                    sp.wait_ge(added, (BRANCHES - 1) * SEQS + s + 1)
                    sp.dma_start(dst[s], x[:, TPS * s:TPS * (s + 1), :]).then_inc(stored, 16)
                sp.wait_ge(stored, 16 * SEQS)


def phase_time_mix(core, io, shared):
    nc = core.nc
    with ExitStack() as ctx:
        def sb(name, shape, dt=F32):
            return ctx.enter_context(nc.sbuf_tensor("tm_" + name, shape, dt))

        def sem(name):
            return core.semaphore("tm_" + name)

        x, x4, w_rkvo = core.x, shared.x4, shared.w_rkvo
        ln_a, v_eps = shared.ln_tm, shared.v_eps
        ln_b = LayerNorm(nc, ctx, "tm_ln1")
        xn_ready = sem("xn")
        v_copied = sem("v_copied")
        cm_normed, cm_turned, cm_hT_ready, cm_dif_ready = (
            sem("cm_normed"), sem("cm_turned"), sem("cm_hT"), sem("cm_dif"))
        veps_a, veps_b, veps_cm, normed = sem("veps_a"), sem("veps_b"), sem("veps_cm"), sem("normed")
        xn = sb("xn", [P, 2, TPS, P])
        hn = sb("ln1_n", [P, TILES, P])
        hT = sb("ln1_T", [P, SEQS, SEQ + 1])
        w_now = sb("w_now", [P, 3, P])
        w_prev = sb("w_prev", [P, 3, P])
        w_decay = sb("w_decay", [P, 1])
        pp = sb("pp", [P, SEQ + 1])
        aa = sb("aa", [P, 2, SEQ + 1])
        bb = sb("bb", [P, 2, SEQ + 1])
        lead = sb("lead", [P, 2, SEQ])
        expo = sb("expo", [P, 2, 4, SEQ])
        e_r = sb("e_r", [P, 2, SEQ])
        v_sb = sb("v_sb", [P, 2, SEQ])
        e2v = sb("e2v", [P, SEQ])
        y2v = sb("y2v", [P, 2, SEQ])
        num = sb("num", [P, 2, SEQ])
        den = sb("den", [P, 2, SEQ])
        den_r = sb("den_r", [P, SEQ])
        recip = sb("recip", [P, SEQ])
        att = sb("att", [P, 2, SEQ])

        turn_ps, kvr_ps, out_ps = core.banks[0], (core.banks[1:4], core.banks[4:7]), core.banks[7]

        decay_act, decay_ready, rstd_ready = sem("decay_act"), sem("decay"), sem("rstd")
        h_turned, hT_ready, w_now_ready, w_prev_ready = sem("h_turned"), sem("hT"), sem("w_now"), sem("w_prev")
        kvr_made, raw_ready, lead_ready, lead_act = sem("kvr"), sem("raw"), sem("lead"), sem("lead_act")
        expo_ready, aabb_ready, num_ready, att_ready = sem("expo"), sem("aabb"), sem("num"), sem("att")
        den_ready = sem("den")
        e2v_ready, neg_r_ready, er_ready, y2v_ready, zeroed = sem("e2v"), sem("neg_r"), sem("er"), sem("y2v"), sem("zeroed")
        out_made, x4_ready = sem("out"), sem("x4")
        dve_step, pool_step, act_step = sem("dve_step"), sem("pool_step"), sem("act_step")

        block = ctx.enter_context(nc.Block())

        @block.sync
        def _(sp):
            core.clear_retired(sp)

        @block.gpsimd
        def _(pool):
            steps = [0]

            def link(ins):
                steps[0] += 1
                ins.then_inc(pool_step, 1)
                pool.wait_ge(pool_step, steps[0])

            link(nc.gpsimd.memset(shared.hT[:, :, 0:1], 0.0))
            nc.gpsimd.memset(hT[:, :, 0:1], 0.0).then_inc(zeroed, 1)
            nc.gpsimd.memset(pp[:, 0:1], -1e38).then_inc(zeroed, 1)
            nc.gpsimd.memset(aa[:, :, 0:1], 0.0).then_inc(zeroed, 1)
            nc.gpsimd.memset(bb[:, :, 0:1], 0.0).then_inc(zeroed, 1)

            pool.wait_ge(shared.w_b_in, 16 * 4)
            for j, name in enumerate(("tmk", "tmv", "tmr")):
                nc.gpsimd.tensor_scalar(w_now[:, j, :], w_rkvo[:, j, :], col(core, name), None,
                                        ALU.mult).then_inc(w_now_ready, 1)
            for j in range(3):
                pool.wait_ge(w_now_ready, j + 1)
                nc.gpsimd.tensor_tensor(w_prev[:, j, :], w_rkvo[:, j, :], w_now[:, j, :],
                                        ALU.subtract).then_inc(w_prev_ready, 1)

            def rstd(s):
                pool.wait_ge(veps_a, s)
                ln_rstd(nc, core, link, ln_a, of_seq(s), rstd_ready)

            def sums(s):
                k = s % 2
                pool.wait_ge(expo_ready, 4 * (s + 1))
                if s >= 2:
                    pool.wait_ge(att_ready, s - 1)
                if s < SEQS - 1:
                    pool.wait_ge(aabb_ready, 2 * s + 1)
                    link(nc.gpsimd.tensor_tensor(den[:, k, :], expo[:, k, 2, :], bb[:, k, 0:SEQ], ALU.mult))
                    nc.gpsimd.tensor_tensor(den[:, k, :], den[:, k, :], expo[:, k, 3, :], ALU.add).then_inc(den_ready, 1)
                pool.wait_ge(v_copied, s + 1)
                nc.gpsimd.tensor_tensor(y2v[:, k, :], expo[:, k, 3, :], v_sb[:, k, :], ALU.mult).then_inc(y2v_ready, 1)
                pool.wait_ge(aabb_ready, 2 * (s + 1))
                link(nc.gpsimd.tensor_tensor(num[:, k, :], expo[:, k, 2, :], aa[:, k, 0:SEQ], ALU.mult))
                pool.wait_ge(y2v_ready, s + 1)
                nc.gpsimd.tensor_tensor(num[:, k, :], num[:, k, :], y2v[:, k, :], ALU.add).then_inc(num_ready, 1)

            rstd(1)
            for s in range(SEQS):
                pool.wait_ge(veps_b, s + 1)
                ln_rstd(nc, core, link, ln_b, of_seq(s))
                ln_apply(nc.gpsimd, ln_b, x4, hn, s, normed)
                if s + 2 < SEQS:
                    rstd(s + 2)
            for s in range(SEQS):
                sums(s)
            pool.wait_ge(veps_cm, 1)
            ln_rstd(nc, core, link, shared.ln_cm, of_seq(0))
            ln_apply(nc.gpsimd, shared.ln_cm, x4, shared.hn, 0, cm_normed)
            pool.wait_ge(cm_hT_ready, 1)
            shift_difference(nc, shared, 0, cm_dif_ready)

        @block.vector
        def _(dve):
            steps = [0]

            def link(ins):
                steps[0] += 1
                ins.then_inc(dve_step, 1)
                dve.wait_ge(dve_step, steps[0])

            w_rows = w_decay[:].broadcast_to([P, SEQ])

            def rows(name):
                return col(core, name, 0, P).unsqueeze(1).broadcast_to([P, TPS, P])

            def affine(s):
                dve.wait_ge(xn_ready, s + 1)
                link(nc.vector.tensor_tensor(xn[:, s % 2], xn[:, s % 2], rows("ln0_w"), ALU.mult))
                link(nc.vector.tensor_tensor(x4[:, of_seq(s), :], xn[:, s % 2], rows("ln0_b"), ALU.add))

            def scans(s):
                k = s % 2
                kk = kvr_ps[k][0][:, :]
                if s == 0:
                    dve.wait_ge(decay_ready, 1)
                    dve.wait_ge(zeroed, 4)
                dve.wait_ge(kvr_made, 3 * s + 1)
                link(nc.vector.tensor_tensor_scan(pp[:, 1:SEQ + 1], w_rows, kk, -1e38, ALU.add, ALU.max))
                if s >= 2:
                    dve.wait_ge(expo_ready, 4 * (s - 1))
                    dve.wait_ge(num_ready, s - 1)
                nc.vector.scalar_tensor_tensor(expo[:, k, 0, :], pp[:, 0:SEQ], w_decay[:], pp[:, 1:SEQ + 1],
                                               ALU.add, ALU.subtract).then_inc(raw_ready, 1)
                nc.vector.tensor_tensor(expo[:, k, 1, :], kk, pp[:, 1:SEQ + 1], ALU.subtract).then_inc(raw_ready, 1)
                nc.vector.scalar_tensor_tensor(lead[:, k, :], pp[:, 0:SEQ], col(core, "first"), kk,
                                               ALU.subtract, ALU.subtract).then_inc(lead_ready, 1)
                dve.wait_ge(expo_ready, 4 * s + 2)
                dve.wait_ge(v_copied, s + 1)
                nc.vector.tensor_tensor(e2v[:], expo[:, k, 1, :], v_sb[:, k, :], ALU.mult).then_inc(e2v_ready, 1)
                nc.vector.tensor_tensor_scan(bb[:, k, 1:SEQ + 1], expo[:, k, 0, :], expo[:, k, 1, :], 0.0,
                                             ALU.mult, ALU.add).then_inc(aabb_ready, 1)
                dve.wait_ge(e2v_ready, s + 1)
                nc.vector.tensor_tensor_scan(aa[:, k, 1:SEQ + 1], expo[:, k, 0, :], e2v[:], 0.0,
                                             ALU.mult, ALU.add).then_inc(aabb_ready, 1)
                dve.wait_ge(kvr_made, 3 * (s + 1))
                nc.vector.tensor_scalar(e_r[:, k, :], kvr_ps[k][2][:, :], -1.0, 80.0, ALU.mult,
                                        ALU.min).then_inc(neg_r_ready, 1)

            def divide(s):
                k = s % 2
                if s < SEQS - 1:
                    dve.wait_ge(den_ready, s + 1)
                dve.wait_ge(er_ready, s + 1)
                link(nc.vector.scalar_tensor_tensor(den_r[:], e_r[:, k, :], 1.0, den[:, k, :], ALU.add, ALU.mult))
                link(nc.vector.reciprocal(recip[:], den_r[:]))
                dve.wait_ge(num_ready, s + 1)
                if s >= 2:
                    dve.wait_ge(out_made, s - 1)
                nc.vector.tensor_tensor(att[:, k, :], num[:, k, :], recip[:], ALU.mult).then_inc(att_ready, 1)

            def join(s):
                a, b = TPS * s, TPS * (s + 1)
                dve.wait_ge(out_made, s + 1)
                nc.vector.tensor_tensor(x4[:, a:b, :], x4[:, a:b, :],
                                        out_ps[:, :].rearrange("p (c d) -> p c d", c=TPS), ALU.add).then_inc(x4_ready, 1)

            def denominator(s):
                k = s % 2
                dve.wait_ge(expo_ready, 4 * (s + 1))
                link(nc.vector.tensor_tensor(den[:, k, :], expo[:, k, 2, :], bb[:, k, 0:SEQ], ALU.mult))
                link(nc.vector.tensor_tensor(den[:, k, :], den[:, k, :], expo[:, k, 3, :], ALU.add))

            for s in range(1, SEQS):
                ln_double_stats(nc, link, ln_a, v_eps, x, s, veps_a)
                affine(s - 1)
                ln_stats(nc, link, ln_b, x4, s - 1, veps_b)
                if s == 1:
                    dve.wait_ge(decay_act, 1)
                    nc.vector.tensor_scalar(w_decay[:], w_decay[:], -1.0, None, ALU.mult).then_inc(decay_ready, 1)
            for s in range(SEQS):
                scans(s)
                if s == 0:
                    affine(SEQS - 1)
                    ln_stats(nc, link, ln_b, x4, SEQS - 1, veps_b)
                if s == SEQS - 1:
                    dve.wait_ge(x4_ready, 1)
                    ln_stats(nc, link, shared.ln_cm, x4, 0, veps_cm)
                if s >= 1:
                    divide(s - 1)
                if s >= 2:
                    join(s - 2)
            denominator(SEQS - 1)
            divide(SEQS - 1)
            join(SEQS - 2)
            dve.wait_ge(cm_dif_ready, 1)
            mix_channels(nc, core, shared, 0)
            join(SEQS - 1)

        @block.scalar
        def _(act):
            def normalise(s):
                if s:
                    act.wait_ge(rstd_ready, s)
                if s >= 2:
                    act.wait_ge(veps_b, s - 1)
                for c in range(TPS):
                    i = TPS * s + c
                    ins = nc.scalar.activation(xn[:, s % 2, c, :], x[:, i, :], ACT.Identity,
                                               scale=ln_a.rstd[:, i:i + 1], bias=ln_a.nbias[:, i:i + 1])
                ins.then_inc(xn_ready, 1)

            def turned(s):
                act.wait_ge(h_turned, s + 1)
                nc.scalar.activation(hT[:, s, 1:SEQ + 1], turn_ps[:, :], ACT.Identity,
                                     bias=col(core, "ln1_b"), scale=col(core, "ln1_w")).then_inc(hT_ready, 1)

            def exponentials(s):
                k = s % 2
                for j in range(2):
                    act.wait_ge(raw_ready, 2 * s + j + 1)
                    nc.scalar.activation(expo[:, k, j, :], expo[:, k, j, :], ACT.Exp).then_inc(expo_ready, 1)
                act.wait_ge(kvr_made, 3 * s + 2)
                if s >= 2:
                    act.wait_ge(e2v_ready, s - 1)
                    act.wait_ge(y2v_ready, s - 1)
                nc.scalar.copy(v_sb[:, k, :], kvr_ps[k][1][:, :]).then_inc(v_copied, 1)
                act.wait_ge(lead_ready, s + 1)
                for j, sign in ((2, -1.0), (3, 1.0)):
                    nc.scalar.activation(expo[:, k, j, :], lead[:, k, :], ACT.Relu, scale=sign).then_inc(lead_act, 1)
                for j in (2, 3):
                    act.wait_ge(lead_act, 2 * s + j - 1)
                    nc.scalar.activation(expo[:, k, j, :], expo[:, k, j, :], ACT.Exp, scale=-1.0).then_inc(expo_ready, 1)
                act.wait_ge(neg_r_ready, s + 1)
                nc.scalar.activation(e_r[:, k, :], e_r[:, k, :], ACT.Exp).then_inc(er_ready, 1)

            normalise(0)
            nc.scalar.activation(w_decay[:], col(core, "decay"), ACT.Exp).then_inc(decay_act, 1)
            normalise(1)
            turned(0)
            normalise(2)
            turned(1)
            normalise(3)
            for s in range(SEQS):
                exponentials(s)
                if s + 2 < SEQS:
                    turned(s + 2)
            act.wait_ge(cm_turned, 1)
            copy_ln2(nc, core, shared, turn_ps, 0, cm_hT_ready)

        @block.tensor
        def _(pe):
            pe.wait_ge(shared.w_b_in, 16 * 4)
            def turn(s):
                for c in range(TPS):
                    pe.wait_ge(normed, TPS * s + c + 1)
                    if c == 0 and s:
                        pe.wait_ge(hT_ready, s)
                    ins = nc.tensor.transpose(turn_ps[:, P * c:P * (c + 1)], hn[:, TPS * s + c, :], core.ident[:])
                ins.then_inc(h_turned, 1)

            def project(s, parts):
                pe.wait_ge(hT_ready, s + 1)
                for j in parts:
                    if s >= 2 and j == 0:
                        pe.wait_ge(lead_ready, s - 1)
                        pe.wait_ge(v_copied, s - 1)
                        pe.wait_ge(neg_r_ready, s - 1)
                    nc.tensor.matmul(kvr_ps[s % 2][j][:, :], w_now[:, j, :], hT[:, s, 1:SEQ + 1],
                                     start=True, stop=False)
                    nc.tensor.matmul(kvr_ps[s % 2][j][:, :], w_prev[:, j, :], hT[:, s, 0:SEQ],
                                     start=False, stop=True).then_inc(kvr_made, 1)

            def output(s):
                pe.wait_ge(att_ready, s + 1)
                if s:
                    pe.wait_ge(x4_ready, s)
                for c in range(TPS):
                    ins = nc.tensor.matmul(out_ps[:, P * c:P * (c + 1)], att[:, s % 2, P * c:P * (c + 1)],
                                           w_rkvo[:, 3, :], start=True, stop=True)
                ins.then_inc(out_made, 1)

            turn(0)
            pe.wait_ge(zeroed, 4)
            pe.wait_ge(w_prev_ready, 3)
            project(0, (0,))
            turn(1)
            project(0, (1, 2))
            turn(2)
            project(1, (0, 1, 2))
            turn(3)
            project(2, (0, 1, 2))
            output(0)
            project(3, (0, 1, 2))
            output(1)
            output(2)
            for c in range(TPS):
                pe.wait_ge(cm_normed, c + 1)
                ins = nc.tensor.transpose(turn_ps[:, P * c:P * (c + 1)], shared.hn[:, c, :], core.ident[:])
            ins.then_inc(cm_turned, 1)
            output(3)


def copy_ln2(nc, core, shared, bank, s, done):
    nc.scalar.activation(shared.hT[:, s, 1:SEQ + 1], bank[:, :], ACT.Identity,
                         bias=col(core, "ln2_b"), scale=col(core, "ln2_w")).then_inc(done, 1)


def shift_difference(nc, shared, s, done):
    nc.gpsimd.tensor_tensor(shared.dif[:, s % 2, :], shared.hT[:, s, 1:SEQ + 1], shared.hT[:, s, 0:SEQ],
                            ALU.subtract).then_inc(done, 1)


def mix_channels(nc, core, shared, s, done=None):
    for j, name in enumerate(("cmk", "cmr")):
        ins = nc.vector.scalar_tensor_tensor(shared.mixed[:, s % 2, j, :], shared.dif[:, s % 2, :], col(core, name),
                                             shared.hT[:, s, 0:SEQ], ALU.mult, ALU.add)
        if done is not None:
            ins.then_inc(done, 1)


def phase_channel_mix(core, io, shared):
    nc = core.nc
    HB = HIDDEN // P
    HRING = 3
    with ExitStack() as ctx:
        def sb(name, shape, dt=F32):
            return ctx.enter_context(nc.sbuf_tensor("cm_" + name, shape, dt))

        def sem(name):
            return core.semaphore("cm_" + name)

        x, x4 = core.x, shared.x4
        ln = shared.ln_cm
        veps_ready, normed, veps_next = sem("veps"), sem("normed"), sem("veps_next")
        hn, mixed = shared.hn, shared.mixed
        relu = sb("relu", [P, HRING, SEQ])
        sq = sb("sq", [P, 2, HB, SEQ])
        sig = sb("sig", [P, 2, SEQ])
        rkv = sb("rkv", [P, 2, SEQ])

        turn_ps, hid_ps, kv_ps, r_ps = core.banks[0], core.banks[1:4], core.banks[4:6], core.banks[6:8]
        h_turned, hT_ready, dif_ready, mixed_ready = sem("h_turned"), sem("hT"), sem("dif"), sem("mixed")
        hid_made, relu_ready, sq_ready, kv_made = sem("hid"), sem("relu"), sem("sq"), sem("kv")
        r_made, sig_ready, rkv_ready, x_ready = sem("r"), sem("sig"), sem("rkv"), sem("x")
        x4_added = sem("x4_added")
        next_normed, next_turned, next_T, next_hi, next_lo = (
            sem("next_normed"), sem("next_turned"), sem("next_T"), sem("next_hi"), sem("next_lo"))
        dve_step, pool_step = sem("dve_step"), sem("pool_step")

        block = ctx.enter_context(nc.Block())

        @block.sync
        def _(sp):
            core.clear_retired(sp)

        @block.gpsimd
        def _(pool):
            steps = [0]

            def link(ins):
                steps[0] += 1
                ins.then_inc(pool_step, 1)
                pool.wait_ge(pool_step, steps[0])

            def normalise(s):
                pool.wait_ge(veps_ready, s)
                ln_rstd(nc, core, link, ln, of_seq(s))
                ln_apply(nc.gpsimd, ln, x4, hn, s, normed)

            def difference(s):
                pool.wait_ge(hT_ready, s)
                if s > 2:
                    pool.wait_ge(mixed_ready, 2 * (s - 2))
                shift_difference(nc, shared, s, dif_ready)

            def add_x4(s):
                nc.gpsimd.tensor_tensor(x[:, of_seq(s), :], x[:, of_seq(s), :], x4[:, of_seq(s), :],
                                        ALU.add).then_inc(x4_added, 1)

            normalise(1)
            add_x4(0)
            for s in range(1, SEQS):
                if s + 1 < SEQS:
                    normalise(s + 1)
                difference(s)
                add_x4(s)
            for s in range(SEQS - 1):
                pool.wait_ge(veps_next, s + 1)
                ln_rstd(nc, core, link, shared.ln, of_seq(s))
                if s == 0:
                    ln_apply(nc.gpsimd, shared.ln, x, hn, 0, next_normed)
            pool.wait_ge(next_hi, 1)
            nc.gpsimd.tensor_tensor(shared.x_lo[:, 0:SEQ], shared.normT[:, 0:SEQ], shared.x_hi[:, 0:SEQ],
                                    ALU.subtract).then_inc(next_lo, 1)

        @block.vector
        def _(dve):
            steps = [0]

            def link(ins):
                steps[0] += 1
                ins.then_inc(dve_step, 1)
                dve.wait_ge(dve_step, steps[0])

            def mixing(s):
                dve.wait_ge(dif_ready, s)
                if s >= 2:
                    dve.wait_ge(hid_made, HB * (s - 1))
                    dve.wait_ge(r_made, s - 1)
                mix_channels(nc, core, shared, s, mixed_ready)

            def squares(s):
                for b in range(HB):
                    n = HB * s + b
                    dve.wait_ge(relu_ready, n + 1)
                    if s >= 2 and b == 0:
                        dve.wait_ge(kv_made, TPS * (s - 1))
                    nc.vector.scalar_tensor_tensor(sq[:, s % 2, b, :], hid_ps[n % HRING][:, :], 0.0,
                                                   relu[:, n % HRING, :], ALU.max, ALU.mult).then_inc(sq_ready, 1)

            def gated(s):
                dve.wait_ge(kv_made, TPS * (s + 1))
                dve.wait_ge(sig_ready, s + 1)
                nc.vector.tensor_tensor(rkv[:, s % 2, :], sig[:, s % 2, :], kv_ps[s % 2][:, :],
                                        ALU.mult).then_inc(rkv_ready, 1)
                dve.wait_ge(rkv_ready, s + 1)
                dve.wait_ge(x4_added, s + 1)
                nc.vector.tensor_tensor(x[:, of_seq(s), :], x[:, of_seq(s), :],
                                        rkv[:, s % 2, :].rearrange("p (c d) -> p c d", c=TPS),
                                        ALU.add).then_inc(x_ready, 1)
                if s < SEQS - 1:
                    dve.wait_ge(x_ready, s + 1)
                    ln_stats(nc, link, shared.ln, x, s, veps_next)

            for s in range(1, SEQS):
                ln_stats(nc, link, ln, x4, s, veps_ready)
            for s in range(SEQS):
                squares(s)
                if s >= 1:
                    gated(s - 1)
                if s + 1 < SEQS:
                    mixing(s + 1)
            gated(SEQS - 1)

        @block.scalar
        def _(act):
            def shifted(s):
                act.wait_ge(h_turned, s)
                copy_ln2(nc, core, shared, turn_ps, s, hT_ready)

            for s in range(SEQS):
                for b in range(HB):
                    n = HB * s + b
                    act.wait_ge(hid_made, n + 1)
                    if n >= HRING:
                        act.wait_ge(sq_ready, n - HRING + 1)
                    nc.scalar.activation(relu[:, n % HRING, :], hid_ps[n % HRING][:, :],
                                         ACT.Relu).then_inc(relu_ready, 1)
                act.wait_ge(r_made, s + 1)
                if s >= 2:
                    act.wait_ge(rkv_ready, s - 1)
                nc.scalar.activation(sig[:, s % 2, :], r_ps[s % 2][:, :], ACT.Sigmoid).then_inc(sig_ready, 1)
                if s == 0:
                    shifted(1)
                if s + 2 < SEQS:
                    shifted(s + 2)
            act.wait_ge(next_turned, 1)
            nc.scalar.mul(shared.normT[:, 0:SEQ], turn_ps[:, :], X_SCALE).then_inc(next_T, 1)
            act.wait_ge(next_T, 1)
            nc.scalar.copy(shared.x_hi[:, 0:SEQ], shared.normT[:, 0:SEQ]).then_inc(next_hi, 1)

        @block.tensor
        def _(pe):
            def turn(s):
                for c in range(TPS):
                    pe.wait_ge(normed, TPS * (s - 1) + c + 1)
                    if c == 0 and s > 1:
                        pe.wait_ge(hT_ready, s - 1)
                    ins = nc.tensor.transpose(turn_ps[:, P * c:P * (c + 1)], hn[:, TPS * s + c, :], core.ident[:])
                ins.then_inc(h_turned, 1)

            def hidden(s):
                if s:
                    pe.wait_ge(mixed_ready, 2 * s - 1)
                for b in range(HB):
                    n = HB * s + b
                    if n >= HRING:
                        pe.wait_ge(sq_ready, n - HRING + 1)
                    nc.tensor.matmul(hid_ps[n % HRING][:, :], shared.w_fk[:, P * b:P * (b + 1)], mixed[:, s % 2, 0, :],
                                     start=True, stop=True).then_inc(hid_made, 1)

            def receptance(s):
                if s:
                    pe.wait_ge(mixed_ready, 2 * s)
                if s >= 2:
                    pe.wait_ge(sig_ready, s - 1)
                for c in range(TPS):
                    ins = nc.tensor.matmul(r_ps[s % 2][:, P * c:P * (c + 1)], mixed[:, s % 2, 1, P * c:P * (c + 1)],
                                           shared.w_fr[:], start=True, stop=True)
                ins.then_inc(r_made, 1)

            def values(s):
                pe.wait_ge(sq_ready, HB * (s + 1))
                if s >= 2:
                    pe.wait_ge(rkv_ready, s - 1)
                for c in range(TPS):
                    for b in range(HB):
                        ins = nc.tensor.matmul(kv_ps[s % 2][:, P * c:P * (c + 1)],
                                               sq[:, s % 2, b, P * c:P * (c + 1)], shared.w_fv[:, b, :],
                                               start=b == 0, stop=b == HB - 1)
                    ins.then_inc(kv_made, 1)

            def turn_next():
                for c in range(TPS):
                    pe.wait_ge(next_normed, c + 1)
                    ins = nc.tensor.transpose(turn_ps[:, P * c:P * (c + 1)], hn[:, c, :], core.ident[:])
                ins.then_inc(next_turned, 1)

            for s in range(SEQS):
                hidden(s)
                receptance(s)
                if s == 0:
                    turn(1)
                if s == SEQS - 1:
                    turn_next()
                values(s)
                if s + 2 < SEQS:
                    turn(s + 2)


class Shared:
    pass


def program(nc, io, stop_after=9):
    core = Core(nc)
    with ExitStack() as top:
        constants(core, top)
        ln_moe1, ln_moe2, ln_tm, ln_cm = (LayerNorm(nc, top, name) for name in ("ln_moe1", "ln_moe2", "ln_tm", "ln_cm"))
        moe_x = (top.enter_context(nc.sbuf_tensor("normT_moe", [P, TOKENS], F32)),
                 top.enter_context(nc.sbuf_tensor("x_hi", [P, TOKENS], F16)),
                 top.enter_context(nc.sbuf_tensor("x_lo", [P, TOKENS], F16)))
        with ExitStack() as mamba:
            sh = Shared()
            sh.normT, sh.x_hi, sh.x_lo = moe_x

            def sb(name, shape, dt=F32):
                return mamba.enter_context(nc.sbuf_tensor(name, shape, dt))
            sh.ln = ln_moe1
            sh.norm = sb("norm", [P, TILES, P])
            sh.q = sb("q", [P, TILES, P])
            sh.xbc = sb("xbc", [P, CONV_BLOCKS, TOKENS])
            sh.sz = sb("sz", [P, TILES, INNER])
            sh.dt_raw = sb("dt_raw", [P, TILES, HEADS])
            sh.xtok = sb("xtok", [P, TILES, XTOK])
            sh.moe_raw = sb("moe_raw", [P, MOE_RING, 3 * FFN])
            sh.w_out = sb("w_out", [P, 2, P])
            sh.w_out_in = top.enter_context(nc.semaphore("w_out_in"))
            phase_mamba_in(core, io, sh)
            core.end_phase()
            phase_ssd(core, io, sh)
            core.end_phase()
        with ExitStack() as rwkv:
            sh = Shared()

            def sb(name, shape, dt=F32):
                return rwkv.enter_context(nc.sbuf_tensor(name, shape, dt))
            sh.ln, sh.ln_cm, sh.ln_tm = ln_moe2, ln_cm, ln_tm
            sh.v_eps = sb("v_eps", [P, TILES])
            sh.normT, sh.x_hi, sh.x_lo = moe_x
            sh.w_rkvo = sb("w_rkvo", [P, 4, P])
            sh.w_fk = sb("w_fk", [P, HIDDEN])
            sh.w_fr = sb("w_fr", [P, P])
            sh.w_fv = sb("w_fv", [P, HIDDEN // P, P])
            sh.w_b_in = top.enter_context(nc.semaphore("w_b_in"))
            phase_moe(core, io, "moe1", ln_moe1, moe_x, double=(ln_tm, sh.v_eps), landed=sh.w_b_in,
                      prefetch=[(sh.w_rkvo, "w_rkvo"), (sh.w_fk, "w_fk"), (sh.w_fr, "w_fr"), (sh.w_fv, "w_fv")])
            core.end_phase()
            sh.x4 = sb("x4", [P, TILES, P])
            sh.hn = sb("hn", [P, TILES, P])
            sh.hT = sb("hT", [P, SEQS, SEQ + 1])
            sh.dif = sb("dif", [P, 2, SEQ])
            sh.mixed = sb("mixed", [P, 2, 2, SEQ])
            phase_time_mix(core, io, sh)
            core.end_phase()
            phase_channel_mix(core, io, sh)
            core.end_phase()
        phase_moe(core, io, "moe2", ln_moe2, moe_x, out=io["out"])
        core.end_phase()
        core.end_phase()


def rope_tables():
    head, half = 8, 4
    inv_freq = 1.0 / 10000.0 ** (np.arange(0, head, 2, dtype=np.float32) / np.float32(head))
    angle = np.arange(SEQ, dtype=np.float32)[:, None] * inv_freq[None, :].astype(np.float32)
    cos, sin = np.cos(angle), np.sin(angle)
    cos = np.tile(np.concatenate([cos, cos], 1), (1, P // head))
    sin = np.tile(np.concatenate([-sin, sin], 1), (1, P // head))
    t = np.stack([cos, sin]).astype(np.float32)
    return np.ascontiguousarray(t.reshape(2, TPS, P, P).transpose(2, 0, 1, 3))


def kernel(**inputs):
    import concourse.bacc as bacc
    from concourse.bass_utils import run_bass_kernel_spmd

    a = {k: np.asarray(v) for k, v in inputs.items()}
    A, B, M = "L0_attn_a_", "L0_attn_b_", "L0_ffn_"

    def column(v):
        return v.reshape(-1, P).T

    def rows(v):
        return np.broadcast_to(v[None, :], (P, v.size))

    w_in = a[A + "W_in"]
    partner = np.arange(P) ^ 4
    wz = a[A + "W_zxbcdt"].T
    cw = a[A + "conv_w"].reshape(CONV_BLOCKS, P, TAPS).transpose(1, 0, 2).reshape(P, -1)
    cols = np.concatenate([
        column(a[A + "norm_pre_w"]), column(a[A + "norm_gated_w"]), column(a[A + "conv_b"]), cw,
        *[column(a[B + n]) for n in ("ln1_w", "ln1_b", "ln2_w", "ln2_b", "time_decay", "time_first",
                                     "tmk", "tmv", "tmr", "cmk", "cmr")],
        *[rows(a[A + n]) for n in ("dt_bias", "A_log", "D_param")],
        rows(a[B + "ln0_w"]), rows(a[B + "ln0_b"])], axis=1)
    def branch(gate, up, down):
        return np.concatenate([gate, up, down.reshape(FBLK, P, P).transpose(1, 0, 2).reshape(P, FFN)], 1)

    moe = [branch(a[M + "ws_gate"], a[M + "ws_up"], a[M + "ws_down"])]
    moe += [branch(a[M + "w_gate"][e], a[M + "w_up"][e], a[M + "w_down"][e]) for e in range(EXPERTS)]
    arrays = {
        "x": a[A + "x"],
        "wq": np.concatenate([w_in[:P].T, w_in[partner].T], 1),
        "wzx": np.concatenate([wz[:, :INNER], wz[:, -HEADS:], wz[:, INNER:INNER + CONV_BLOCKS * P]], 1),
        "rope": rope_tables(),
        "cols": cols,
        "w_out": a[A + "W_out"].T.reshape(2, P, P).transpose(1, 0, 2),
        "router_w": a[M + "gate_w"],
        "moe": np.stack(moe),
        "w_rkvo": np.stack([a[B + n].T for n in ("Wk", "Wv", "Wr", "Wo")], 1),
        "w_fk": a[B + "Wfk"].T,
        "w_fr": a[B + "Wfr"].T,
        "w_fv": a[B + "Wfv"].T.reshape(HIDDEN // P, P, P).transpose(1, 0, 2),
    }
    arrays = {k: np.ascontiguousarray(v) for k, v in arrays.items()}
    nc = bacc.Bacc("TRN2", target_bir_lowering=False, num_devices=1)
    io = {k: nc.dram_tensor("in_" + k, v.shape, F32, kind="ExternalInput").ap() for k, v in arrays.items()}
    io["out"] = nc.dram_tensor("out", (SEQS, SEQ, P), F32, kind="ExternalOutput").ap()
    program(nc, io)
    r = run_bass_kernel_spmd(nc, [{"in_" + k: v for k, v in arrays.items()}], core_ids=[0])
    return r.results[0]["out"]
```
